# Optimizing a Trainium2 kernel written in Bass

```python
import numpy as np
import jax
import jax.numpy as jnp

def _softmax(x, axis=-1):
    return jax.nn.softmax(x, axis=axis)

def _gelu(x):
    return jax.nn.gelu(x, approximate=True)

def _silu(x):
    return jax.nn.silu(x)

def _sigmoid(x):
    return jax.nn.sigmoid(x)

def _layernorm(x, axis=-1, eps=1e-05):
    m = jnp.mean(x, axis=axis, keepdims=True)
    v = jnp.var(x, axis=axis, keepdims=True)
    return (x - m) / jnp.sqrt(v + eps)

def _scatter_add(tgt, idx, src, axis=0):
    return tgt.at[idx].add(src)

def _segment_sum(src, seg, n):
    return jax.ops.segment_sum(src, seg, n)
kernel_name = 'mk_perceiver_d1_seqx_r4_e25317'

def setup_inputs(seed: int=0):
    np.random.seed(seed)
    _w = jnp.asarray

    def _rec_inputs():
        import jax
        import jax.numpy as jnp
        _rk = jax.random.key(seed)
        x = -0.0002928 + 1 * jax.random.normal(jax.random.fold_in(_rk, 1), (64, 64, 256), jnp.float32)
        _lenS = 64 - jax.random.randint(jax.random.fold_in(_rk, 7), (64,), 0, max(1, 64 // 4) + 1, jnp.int32)
        _lenS2 = 256 - jax.random.randint(jax.random.fold_in(_rk, 8), (64,), 0, max(1, 256 // 4) + 1, jnp.int32)
        _ctx_1024P = jax.random.normal(jax.random.fold_in(_rk, 11), (64, 16, 256), jnp.float32)
        _ctx_1024c = jax.random.dirichlet(jax.random.fold_in(_rk, 511), 0.3 * jnp.ones((16,), jnp.float32), (64, 256))
        _ctx_1024t = jnp.einsum('bsk,bkd->bsd', _ctx_1024c, _ctx_1024P)
        _ctx_1024t = _ctx_1024t * jax.lax.rsqrt(jnp.mean(jnp.square(_ctx_1024t)) + 1e-12) * 0.953939
        ctx_1024 = -1.39393e-06 + 0.999914 * (_ctx_1024t + 0.3 * jax.random.normal(jax.random.fold_in(_rk, 611), (64, 256, 256), jnp.float32))
        _validS = jnp.arange(64)[None, :] < _lenS[:, None]
        _validS2 = jnp.arange(256)[None, :] < _lenS2[:, None]
        _causal = jnp.tril(jnp.ones((64, 64), dtype=bool))
        mask_BxS2_bf0 = jnp.logical_not(jnp.ones((64, 256), dtype=bool))
        return (x, ctx_1024, mask_BxS2_bf0)
    x, ctx_1024, mask_BxS2_bf0 = _rec_inputs()

    def _L0_xattn_setup():
        import jax, jax.numpy as jnp
        import numpy as np
        B, N, D = (2, 512, 256)
        H = 16
        HC = D // H
        ROPE_BASE = 10000.0

        def _rope(x):
            c = x.shape[-1]
            n = x.shape[-2]
            inv_freq = 1.0 / ROPE_BASE ** (jnp.arange(0, c, 2, dtype=jnp.float32) / c)
            t = jnp.arange(n, dtype=jnp.float32)[:, None] * inv_freq[None, :]
            cos = jnp.repeat(jnp.cos(t), 2, axis=-1).astype(x.dtype)
            sin = jnp.repeat(jnp.sin(t), 2, axis=-1).astype(x.dtype)
            x1 = x[..., ::2]
            x2 = x[..., 1::2]
            x_rot = jnp.stack([-x2, x1], axis=-1).reshape(x.shape)
            return x * cos + x_rot * sin
        key = jax.random.key(seed)
        ks = jax.random.split(key, 10)
        s_in = 1.0 / np.sqrt(D)
        return {'x_q': jax.random.normal(ks[0], (B, N, D), jnp.float32), 'x_kv': jax.random.normal(ks[1], (B, N, D), jnp.float32), 'pad_mask': jnp.zeros((B, N), dtype=bool), 'Wq': jax.random.normal(ks[2], (D, D), jnp.float32) * s_in, 'bq': jnp.zeros((D,), jnp.float32), 'Wk': jax.random.normal(ks[3], (D, D), jnp.float32) * s_in, 'bk': jnp.zeros((D,), jnp.float32), 'Wv': jax.random.normal(ks[4], (D, D), jnp.float32) * s_in, 'bv': jnp.zeros((D,), jnp.float32), 'Wo': jax.random.normal(ks[5], (D, D), jnp.float32) * s_in, 'bo': jnp.zeros((D,), jnp.float32)}
    _L0_xattn_all = _L0_xattn_setup()
    _L0_xattn_in = {k: v for k, v in _L0_xattn_all.items() if k in ('Wq', 'bq', 'Wk', 'bk', 'Wv', 'bv', 'Wo', 'bo')}
    del _L0_xattn_all

    def _L0_attn_setup():
        import jax, jax.numpy as jnp
        from jax import lax
        import numpy as np
        D = 256
        H = 16
        DK = D // 2 // H
        DV = D // H
        GATE_NORM = 16.0
        SCALE = DK ** (-0.5)
        EPS = 1e-05

        def _split_heads(x, dh):
            B, L, _ = x.shape
            return x.reshape(B, L, H, dh).transpose(0, 2, 1, 3)

        def _gla_scan(q, k, v, log_gate):
            B = q.shape[0]
            qt = jnp.moveaxis(q, 2, 0)
            kt = jnp.moveaxis(k, 2, 0)
            vt = jnp.moveaxis(v, 2, 0)
            gt = jnp.exp(jnp.moveaxis(log_gate, 2, 0))

            def step(state, inp):
                qq, kk, vv, gg = inp
                state = state * gg[..., None] + kk[..., :, None] * vv[..., None, :]
                out = jnp.einsum('bhd,bhde->bhe', qq, state)
                return (state, out)
            init = jnp.zeros((B, H, DK, DV), dtype=q.dtype)
            _, outs = lax.scan(step, init, (qt, kt, vt, gt))
            return jnp.moveaxis(outs, 0, 2)
        key = jax.random.key(seed)
        ks = jax.random.split(key, 10)
        s = 0.02
        return {'inputs': jax.random.normal(ks[0], (4, 1024, D), dtype=jnp.float32), 'Wq': jax.random.normal(ks[1], (D, D // 2), dtype=jnp.float32) * s, 'Wk': jax.random.normal(ks[2], (D, D // 2), dtype=jnp.float32) * s, 'Wg1': jax.random.normal(ks[3], (D, 16), dtype=jnp.float32) * s, 'Wg2': jax.random.normal(ks[4], (16, D // 2), dtype=jnp.float32) * s, 'Wv': jax.random.normal(ks[5], (D, D), dtype=jnp.float32) * s, 'Wg': jax.random.normal(ks[6], (D, D), dtype=jnp.float32) * s, 'bg': jax.random.normal(ks[7], (D,), dtype=jnp.float32) * s, 'Wo': jax.random.normal(ks[8], (D, D), dtype=jnp.float32) * s}
    _L0_attn_all = _L0_attn_setup()
    _L0_attn_in = {k: v for k, v in _L0_attn_all.items() if k in ('Wq', 'Wk', 'Wg1', 'Wg2', 'Wv', 'Wg', 'bg', 'Wo')}
    del _L0_attn_all

    def _L0_ffn_setup():
        import jax, jax.numpy as jnp
        import numpy as np
        DIM = 256
        HID = 704
        N_ROUTED = 7
        TOPK = 2
        B, S = (4, 512)

        def _expert(x, wg, wu, wd):
            return jax.nn.silu(x @ wg) * (x @ wu) @ wd
        key = jax.random.key(seed)
        ks = jax.random.split(key, 9)
        s = 0.02
        x = jax.random.normal(ks[0], (B, S, DIM), jnp.float32)
        shared_gate = jax.random.normal(ks[1], (DIM, HID), jnp.float32) * s
        shared_up = jax.random.normal(ks[2], (DIM, HID), jnp.float32) * s
        shared_down = jax.random.normal(ks[3], (HID, DIM), jnp.float32) * s
        routed_gate = jax.random.normal(ks[4], (N_ROUTED, DIM, HID), jnp.float32) * s
        routed_up = jax.random.normal(ks[5], (N_ROUTED, DIM, HID), jnp.float32) * s
        routed_down = jax.random.normal(ks[6], (N_ROUTED, HID, DIM), jnp.float32) * s
        Wr = jax.random.normal(ks[7], (DIM, N_ROUTED), jnp.float32) * s
        routing_bias = jax.random.normal(ks[8], (N_ROUTED,), jnp.float32)
        return dict(x=x, shared_gate=shared_gate, shared_up=shared_up, shared_down=shared_down, routed_gate=routed_gate, routed_up=routed_up, routed_down=routed_down, Wr=Wr, routing_bias=routing_bias)
    _L0_ffn_all = _L0_ffn_setup()
    _L0_ffn_in = {k: v for k, v in _L0_ffn_all.items() if k in ('shared_gate', 'shared_up', 'shared_down', 'routed_gate', 'routed_up', 'routed_down', 'Wr', 'routing_bias')}
    del _L0_ffn_all
    return {'x': x, 'ctx_1024': ctx_1024, 'mask_BxS2_bf0': mask_BxS2_bf0, 'L0_xattn_Wq': _L0_xattn_in['Wq'], 'L0_xattn_bq': _L0_xattn_in['bq'], 'L0_xattn_Wk': _L0_xattn_in['Wk'], 'L0_xattn_bk': _L0_xattn_in['bk'], 'L0_xattn_Wv': _L0_xattn_in['Wv'], 'L0_xattn_bv': _L0_xattn_in['bv'], 'L0_xattn_Wo': _L0_xattn_in['Wo'], 'L0_xattn_bo': _L0_xattn_in['bo'], 'L0_attn_Wq': _L0_attn_in['Wq'], 'L0_attn_Wk': _L0_attn_in['Wk'], 'L0_attn_Wg1': _L0_attn_in['Wg1'], 'L0_attn_Wg2': _L0_attn_in['Wg2'], 'L0_attn_Wv': _L0_attn_in['Wv'], 'L0_attn_Wg': _L0_attn_in['Wg'], 'L0_attn_bg': _L0_attn_in['bg'], 'L0_attn_Wo': _L0_attn_in['Wo'], 'L0_ffn_shared_gate': _L0_ffn_in['shared_gate'], 'L0_ffn_shared_up': _L0_ffn_in['shared_up'], 'L0_ffn_shared_down': _L0_ffn_in['shared_down'], 'L0_ffn_routed_gate': _L0_ffn_in['routed_gate'], 'L0_ffn_routed_up': _L0_ffn_in['routed_up'], 'L0_ffn_routed_down': _L0_ffn_in['routed_down'], 'L0_ffn_Wr': _L0_ffn_in['Wr'], 'L0_ffn_routing_bias': _L0_ffn_in['routing_bias']}

def reference(x, ctx_1024, mask_BxS2_bf0, L0_xattn_Wq, L0_xattn_bq, L0_xattn_Wk, L0_xattn_bk, L0_xattn_Wv, L0_xattn_bv, L0_xattn_Wo, L0_xattn_bo, L0_attn_Wq, L0_attn_Wk, L0_attn_Wg1, L0_attn_Wg2, L0_attn_Wv, L0_attn_Wg, L0_attn_bg, L0_attn_Wo, L0_ffn_shared_gate, L0_ffn_shared_up, L0_ffn_shared_down, L0_ffn_routed_gate, L0_ffn_routed_up, L0_ffn_routed_down, L0_ffn_Wr, L0_ffn_routing_bias):
    import jax
    import jax.numpy as jnp

    def _L0_xattn_ref(x_q, x_kv, pad_mask, Wq, bq, Wk, bk, Wv, bv, Wo, bo):
        import jax, jax.numpy as jnp
        import numpy as np
        B, N, D = (2, 512, 256)
        H = 16
        HC = D // H
        ROPE_BASE = 10000.0

        def _rope(x):
            c = x.shape[-1]
            n = x.shape[-2]
            inv_freq = 1.0 / ROPE_BASE ** (jnp.arange(0, c, 2, dtype=jnp.float32) / c)
            t = jnp.arange(n, dtype=jnp.float32)[:, None] * inv_freq[None, :]
            cos = jnp.repeat(jnp.cos(t), 2, axis=-1).astype(x.dtype)
            sin = jnp.repeat(jnp.sin(t), 2, axis=-1).astype(x.dtype)
            x1 = x[..., ::2]
            x2 = x[..., 1::2]
            x_rot = jnp.stack([-x2, x1], axis=-1).reshape(x.shape)
            return x * cos + x_rot * sin
        dp_scale = HC ** (-0.5)
        q = x_q @ Wq + bq
        k = x_kv @ Wk + bk
        v = x_kv @ Wv + bv

        def split_heads(x):
            b, n, _ = x.shape
            return x.reshape(b, n, H, -1).transpose(0, 2, 1, 3)
        q, k, v = (split_heads(q), split_heads(k), split_heads(v))
        q = q * dp_scale
        q = _rope(q)
        k = _rope(k)
        attn = jnp.einsum('bhic,bhjc->bhij', q, k)
        neg = -jnp.finfo(attn.dtype).max
        attn = jnp.where(pad_mask[:, None, None, :], neg, attn)
        i, j = (q.shape[2], k.shape[2])
        causal = jnp.triu(jnp.ones((i, j), dtype=bool), k=j - i + 1)
        attn = jnp.where(causal, neg, attn)
        attn = jax.nn.softmax(attn, axis=-1)
        o = jnp.einsum('bhij,bhjc->bhic', attn, v)
        b, h, n, c = o.shape
        o = o.transpose(0, 2, 1, 3).reshape(b, n, h * c)
        return o @ Wo + bo

    def _L0_attn_ref(inputs, Wq, Wk, Wg1, Wg2, Wv, Wg, bg, Wo):
        import jax, jax.numpy as jnp
        from jax import lax
        import numpy as np
        D = 256
        H = 16
        DK = D // 2 // H
        DV = D // H
        GATE_NORM = 16.0
        SCALE = DK ** (-0.5)
        EPS = 1e-05

        def _split_heads(x, dh):
            B, L, _ = x.shape
            return x.reshape(B, L, H, dh).transpose(0, 2, 1, 3)

        def _gla_scan(q, k, v, log_gate):
            B = q.shape[0]
            qt = jnp.moveaxis(q, 2, 0)
            kt = jnp.moveaxis(k, 2, 0)
            vt = jnp.moveaxis(v, 2, 0)
            gt = jnp.exp(jnp.moveaxis(log_gate, 2, 0))

            def step(state, inp):
                qq, kk, vv, gg = inp
                state = state * gg[..., None] + kk[..., :, None] * vv[..., None, :]
                out = jnp.einsum('bhd,bhde->bhe', qq, state)
                return (state, out)
            init = jnp.zeros((B, H, DK, DV), dtype=q.dtype)
            _, outs = lax.scan(step, init, (qt, kt, vt, gt))
            return jnp.moveaxis(outs, 0, 2)
        B, L, _ = inputs.shape
        q = _split_heads(inputs @ Wq, DK)
        k = _split_heads(inputs @ Wk * SCALE, DK)
        kg = _split_heads(inputs @ Wg1 @ Wg2, DK)
        v = _split_heads(inputs @ Wv, DV)
        gate = jax.nn.silu(inputs @ Wg + bg)
        log_gate = jax.nn.log_sigmoid(kg) / GATE_NORM
        o = _gla_scan(q, k, v, log_gate)
        mu = jnp.mean(o, axis=-1, keepdims=True)
        var = jnp.var(o, axis=-1, keepdims=True)
        o = (o - mu) * lax.rsqrt(var + EPS)
        o = o.transpose(0, 2, 1, 3).reshape(B, L, D)
        return gate * o @ Wo

    def _L0_ffn_ref(x, shared_gate, shared_up, shared_down, routed_gate, routed_up, routed_down, Wr, routing_bias):
        import jax, jax.numpy as jnp
        import numpy as np
        DIM = 256
        HID = 704
        N_ROUTED = 7
        TOPK = 2
        B, S = (4, 512)

        def _expert(x, wg, wu, wd):
            return jax.nn.silu(x @ wg) * (x @ wu) @ wd
        b, s, d = x.shape
        n_exp = routed_gate.shape[0]
        shared_out = _expert(x, shared_gate, shared_up, shared_down)
        logits = x @ Wr * routing_bias
        probs = jax.nn.sigmoid(logits)
        scores, idx = jax.lax.top_k(probs, TOPK)
        scores = scores / scores.sum(-1, keepdims=True)
        t = b * s
        xf = x.reshape(t, d)
        weights = jnp.zeros((t, n_exp), x.dtype).at[jnp.arange(t)[:, None], idx.reshape(t, TOPK)].add(scores.reshape(t, TOPK))
        combined = jnp.zeros_like(xf)
        for e in range(n_exp):
            combined = combined + _expert(xf, routed_gate[e], routed_up[e], routed_down[e]) * weights[:, e:e + 1]
        return shared_out + combined.reshape(b, s, d)
    x = x + _L0_xattn_ref(_layernorm(x, axis=-1), ctx_1024, mask_BxS2_bf0, L0_xattn_Wq, L0_xattn_bq, L0_xattn_Wk, L0_xattn_bk, L0_xattn_Wv, L0_xattn_bv, L0_xattn_Wo, L0_xattn_bo)
    x = x + _L0_attn_ref(_layernorm(x, axis=-1), L0_attn_Wq, L0_attn_Wk, L0_attn_Wg1, L0_attn_Wg2, L0_attn_Wv, L0_attn_Wg, L0_attn_bg, L0_attn_Wo)
    x = x + _L0_ffn_ref(_layernorm(x, axis=-1), L0_ffn_shared_gate, L0_ffn_shared_up, L0_ffn_shared_down, L0_ffn_routed_gate, L0_ffn_routed_up, L0_ffn_routed_down, L0_ffn_Wr, L0_ffn_routing_bias)
    return x

_drawn_inputs = setup_inputs


def setup_inputs(seed=0):
    import zlib

    import numpy as np

    out = dict(_drawn_inputs(seed))
    spreads = {'L0_xattn_bq': (0.0, 0.461),
     'L0_xattn_bk': (0.0, 0.8),
     'L0_xattn_bv': (0.0, 0.1),
     'L0_xattn_bo': (0.0, 0.1)}
    factors = {'L0_attn_Wg1': 8.0,
     'L0_attn_Wg2': 8.0,
     'L0_attn_bg': 8.0,
     'L0_ffn_routed_gate': 3.283,
     'L0_ffn_routed_up': 3.24,
     'L0_ffn_routed_down': 3.246,
     'L0_ffn_Wr': 3.974,
     'L0_ffn_routing_bias': 4.48,
     'L0_ffn_shared_gate': 2.875,
     'L0_ffn_shared_up': 2.843,
     'L0_ffn_shared_down': 2.844}
    for name, (base, spread) in spreads.items():
        noise = np.random.default_rng([zlib.crc32(name.encode()), seed]).standard_normal(out[name].shape)
        drawn = base * np.exp(spread * noise) if base else spread * noise
        out[name] = jnp.asarray(drawn.astype(out[name].dtype))
    for name, factor in factors.items():
        out[name] = (out[name] * factor).astype(out[name].dtype)
    return out
```

```python
from contextlib import ExitStack

import numpy as np
import concourse.bass as bass
from concourse import mybir

ALU = mybir.AluOpType
ACT = mybir.ActivationFunctionType
AX = mybir.AxisListType
F32 = mybir.dt.float32
BF16 = mybir.dt.bfloat16
F16 = mybir.dt.float16
I32 = mybir.dt.int32
U32 = mybir.dt.uint32
U8 = mybir.dt.uint8

P = 128
D = 256
DK = D // P
NB, SQ, SK = 64, 64, 256
NPAIR = NB // 2
H, HC = 16, 16
GK, GV = 8, 16
NCH, CH = 4, 16
GATE_NORM = 16.0
EPS = 1e-5
HID = 704
HT = (HID + P - 1) // P
HR = HID - (HT - 1) * P
HH = HID // 2
NE, TOPK = 7, 2
NTILE = NB * SQ // P
NSLOT = (NB * SQ * TOPK + NE * (P - 1)) // P
NT = NTILE + NSLOT
EW_UP, EW_DOWN = DK * 2 * HID, HT * D
EW = EW_UP + EW_DOWN
EARLY = 2
W_SCALE = 2.0 ** 6
V_SCALE = 2.0 ** 4
A_SCALE = 2.0 ** 6
NEG = -(2.0 ** 127)

CONST = {}
_at = 0
for _name, _n in (("ident", P), ("causal", SK), ("cosk", 32), ("sink", 32), ("cosq", HC), ("sinq", HC),
                  ("par", 2), ("head4", 4), ("gla", NCH * CH), ("upper", P), ("eps", 1), ("lnscale", 1),
                  ("one", 1), ("tile", NSLOT), ("desc", NE)):
    CONST[_name] = (_at, _at + _n)
    _at += _n
NCONST = _at


def constants():
    c = np.zeros((P, NCONST), np.float32)
    p = np.arange(P)

    def put(name, a):
        lo, hi = CONST[name]
        c[:, lo:hi] = np.broadcast_to(np.asarray(a, np.float32).reshape(-1, hi - lo), (P, hi - lo))

    inv = (1.0 / 10000.0 ** (np.arange(0, HC, 2, dtype=np.float32) / np.float32(HC))).astype(np.float32)

    def rope(pos, scale):
        t = pos[..., None].astype(np.float32) * inv
        cos = np.repeat(np.cos(t), 2, axis=-1)
        sin = np.repeat(np.sin(t), 2, axis=-1)
        sin[..., ::2] *= -1.0
        return cos * scale, sin * scale

    ck, sk = rope(p[:, None] + P * np.arange(SK // P)[None, :], 1.0)
    cq, sq = rope(p % SQ, HC ** -0.5)
    put("ident", np.eye(P))
    put("causal", np.arange(SK)[None, :] <= (p % SQ)[:, None] + SK - SQ)
    put("cosk", ck.reshape(P, -1))
    put("sink", sk.reshape(P, -1))
    put("cosq", cq)
    put("sinq", sq)
    put("par", (p[:, None] // HC) % 2 == np.arange(2)[None, :])
    put("head4", (p[:, None] // GK) % 4 == np.arange(4)[None, :])
    put("gla", (np.arange(SQ)[None, :] >= (p % SQ)[:, None]) * (A_SCALE / W_SCALE ** 2))
    put("upper", p[:, None] < p[None, :])
    put("eps", np.full((P, 1), EPS))
    put("lnscale", np.full((P, 1), np.log(GK ** -0.5)))
    put("one", np.ones((P, 1)))
    put("tile", np.arange(NSLOT)[None, :])
    put("desc", np.arange(NE, 0, -1)[None, :])
    return c


def bc(ap, axis, n):
    v = ap.unsqueeze(axis)
    shape = list(v.shape)
    shape[axis] = n
    return v.to_broadcast(shape)


class Step:

    def __init__(self, i, off):
        self.i, self.off = i, off

    def n(self, per, add=0):
        return self.i * (2 * per) + (self.off * per + add)

    def next(self, k=1):
        return Step(self.i, self.off + k)

    @property
    def par(self):
        return self.off % 2

    @property
    def half(self):
        return self.i + self.off // 2


def wait(eng, sem, value):
    if isinstance(value, int) and value <= 0:
        return
    eng.wait_ge(sem, value)


def build(nc, x, ctx_in, pad, xWq, xbq, xWk, xbk, xWv, xbv, xWo, xbo, gWq, gWk, gWg1, gWg2, gWv, gWg, gbg, gWo,
          sgate, sup, sdown, rgate, rup, rdown, Wr, rbias, consts_in, out):
    with ExitStack() as stack:
        program(nc, stack, x, ctx_in, pad, xWq, xbq, xWk, xbk, xWv, xbv, xWo, xbo, gWq, gWk, gWg1, gWg2, gWv,
                gWg, gbg, gWo, sgate, sup, sdown, rgate, rup, rdown, Wr, rbias, consts_in, out)


def program(nc, stack, x, ctx_in, pad, xWq, xbq, xWk, xbk, xWv, xbv, xWo, xbo, gWq, gWk, gWg1, gWg2, gWv,
            gWg, gbg, gWo, sgate, sup, sdown, rgate, rup, rdown, Wr, rbias, consts_in, out):
    def sb(name, shape, dt=F32):
        return stack.enter_context(nc.sbuf_tensor(name, shape, dt))

    def sem(name):
        return stack.enter_context(nc.semaphore(name))

    rows_in = nc.dram_tensor("rows_in", [NT * P, D], F32, kind="Internal").ap()
    rows_out = nc.dram_tensor("rows_out", [NT * P, D], F32, kind="Internal").ap()

    experts = sb("experts", [P, 1 + NE, EW])
    x2_all = sb("x2_all", [P, NTILE, D])
    cst = sb("cst", [P, NCONST])
    logits = sb("logits", [P, NTILE, NE])
    work = sb("work", [P, 8900])

    arenas = [[experts[:, EARLY:, :].rearrange("p e n -> p (e n)"), 0, (1 + NE - EARLY) * EW],
              [work[:, :], 0, 8900]]

    def place(n, which=None):
        for k, a in enumerate(arenas):
            if (which is None or k == which) and a[1] + n <= a[2]:
                a[1] += n
                return a[0][:, a[1] - n:a[1]]
        raise ValueError("no room")

    def const(name):
        lo, hi = CONST[name]
        return cst[:, lo:hi]

    ident = const("ident")
    w_q = place(DK * D).rearrange("p (k n) -> p k n", k=DK)
    w_kv = place(DK * 2 * D).rearrange("p (k n) -> p k n", k=DK)
    w_o = place(2 * D).rearrange("p (a n) -> p a n", a=2)
    w_gqk = place(DK * D).rearrange("p (k n) -> p k n", k=DK)
    w_g1 = place(DK * 16).rearrange("p (k n) -> p k n", k=DK)

    def halves(k, n):
        return [place(k * n // 2).bitcast(F16).rearrange("p (k n) -> p k n", k=k) for _ in range(2)]

    w_gqk_s, w_g1_s, w_gvg_s = halves(DK, D), halves(DK, 16), halves(DK, 2 * D)
    w_g2 = place(P)
    w_gvg = place(DK * 2 * D).rearrange("p (k n) -> p k n", k=DK)
    w_go = place(DK * D).rearrange("p (k n) -> p k n", k=DK)
    w_r = place(DK * NE).rearrange("p (k n) -> p k n", k=DK)
    b_kv = place(2 * D)
    b_q = place(D)
    b_o = place(D)
    b_g = place(D)
    ident_bf = place(P // 2).bitcast(BF16)
    x_in = [place(D) for _ in range(2)]
    x_res = place(D)
    pad_in = [place(2 * SK // 4).bitcast(U8).rearrange("p (b j) -> p b j", b=2) for _ in range(2)]
    keep = place(2 * SK).rearrange("p (b j) -> p b j", b=2)
    seen = place(2 * SK).rearrange("p (b j) -> p b j", b=2)
    masks = [place(2 * SK // 2).bitcast(BF16).rearrange("p (b j) -> p b j", b=2) for _ in range(2)]
    ctx_rows = place(4 * D).rearrange("p (t n) -> p t n", t=4)
    ctx_t = place(DK * 4 * P).rearrange("p (k n) -> p k n", k=DK)
    kv = place(4 * 2 * D).rearrange("p (t n) -> p t n", t=4)
    k_rot = place(4 * D).rearrange("p (t n) -> p t n", t=4)
    k_swap = place(4 * D).rearrange("p (t n) -> p t n", t=4)
    k_t = place(2 * 2 * SK).rearrange("p (g b j) -> p g b j", g=2, b=2)
    xn = place(D)
    xn_t = place(DK * P).rearrange("p (k n) -> p k n", k=DK)
    q_nat = place(D)
    q_rot = place(D)
    q_swap = place(D)
    q_t = place(2 * 2 * 2 * SQ).rearrange("p (g b a i) -> p g b a i", g=2, b=2, a=2)
    probs = [place(8 * SK).rearrange("p (s j) -> p s j", s=8) for _ in range(2)]
    probs_s = halves(4, 4 * P)
    v_s = [halves(4, D) for _ in range(2)]
    heads_out = [place(8 * HC).rearrange("p (h c) -> p h c", h=8) for _ in range(2)]
    heads_t = place(2 * 2 * SQ).rearrange("p (a b i) -> p a b i", a=2, b=2)
    neg_max = [place(8) for _ in range(2)]
    row_sum = [place(8) for _ in range(2)]
    row_inv = place(8)
    x1 = place(D)
    x1n = place(D)
    x1n_s = halves(DK, P)
    g_v_s = halves(1, D)
    gate = place(D)
    gate_e = place(D)
    gate_i = place(D)
    low_t = place(P)
    kg_abs = place(P)
    kg_min = place(P)
    kg_exp = place(P)
    kg_ln = place(P)
    log_gate = place(P)
    cum = place(2 * SQ).rearrange("p (b i) -> p b i", b=2)
    ref = place(2 * NCH).rearrange("p (b c) -> p b c", b=2)
    q_dec = place(2 * SQ)
    k_dec = place(NCH * 2 * SQ).rearrange("p (c b i) -> p c b i", c=NCH, b=2)
    qs_t = place(2 * SQ)
    q_heads = place(2 * NCH * 4 * CH).rearrange("p (b c h t) -> p b c h t", b=2, c=NCH, h=4)
    k_heads = place(NCH * 2 * SQ).rearrange("p (c b i) -> p c b i", c=NCH, b=2)
    a_t = w_gvg.rearrange("p k n -> p (k n)").rearrange("p (r h c t) -> p r h c t", r=4, h=4, c=NCH)
    a_s = [h.rearrange("p r (h c t) -> p r h c t", h=4, c=NCH) for h in halves(4, 4 * NCH * CH)]
    g_out = place(D)
    g_sq = place(D)
    g_norm = place(D)
    g_norm_t = place(DK * P).rearrange("p (k n) -> p k n", k=DK)
    g_stat = place(4 * H).rearrange("p (k h) -> p k h", k=4)
    x2n = [place(D) for _ in range(2)]
    x2n_t = place(DK * P).rearrange("p (k n) -> p k n", k=DK)
    stats = [place(10) for _ in range(3)]

    warena = [0]

    def place2(n):
        warena[0] += n
        assert warena[0] <= 8900
        return work[:, warena[0] - n:warena[0]]

    e_rows = [place2(D) for _ in range(2)]
    e_rows_t = [place2(DK * P).rearrange("p (k n) -> p k n", k=DK) for _ in range(2)]
    e_silu = place2(HID)
    e_hid = place2(HT * P)
    e_hid_t = place2(HT * P).rearrange("p (c n) -> p c n", c=HT)
    e_y = [place2(D) for _ in range(2)]
    stage_rows = [place2(D) for _ in range(2)]
    got = [[place2(D) for _ in range(3)] for _ in range(2)]
    w_tok = place2(TOPK * NTILE).rearrange("p (c t) -> p c t", c=TOPK)
    slot_i = place2(TOPK * NTILE).bitcast(U32).rearrange("p (c t) -> p c t", c=TOPK)
    tile_e = place2(NT).bitcast(I32)
    rt = [0]

    def place3(n):
        rt[0] += n
        assert rt[0] <= EW
        return experts[:, NE, rt[0] - n:rt[0]]

    L = NTILE * NE
    te = lambda a: a.rearrange("p (t e) -> p t e", e=NE)
    et = lambda a: a.rearrange("p (e t) -> p e t", e=NE)
    r_z, r_e, r_p, r_c, r_eq = (te(place3(L)) for _ in range(5))
    r_oh = [te(place3(L)) for _ in range(TOPK)]
    r_sel = te(place3(L))
    r_in, r_tot = te(place3(L)), te(place3(L))
    r_cum, r_pos = te(place3(L)), te(place3(L))
    r_m = place3(6 * NTILE).rearrange("p (k t) -> p k t", k=6)
    r_n = place3(6 * NE).rearrange("p (k e) -> p k e", k=6)
    r_ni = place3(NE).bitcast(I32)
    r_t = place3(NSLOT * NE).rearrange("p (j e) -> p j e", e=NE)
    r_tf = place3(NSLOT)
    r_bias = place3(NE)
    r_ones = place3(P)

    ps = stack.enter_context(nc.psum_tensor("ps", [P, 8, 512], F32))
    bank_ta, bank_tb, bank_ma, bank_mb = (ps[:, k, :] for k in range(4, 8))

    def probs_bank(b, r):
        return ((bank_ma, bank_mb), (bank_ta, bank_tb))[b][r % 2]

    S = {}
    for name in """
        consts_loaded weights_loaded waits_met ident_bf_ready fill_ready slots_filled biasr_loaded
        ctx_loaded ctx_turned ctx_t_ready kv_done kv_ready k_prod_ready k_swap_ready k_rot_ready k_turned k_t_ready
        x_stat_ready x_log_ready x_rstd_ready xn_ready xn_turned xn_t_ready q_done q_nat_ready q_prod_ready q_swap_ready
        q_rot_ready q_turned q_t_ready pad_read seen_ready masks_ready x_res_ready x_bn
        scores_done max_ready exp_done probs_turned probs_hi_ready probs_lo_ready v_hi_ready v_lo_ready gla_hi_ready gla_lo_ready a_hi_ready a_lo_ready g_v_hi_ready av_done inv_ready av_ready heads_turned
        heads_t_ready proj_done x1_ready x1_bn x1_stat_ready x1_log_ready x1_rstd_ready x1n_ready x1n_turned x1n_hi_ready x1n_lo_ready
        vg_done g_v_ready gate_ready qkl_done low_t_ready kg_done kg_abs_ready kg_min_ready gate_exp_ready gate_one
        gate_inv gate_silu kg_exp_ready kg_ln_ready log_gate_ready cum_ready ref_zero ref_ready dec_ready dec_k_ready dec_min dec_exp_q
        dec_exp_k qs_ready q_heads_ready k_heads_ready a_done a_ready go_done go_ready gs_sum gs_mean gs_cent gs_sq
        gs_var gs_log gs_rstd gn_scaled gn_ready gn_turned gn_t_ready gproj_done x2_ready x2_bn x2_stat_ready
        x2_log_ready x2_rstd_ready x2n_ready x2n_turned x2n_t_ready logits_done logits_ready
        early_experts late_experts route_step route_exp route_mm table_ready staged_scattered
        rows_turned rows_t_ready up_done silu_ready hid_ready hid_turned hid_t_lo hid_t_hi down_done y_ready tail_zero
        sum_ready last_store
    """.split():
        S[name] = sem(name)
    x_loaded = [sem(f"x_loaded{k}") for k in range(2)]
    pad_loaded = [sem(f"pad_loaded{k}") for k in range(2)]
    x2n_stored = [sem(f"x2n_stored{k}") for k in range(2)]
    staged = [sem(f"staged{k}") for k in range(2)]
    scattered = [sem(f"scattered{k}") for k in range(2)]
    rows_loaded = [sem(f"rows_loaded{k}") for k in range(2)]
    y_stored = [sem(f"y_stored{k}") for k in range(2)]
    got_rows = [[sem(f"got_rows{k}{c}") for c in range(3)] for k in range(2)]
    sum_stored = [sem(f"sum_stored{k}") for k in range(2)]

    pairs = x.rearrange("(q b) s d -> q (b s) d", b=2)
    ctx_pairs = ctx_in.rearrange("(q b) (t p) d -> q p (b t) d", b=2, p=P)
    pad_pairs = pad.rearrange("(q b) j -> q (b j)", b=2)
    out_tiles = out.rearrange("(q b) s d -> q (b s) d", b=2)
    in_tiles = rows_in.rearrange("(t p) d -> t p d", p=P)
    res_tiles = rows_out.rearrange("(t p) d -> t p d", p=P)

    def over_pairs(eng, first, body, last):
        first(Step(0, 0))
        body(Step(0, 1))
        body(Step(0, 2))
        with eng.Fori(1, (NPAIR - 2) // 2) as i:
            body(Step(i, 1))
            body(Step(i, 2))
        last(Step(0, NPAIR - 1))

    block = stack.enter_context(nc.Block())

    def apart(eng):
        eng.sem_inc(S["waits_met"], 1)

    @block.sync
    def _(sp):
        sp.dma_start(cst[:, :], consts_in).then_inc(S["consts_loaded"], 16)

        def load_x(j):
            wait(sp, S["x_res_ready"], j.n(1, -1))
            wait(sp, S["xn_ready"], j.n(1, -1))
            apart(sp)
            sp.dma_start(x_in[j.par], pairs[j.n(1)]).then_inc(x_loaded[j.par], 16)
            wait(sp, S["pad_read"], j.n(1, -1))
            apart(sp)
            sp.dma_start(pad_in[j.par].rearrange("p b j -> p (b j)"),
                         pad_pairs[j.n(1)].partition_broadcast(P)).then_inc(pad_loaded[j.par], 16)

        def load_ctx(j):
            wait(sp, S["ctx_turned"], j.n(2))
            apart(sp)
            sp.dma_start(ctx_rows, ctx_pairs[j.n(1)]).then_inc(S["ctx_loaded"], 16)

        def store_x2n(g):
            wait(sp, S["x2n_ready"], g.n(1, 1))
            apart(sp)
            sp.dma_start(in_tiles[g.n(1)], x2n[g.par]).then_inc(x2n_stored[g.par], 16)

        load_ctx(Step(0, 0))
        load_x(Step(0, 0))
        load_x(Step(0, 1))
        wl = S["weights_loaded"]

        def kmaj(w):
            return w.rearrange("(k p) n -> p k n", p=P)

        count = [0]

        def wload(dst, src):
            sp.dma_start(dst, src).then_inc(wl, 16)
            count[0] += 1

        wload(w_kv[:, :, 0:D], kmaj(xWk))
        wload(w_kv[:, :, D:2 * D], kmaj(xWv))
        wload(w_q, kmaj(xWq))
        for hp in range(8):
            for a in range(2):
                row = (2 * hp + a) * HC
                wload(w_o[hp * HC:(hp + 1) * HC, a, :], xWo[row:row + HC, :])
        wload(w_gqk[:, :, 0:P], kmaj(gWq))
        wload(w_gqk[:, :, P:2 * P], kmaj(gWk))
        wload(w_g1, kmaj(gWg1))
        wload(w_g2[0:16, :], gWg2)
        wload(w_gvg[:, :, 0:D], kmaj(gWv))
        wload(w_gvg[:, :, D:2 * D], kmaj(gWg))
        wload(w_go, kmaj(gWo))
        wload(w_r, kmaj(Wr))
        wload(b_kv[:, 0:D], xbk.partition_broadcast(P))
        wload(b_kv[:, D:2 * D], xbv.partition_broadcast(P))
        wload(b_q, xbq.partition_broadcast(P))
        wload(b_o, xbo.partition_broadcast(P))
        wload(b_g, gbg.partition_broadcast(P))
        assert count[0] == WEIGHT_DMAS
        load_ctx(Step(0, 1))

        def step(p, nxt2=True):
            if nxt2:
                load_x(p.next(2))
                load_ctx(p.next(2))
            store_x2n(p.next(-1))

        def first(p):
            load_x(p.next(2))
            load_ctx(p.next(2))

        first(Step(0, 0))
        step(Step(0, 1))
        step(Step(0, 2))
        with sp.Fori(1, (NPAIR - 4) // 2) as i:
            step(Step(i, 1))
            step(Step(i, 2))
        step(Step(0, NPAIR - 3))
        step(Step(0, NPAIR - 2), False)
        step(Step(0, NPAIR - 1), False)
        store_x2n(Step(0, NPAIR - 1))

        sp.wait_ge(x2n_stored[0], 16 * NPAIR // 2)
        sp.wait_ge(x2n_stored[1], 16 * NPAIR // 2)
        sp.wait_ge(S["logits_ready"], NPAIR)

        def load_rows(t, k):
            wait(sp, S["rows_turned"], t - 1)
            apart(sp)
            sp.dma_start(e_rows[k], in_tiles[t]).then_inc(rows_loaded[k], 16)

        def stage(t):
            if t >= 2:
                sp.wait_ge(scattered[t % 2], 32 * (t // 2))
            sp.dma_start(stage_rows[t % 2], in_tiles[t]).then_inc(staged[t % 2], 16)

        def store_y(t, k):
            wait(sp, S["y_ready"], t + 1)
            apart(sp)
            sp.dma_start(res_tiles[t], e_y[k]).then_inc(y_stored[k], 16)

        sp.dma_start(r_bias, rbias.partition_broadcast(P)).then_inc(S["biasr_loaded"], 16)
        load_rows(0, 0)
        load_rows(1, 1)
        for t in range(2, NTILE):
            stage(t - 2)
            load_rows(t, t % 2)
            if t >= 4:
                store_y(t - 4, t % 2)
        stage(NTILE - 2)
        stage(NTILE - 1)
        for k in range(2):
            sp.wait_ge(scattered[k], 32 * (NTILE // 2))
        with sp.Fori(NTILE // 2, NT // 2) as i:
            for k in range(2):
                load_rows(i * 2 + k, k)
                store_y(i * 2 + k - 4, k)

        for t in range(NT - 4, NT):
            store_y(t, t % 2)
        def store_sum(t):
            sp.wait_ge(S["sum_ready"], t + 1)
            sp.dma_start(out_tiles[t], x2_all[:, t, :]).then_inc(sum_stored[t % 2], 16)

        sp.wait_ge(y_stored[0], 16 * NT // 2)
        sp.wait_ge(y_stored[1], 16 * NT // 2)
        for t in range(NTILE):
            if t >= 2:
                store_sum(t - 2)
            sp.dma_start(got[t % 2][2], res_tiles[t]).then_inc(got_rows[t % 2][2], 16)
        store_sum(NTILE - 2)
        store_sum(NTILE - 1)
        sp.wait_ge(sum_stored[0], 16 * NTILE // 2)
        sp.wait_ge(sum_stored[1], 16 * NTILE // 2)

    @block.gpsimd
    def _(pool):
        zeros = experts[:, 1, 0:8 * D].rearrange("p (t d) -> p t d", t=8)
        nc.gpsimd.memset(zeros, 0.0).then_inc(S["fill_ready"], 1)
        pool.wait_ge(S["consts_loaded"], 16)
        nc.gpsimd.tensor_copy(ident_bf, ident).then_inc(S["ident_bf_ready"], 1)
        pool.wait_ge(S["fill_ready"], 1)

        def fill_slots():
            for t in range(NTILE, NT, 8):
                m = min(8, NT - t)
                pool.dma_start(in_tiles[t:t + m].rearrange("t p d -> p t d"), zeros[:, 0:m, :])\
                    .then_inc(S["slots_filled"], 16)

        def load_expert(e, s):
            w = experts[:, e, :]
            up = w[:, 0:EW_UP].rearrange("p (k c n) -> p k c n", k=DK, c=2)
            down = w[:, EW_UP:].rearrange("p (c n) -> p c n", c=HT)
            g, u, d = (sgate, sup, sdown) if e == 0 else (rgate[e - 1], rup[e - 1], rdown[e - 1])
            pool.dma_start(up[:, :, 0, :], g.rearrange("(k p) n -> p k n", p=P)).then_inc(s, 16)
            pool.dma_start(up[:, :, 1, :], u.rearrange("(k p) n -> p k n", p=P)).then_inc(s, 16)
            pool.dma_start(down[:, 0:HT - 1, :], d[0:(HT - 1) * P, :].rearrange("(c p) n -> p c n", p=P))\
                .then_inc(s, 16)
            pool.dma_start(down[0:HR, HT - 1, :], d[(HT - 1) * P:, :]).then_inc(s, 16)

        def masks_of(j):
            wait(pool, pad_loaded[j.par], j.half * 16 + 16)
            wait(pool, S["scores_done"], j.n(2, -2))
            wait(pool, S["masks_ready"], j.n(1))
            apart(pool)
            nc.gpsimd.tensor_scalar(keep, pad_in[j.par], -1.0, 1.0, ALU.mult, ALU.add).then_inc(S["pad_read"], 1)
            wait(pool, S["pad_read"], j.n(1, 1))
            nc.gpsimd.tensor_tensor(seen, keep, bc(const("causal"), 1, 2), ALU.mult).then_inc(S["seen_ready"], 1)
            wait(pool, S["seen_ready"], j.n(1, 1))
            apart(pool)
            nc.gpsimd.tensor_scalar(masks[j.par], seen, -NEG, NEG, ALU.mult, ALU.add).then_inc(S["masks_ready"], 1)

        def rope_k(j):
            kb = kv
            wait(pool, S["kv_ready"], j.n(4, 4))
            wait(pool, S["k_rot_ready"], j.n(1))
            sin = const("sink").rearrange("p (t i e) -> p t i e", t=2, e=2)
            for b in range(2):
                for e in range(2):
                    for t in range(2):
                        src = kb[:, 2 * b + t, 0:D].rearrange("p (h i e) -> p h i e", h=H, e=2)
                        dst = k_swap[:, 2 * b + t, :].rearrange("p (h i e) -> p h i e", h=H, e=2)
                        ins = nc.gpsimd.tensor_tensor(dst[:, :, :, e], src[:, :, :, 1 - e],
                                                      bc(sin[:, t, :, e], 1, H), ALU.mult)
            ins.then_inc(S["k_swap_ready"], 1)

        def split_v(j):
            wait(pool, S["av_done"], j.n(2, -2))
            high, low = v_s[j.par]
            values = kv[:, :, D:2 * D]
            apart(pool)
            nc.gpsimd.tensor_scalar(high, values, 1.0, None, ALU.mult).then_inc(S["v_hi_ready"], 1)
            wait(pool, S["v_hi_ready"], j.n(1, 1))
            nc.gpsimd.tensor_tensor(low, values, high, ALU.subtract).then_inc(S["v_lo_ready"], 1)

        def split_a(g):
            wait(pool, S["a_ready"], g.n(4, 4))
            apart(pool)
            nc.gpsimd.tensor_scalar(a_s[0], a_t, 1.0, None, ALU.mult).then_inc(S["a_hi_ready"], 1)
            wait(pool, S["a_hi_ready"], g.n(1, 1))
            nc.gpsimd.tensor_tensor(a_s[1], a_t, a_s[0], ALU.subtract).then_inc(S["a_lo_ready"], 1)

        def rope_q(j):
            wait(pool, S["q_nat_ready"], j.n(1, 1))
            sin = const("sinq").rearrange("p (i e) -> p i e", e=2)
            src = q_nat.rearrange("p (h i e) -> p h i e", h=H, e=2)
            dst = q_swap.rearrange("p (h i e) -> p h i e", h=H, e=2)
            for e in range(2):
                ins = nc.gpsimd.tensor_tensor(dst[:, :, :, e], src[:, :, :, 1 - e], bc(sin[:, :, e], 1, H), ALU.mult)
            ins.then_inc(S["q_swap_ready"], 1)

        def residual(p):
            wait(pool, x_loaded[p.par], p.half * 16 + 16)
            wait(pool, S["x1_ready"], p.n(1))
            nc.gpsimd.tensor_tensor(x_res, x_in[p.par], b_o, ALU.add).then_inc(S["x_res_ready"], 1)

        def step(p, nxt=True, gla=True):
            residual(p)
            if nxt:
                masks_of(p.next())
                rope_k(p.next())
            if gla:
                split_a(p.next(-1))
            if nxt:
                split_v(p.next())
                rope_q(p.next())

        pool.wait_ge(S["weights_loaded"], 16 * WEIGHT_DMAS)
        masks_of(Step(0, 0))
        rope_k(Step(0, 0))
        split_v(Step(0, 0))
        rope_q(Step(0, 0))

        def first(p):
            step(p, gla=False)
            load_expert(0, S["early_experts"])
            fill_slots()

        over_pairs(pool, first, step, lambda p: step(p, False))
        split_a(Step(0, NPAIR - 1))

        pool.wait_ge(S["logits_ready"], NPAIR)
        for k in range(2):
            pool.wait_ge(x2n_stored[k], 16 * NPAIR // 2)
        pool.wait_ge(S["slots_filled"], 16 * N_FILL)
        for e in range(1, NE):
            load_expert(e, S["late_experts"])
        pool.wait_ge(S["table_ready"], 1)
        load_expert(NE, S["late_experts"])
        for t in range(NTILE):
            pool.wait_ge(staged[t % 2], 16 * (t // 2 + 1))
            for c in range(TOPK):
                pool.indirect_dma_start(
                    out=rows_in, out_offset=bass.IndirectOffsetOnAxis(ap=slot_i[:, c, t:t + 1], axis=0),
                    in_=stage_rows[t % 2], in_offset=None).then_inc(scattered[t % 2], 16)
        for k in range(2):
            pool.wait_ge(y_stored[k], 16 * NT // 2)
        for t in range(NTILE):
            if t >= 2:
                pool.wait_ge(S["sum_ready"], t - 1)
            for c in range(TOPK):
                pool.indirect_dma_start(
                    out=got[t % 2][c], out_offset=None, in_=rows_out,
                    in_offset=bass.IndirectOffsetOnAxis(ap=slot_i[:, c, t:t + 1], axis=0))\
                    .then_inc(got_rows[t % 2][c], 16)

    @block.tensor
    def _(pe):
        def turn(bank, src, done):
            n = len(src)
            for k, a in enumerate(src):
                ins = pe.transpose(bank[:, k * P:(k + 1) * P], a, ident)
            ins.then_inc(done, 1)

        def product(bank, lhs, rhs, done, last=True):
            for k in range(len(lhs)):
                ins = pe.matmul(bank, lhs[k], rhs[k], start=(k == 0), stop=(k == len(lhs) - 1))
            if done is not None:
                ins.then_inc(done, 1)

        def split_product(bank, lhs, rhs, done, last=True):
            for k in range(len(lhs[0])):
                for a, b in ((0, 0), (0, 1), (1, 0)):
                    ins = pe.matmul(bank, lhs[a][k], rhs[b][k], start=(k == 0 and a + b == 0),
                                    stop=(k == len(lhs[0]) - 1 and a == 1))
            if done is not None:
                ins.then_inc(done, 1)

        def blocks(halves, lo=None, hi=None):
            return [[h[:, k, lo:hi] for k in range(h.shape[1])] for h in halves]

        def turn_ctx(j):
            wait(pe, S["ctx_loaded"], j.n(16, 16))
            for k, bank in enumerate((bank_ma, bank_mb)):
                turn(bank, [ctx_rows[:, t, k * P:(k + 1) * P] for t in range(4)], S["ctx_turned"])

        def project_kv(j, t):
            wait(pe, S["ctx_t_ready"], j.n(2, 2))
            if t >= 2:
                wait(pe, S["kv_ready"], j.n(4, t - 1))
            bank = (bank_ma, bank_mb)[t % 2]
            product(bank, [ctx_t[:, k, t * P:(t + 1) * P] for k in range(DK)],
                    [w_kv[:, k, :] for k in range(DK)], S["kv_done"])

        def turn_k(j):
            wait(pe, S["k_rot_ready"], j.n(1, 1))
            for g, bank in enumerate((bank_tb, bank_mb)):
                turn(bank, [k_rot[:, t, g * P:(g + 1) * P] for t in range(4)], S["k_turned"])

        def turn_xn(j):
            wait(pe, S["xn_ready"], j.n(1, 1))
            turn(bank_ta, [xn[:, k * P:(k + 1) * P] for k in range(DK)], S["xn_turned"])

        def project_q(j):
            wait(pe, S["xn_t_ready"], j.n(1, 1))
            product(bank_ta[:, 0:D], [xn_t[:, k, :] for k in range(DK)], [w_q[:, k, :] for k in range(DK)],
                    S["q_done"])

        def turn_q(j):
            wait(pe, S["q_rot_ready"], j.n(1, 1))
            turn(bank_mb, [q_rot[:, g * P:(g + 1) * P] for g in range(2)], S["q_turned"])

        def scores(p, b):
            wait(pe, S["masks_ready"], p.n(1, 1))
            wait(pe, S["k_t_ready"], p.n(2, 2))
            wait(pe, S["q_t_ready"], p.n(1, 1))
            for r in range(4):
                pe.matmul(ps[:, r, :].rearrange("p (g j) -> p g j", g=2), ident_bf, bc(masks[p.par][:, b, :], 1, 2),
                          start=True, stop=False)
            for g in range(2):
                for r in range(4):
                    q = slice(32 * r, 32 * r + 32)
                    ins = pe.matmul(ps[:, r, g * SK:(g + 1) * SK], q_t[q, g, b, :, :].rearrange("p a i -> p (a i)"),
                                    k_t[q, g, b, :], start=False, stop=(g == 1))
            ins.then_inc(S["scores_done"], 1)

        def turn_probs(p, b):
            for r in range(4):
                wait(pe, S["exp_done"], p.n(16, 8 * b + 2 * r + 2))
                if r >= 2:
                    wait(pe, S["probs_lo_ready"], p.n(8, 4 * b + r - 1))
                turn(probs_bank(b, r),
                     [probs[b][:, 2 * r + g, t * P:(t + 1) * P] for g in range(2) for t in range(2)],
                     S["probs_turned"])

        def weigh_values(p, b, bank):
            wait(pe, S["probs_lo_ready"], p.n(8, 4 * b + 4))
            wait(pe, S["v_lo_ready"], p.n(1, 1))
            for hp in range(8):
                g, r = hp // 4, hp % 4
                split_product(bank[:, hp * 32:hp * 32 + 32],
                              [[h[:, r, (2 * g + t) * P:(2 * g + t + 1) * P] for t in range(2)] for h in probs_s],
                              [[h[:, 2 * b + t, hp * 32:hp * 32 + 32] for t in range(2)] for h in v_s[p.par]],
                              S["av_done"] if hp == 7 else None)

        def turn_heads(p, b, bank):
            wait(pe, S["av_ready"], p.n(2, b + 1))
            turn(bank, [heads_out[b].rearrange("p h c -> p (h c)")], S["heads_turned"])

        def project_out(p):
            wait(pe, S["heads_t_ready"], p.n(2, 2))
            product(bank_mb[:, 0:D], [heads_t[:, a, :, :].rearrange("p b i -> p (b i)") for a in range(2)],
                    [w_o[:, a, :] for a in range(2)], S["proj_done"])

        def g_turn_x(g):
            wait(pe, S["x1n_ready"], g.n(1, 1))
            turn(bank_ta, [x1n[:, k * P:(k + 1) * P] for k in range(DK)], S["x1n_turned"])

        def g_project(g):
            wait(pe, S["x1n_lo_ready"], g.n(1, 1))
            wait(pe, S["gla_lo_ready"], 3)
            split_product(bank_tb, blocks(x1n_s), blocks(w_gvg_s), S["vg_done"])
            for c in range(2):
                split_product(bank_ta[:, c * P:(c + 1) * P], blocks(w_gqk_s, c * P, (c + 1) * P), blocks(x1n_s), None)
            split_product(bank_ta[0:16, 2 * P:3 * P], blocks(w_g1_s), blocks(x1n_s), S["qkl_done"])

        def g_gate(g):
            wait(pe, S["low_t_ready"], g.n(1, 1))
            wait(pe, S["g_v_ready"], g.n(1, 1))
            product(bank_tb[:, 0:P], [w_g2[0:16, :]], [low_t[0:16, :]], S["kg_done"])

        def g_scores(g):
            wait(pe, S["k_heads_ready"], g.n(1, 1))
            wait(pe, S["q_heads_ready"], g.n(1, 1))
            for r in range(4):
                q = slice(32 * r, 32 * r + 32)
                for b in range(2):
                    for c in range(NCH):
                        ins = pe.matmul(ps[SQ * b:SQ * b + SQ, r, c * 64:(c + 1) * 64], k_heads[q, c, b, :],
                                        q_heads[q, b, c, :, :].rearrange("p h t -> p (h t)"), start=True, stop=True)
            ins.then_inc(S["a_done"], 1)

        def g_values(g):
            wait(pe, S["a_lo_ready"], g.n(1, 1))
            wait(pe, S["g_v_ready"], g.n(1, 1))
            apart(pe)
            for b in range(2):
                rows = slice(SQ * b, SQ * b + SQ)
                for h in range(H):
                    split_product(bank_ma[rows, h * GV:(h + 1) * GV],
                                  [[a[rows, h // 4, h % 4, :, :].rearrange("p c t -> p (c t)")] for a in a_s],
                                  [[a[rows, 0, h * GV:(h + 1) * GV]] for a in g_v_s],
                                  S["go_done"] if (b, h) == (1, H - 1) else None)

        def g_turn_out(g):
            wait(pe, S["gn_ready"], g.n(1, 1))
            turn(bank_ma, [g_norm[:, k * P:(k + 1) * P] for k in range(DK)], S["gn_turned"])

        def g_project_out(g):
            wait(pe, S["gn_t_ready"], g.n(1, 1))
            product(bank_mb[:, 0:D], [g_norm_t[:, k, :] for k in range(DK)], [w_go[:, k, :] for k in range(DK)],
                    S["gproj_done"])

        def g_turn_x2(g):
            wait(pe, S["x2n_ready"], g.n(1, 1))
            turn(bank_ta, [x2n[g.par][:, k * P:(k + 1) * P] for k in range(DK)], S["x2n_turned"])

        def g_logits(g):
            wait(pe, S["x2n_t_ready"], g.n(1, 1))
            product(bank_ma[:, 0:NE], [x2n_t[:, k, :] for k in range(DK)], [w_r[:, k, :] for k in range(DK)],
                    S["logits_done"])

        def step(p, nxt=True, gla=True, att=True):
            g, j = p.next(-1), p.next()
            if att:
                wait(pe, S["exp_done"], p.n(16))
                scores(p, 0)
            if gla:
                wait(pe, S["probs_lo_ready"], p.n(8))
                wait(pe, S["x2n_t_ready"], g.n(1))
                g_turn_x(g)
            if nxt:
                wait(pe, S["av_ready"], p.n(2))
                wait(pe, S["logits_ready"], g.n(1))
                wait(pe, S["x1_ready"], p.n(1))
                turn_ctx(j)
            if gla:
                wait(pe, S["heads_t_ready"], p.n(2))
                g_project(g)
            if nxt:
                project_kv(j, 0)
            if gla:
                g_gate(g)
            if nxt:
                for t in range(1, 4):
                    project_kv(j, t)
            if att:
                wait(pe, S["kv_ready"], (j if nxt else p).n(4, 4))
                wait(pe, S["av_ready"], p.n(2))
                wait(pe, S["x1_ready"], p.n(1))
                wait(pe, S["q_t_ready"], p.n(1, 1))
                if gla:
                    wait(pe, S["logits_ready"], g.n(1))
                turn_probs(p, 0)
            if gla:
                wait(pe, S["exp_done"], p.n(16, 8 if att else 0))
                g_scores(g)
            if nxt:
                wait(pe, S["k_heads_ready"], p.n(1))
                wait(pe, S["q_nat_ready"], p.n(1, 1))
                turn_xn(j)
            if att:
                weigh_values(p, 0, bank_mb)
                wait(pe, S["exp_done"], p.n(16, 8))
                wait(pe, S["a_ready"], p.n(4))
                scores(p, 1)
            if gla:
                if not att:
                    wait(pe, S["logits_ready"], g.n(1))
                    wait(pe, S["av_ready"], p.n(2))
                g_values(g)
            if att:
                wait(pe, S["go_ready"], p.n(1))
                turn_heads(p, 0, bank_ma)
            if nxt:
                wait(pe, S["av_ready"], p.n(2, 1))
                wait(pe, S["kg_abs_ready"], p.n(1))
                turn_k(j)
                project_q(j)
            if att:
                if nxt:
                    wait(pe, S["q_nat_ready"], j.n(1, 1))
                    wait(pe, S["k_t_ready"], j.n(2, 1))
                else:
                    wait(pe, S["k_heads_ready"], p.n(1))
                    wait(pe, S["kg_abs_ready"], p.n(1))
                turn_probs(p, 1)
            if gla:
                if att:
                    wait(pe, S["heads_t_ready"], p.n(2, 1))
                g_turn_out(g)
                if nxt:
                    wait(pe, S["k_t_ready"], j.n(2, 2))
                elif att:
                    wait(pe, S["av_ready"], p.n(2, 1))
                else:
                    wait(pe, S["x1_ready"], p.n(1))
                g_project_out(g)
            if att:
                wait(pe, S["gn_t_ready"], p.n(1))
                wait(pe, S["heads_t_ready"], p.n(2, 1))
                weigh_values(p, 1, bank_ma)
            if nxt:
                wait(pe, S["x2_ready"], p.n(1))
                wait(pe, S["k_t_ready"], j.n(2, 2))
                turn_q(j)
            if att:
                turn_heads(p, 1, bank_tb)
            if gla:
                if att:
                    wait(pe, S["probs_lo_ready"], p.n(8, 8))
                g_turn_x2(g)
            if att:
                if nxt:
                    wait(pe, S["q_t_ready"], j.n(1, 1))
                wait(pe, S["x2_ready"], p.n(1))
                project_out(p)
            if gla:
                if att:
                    wait(pe, S["av_ready"], p.n(2, 2))
                g_logits(g)

        pe.wait_ge(S["consts_loaded"], 16)
        pe.wait_ge(S["weights_loaded"], 16 * WEIGHT_DMAS)
        pe.wait_ge(S["ident_bf_ready"], 1)
        zero = Step(0, 0)
        turn_ctx(zero)
        for t in range(4):
            project_kv(zero, t)
        turn_xn(zero)
        pe.wait_ge(S["kv_ready"], 4)
        turn_k(zero)
        project_q(zero)
        pe.wait_ge(S["k_t_ready"], 2)
        turn_q(zero)
        over_pairs(pe, lambda p: step(p, gla=False), step, lambda p: step(p, nxt=False))
        step(Step(0, NPAIR), nxt=False, att=False)

        pe.wait_ge(S["logits_ready"], NPAIR)
        pe.wait_ge(S["route_step"], ROUTE_SELECTED)
        sel = r_sel.rearrange("p t e -> p (t e)")
        pe.matmul(bank_ma[:, 0:L], const("upper"), sel, start=True, stop=True).then_inc(S["route_mm"], 1)
        pe.matmul(bank_mb[:, 0:L], r_ones, sel, start=True, stop=True).then_inc(S["route_mm"], 1)

        def turn_rows(t, k, n):
            wait(pe, rows_loaded[k], n * 16)
            wait(pe, S["rows_t_ready"], t)
            turn(ps[:, 0, :], [e_rows[k][:, c * P:(c + 1) * P] for c in range(DK)], S["rows_turned"])

        def up(t, k, e):
            wait(pe, S["rows_t_ready"], t + 1)
            wait(pe, S["hid_ready"], t)
            for q in range(4):
                for c in range(DK):
                    w = experts[:, e, c * 2 * HID + q * HH:c * 2 * HID + (q + 1) * HH]
                    ins = pe.matmul(ps[:, 1 + q, 0:HH], e_rows_t[k][:, c, :], w, start=(c == 0), stop=(c == DK - 1))
            ins.then_inc(S["up_done"], 1)

        def turn_hidden(t):
            wait(pe, S["hid_ready"], t + 1)
            for half, free in enumerate(("hid_t_lo", "hid_t_hi")):
                wait(pe, S[free], t)
                for c in range(3):
                    blk = 3 * half + c
                    ins = pe.transpose(ps[:, 5 + half, c * P:(c + 1) * P], e_hid[:, blk * P:(blk + 1) * P], ident)
                ins.then_inc(S["hid_turned"], 1)

        def down(t, e):
            wait(pe, S["hid_t_lo"], t + 1)
            wait(pe, S["hid_t_hi"], t + 1)
            wait(pe, S["y_ready"], t)
            for c in range(HT):
                n = P if c < HT - 1 else HR
                ins = pe.matmul(ps[:, 7, 0:D], e_hid_t[0:n, c, :],
                                experts[0:n, e, EW_UP + c * D:EW_UP + (c + 1) * D],
                                start=(c == 0), stop=(c == HT - 1))
            ins.then_inc(S["down_done"], 1)

        pe.wait_ge(S["early_experts"], 64)
        pe.wait_ge(S["gn_t_ready"], NPAIR)
        pe.wait_ge(S["tail_zero"], 1)
        pe.wait_ge(S["a_ready"], 4 * NPAIR)
        pe.wait_ge(S["x2n_t_ready"], NPAIR)
        turn_rows(0, 0, 1)
        up(0, 0, 0)
        turn_rows(1, 1, 1)
        pe.wait_ge(S["route_step"], ROUTE_SELECTED + 6)
        turn_hidden(0)

        def tile(t, k, e, e_before, n_next):
            up(t, k, e)
            down(t - 1, e_before)
            turn_rows(t + 1, 1 - k, n_next)
            turn_hidden(t)

        pe.wait_ge(S["route_step"], ROUTE_DONE)
        tile(1, 1, 0, 0, 2)
        with pe.Fori(1, NTILE // 2) as i:
            tile(i * 2, 0, 0, 0, i + 1)
            tile(i * 2 + 1, 1, 0, 0, i + 2)
        pe.wait_ge(S["late_experts"], 64 * NE)
        pe.wait_ge(S["table_ready"], 1)
        with pe.Fori(NTILE // 2, NT // 2 - 1) as i:
            e0 = pe.value_load(tile_e[0:1, bass.ds(i * 2 - 1, 1)], min_val=0, max_val=NE)
            e1 = pe.value_load(tile_e[0:1, bass.ds(i * 2, 1)], min_val=0, max_val=NE)
            e2 = pe.value_load(tile_e[0:1, bass.ds(i * 2 + 1, 1)], min_val=0, max_val=NE)
            tile(i * 2, 0, e1, e0, i + 1)
            tile(i * 2 + 1, 1, e2, e1, i + 2)
        e0 = pe.value_load(tile_e[0:1, NT - 3:NT - 2], min_val=0, max_val=NE)
        e1 = pe.value_load(tile_e[0:1, NT - 2:NT - 1], min_val=0, max_val=NE)
        e2 = pe.value_load(tile_e[0:1, NT - 1:NT], min_val=0, max_val=NE)
        tile(NT - 2, 0, e1, e0, NT // 2)
        up(NT - 1, 1, e2)
        down(NT - 2, e1)
        turn_hidden(NT - 1)
        down(NT - 1, e2)

    @block.scalar
    def _(act):
        def copy(dst, src, done):
            nc.scalar.activation(dst, src, ACT.Copy).then_inc(done, 1)

        def rstd(k, which, n):
            wait(act, S[which + "_stat_ready"], n)
            nc.scalar.activation(stats[k][:, 8:9], stats[k][:, 7:8], ACT.Ln, bias=const("eps"))\
                .then_inc(S[which + "_log_ready"], 1)
            wait(act, S[which + "_log_ready"], n)
            nc.scalar.activation(stats[k][:, 9:10], stats[k][:, 8:9], ACT.Exp, scale=-0.5)\
                .then_inc(S[which + "_rstd_ready"], 1)

        def ctx_copies(j):
            for k, bank in enumerate((bank_ma, bank_mb)):
                wait(act, S["ctx_turned"], j.n(2, k + 1))
                copy(ctx_t[:, k, :], bank, S["ctx_t_ready"])

        def k_copies(j):
            wait(act, S["scores_done"], j.n(2))
            for g, bank in enumerate((bank_tb, bank_mb)):
                wait(act, S["k_turned"], j.n(2, g + 1))
                copy(k_t[:, g, :, :].rearrange("p b j -> p (b j)"), bank, S["k_t_ready"])

        def exps(p, b, r):
            wait(act, S["max_ready"], p.n(8, 4 * b + r + 1))
            wait(act, S["probs_turned"], p.n(8, 4 * b - 4))
            wait(act, S["inv_ready"], p.n(2, b - 1))
            for g in range(2):
                hp = 4 * g + r
                nc.scalar.activation(probs[b][:, 2 * r + g, :], ps[:, r, g * SK:(g + 1) * SK], ACT.Exp,
                                     bias=neg_max[b][:, hp:hp + 1], accum_out=row_sum[b][:, hp:hp + 1])\
                    .then_inc(S["exp_done"], 1)

        def probs_high(p, b):
            wait(act, S["av_done"], p.n(2, b))
            for r in range(4):
                wait(act, S["probs_turned"], p.n(8, 4 * b + r + 1))
                copy(probs_s[0][:, r, :], probs_bank(b, r), S["probs_hi_ready"])

        def heads_copy(p, b, bank):
            wait(act, S["heads_turned"], p.n(2, b + 1))
            wait(act, S["proj_done"], p.n(1))
            copy(heads_t[:, :, b, :], bank[:, 0:P].rearrange("p (a i) -> p a i", a=2), S["heads_t_ready"])

        def two_blocks(dst, bank, turned, n, done):
            wait(act, S[turned], n)
            copy(dst, bank[:, 0:D].rearrange("p (k n) -> p k n", k=DK), S[done])

        def step(p, nxt=True, gla=True, att=True):
            g, j = p.next(-1), p.next()
            if gla:
                two_blocks(x1n_s[0], bank_ta, "x1n_turned", p.n(1), "x1n_hi_ready")
            if nxt:
                rstd(0, "x", j.n(1, 1))
                ctx_copies(j)
            if att:
                exps(p, 0, 0)
            if gla:
                wait(act, S["qkl_done"], p.n(1))
                nc.scalar.activation(low_t[0:16, :], bank_ta[0:16, 2 * P:3 * P], ACT.Copy, scale=1 / W_SCALE)\
                    .then_inc(S["low_t_ready"], 1)
            if att:
                for r in range(1, 4):
                    exps(p, 0, r)
            if gla:
                wait(act, S["kg_abs_ready"], p.n(1))
                nc.scalar.activation(kg_exp, kg_abs, ACT.Exp, scale=-1.0).then_inc(S["kg_exp_ready"], 1)
                wait(act, S["kg_exp_ready"], p.n(1))
                nc.scalar.activation(kg_ln, kg_exp, ACT.Ln, bias=const("one")).then_inc(S["kg_ln_ready"], 1)
                wait(act, S["dec_ready"], p.n(1))
                nc.scalar.activation(q_dec, q_dec, ACT.Exp, scale=1.0 / GATE_NORM).then_inc(S["dec_exp_q"], 1)
                wait(act, S["dec_min"], p.n(1))
                nc.scalar.activation(k_dec.rearrange("p c b i -> p (c b i)"), k_dec.rearrange("p c b i -> p (c b i)"),
                                     ACT.Exp, bias=const("lnscale"), scale=1.0 / GATE_NORM).then_inc(S["dec_exp_k"], 1)
            if att:
                probs_high(p, 0)
            if gla:
                wait(act, S["gate_ready"], p.n(1))
                nc.scalar.activation(gate_e, gate, ACT.Exp, scale=-1.0).then_inc(S["gate_exp_ready"], 1)
                wait(act, S["gate_exp_ready"], p.n(1))
                nc.scalar.activation(gate_e, gate_e, ACT.Ln, bias=const("one")).then_inc(S["gate_one"], 1)
                wait(act, S["gate_one"], p.n(1))
                wait(act, S["gn_scaled"], g.n(1))
                nc.scalar.activation(gate_i, gate_e, ACT.Exp, scale=-1.0).then_inc(S["gate_inv"], 1)
            if nxt:
                two_blocks(xn_t, bank_ta, "xn_turned", j.n(1, 1), "xn_t_ready")
            if att:
                exps(p, 1, 0)
            if gla:
                wait(act, S["go_done"], p.n(1))
                nc.scalar.activation(g_out, bank_ma[:, 0:D], ACT.Copy, scale=1 / (A_SCALE * V_SCALE))\
                    .then_inc(S["go_ready"], 1)
            if att:
                exps(p, 1, 1)
                heads_copy(p, 0, bank_ma)
                exps(p, 1, 2)
            if nxt:
                k_copies(j)
            if att:
                exps(p, 1, 3)
            if gla:
                wait(act, S["gs_var"], p.n(1))
                nc.scalar.activation(g_stat[:, 2, :], g_stat[:, 1, :], ACT.Ln, bias=const("eps"), scale=1.0 / GV)\
                    .then_inc(S["gs_log"], 1)
                wait(act, S["gs_log"], p.n(1))
                nc.scalar.activation(g_stat[:, 3, :], g_stat[:, 2, :], ACT.Exp, scale=-0.5).then_inc(S["gs_rstd"], 1)
            if att:
                probs_high(p, 1)
            if gla:
                two_blocks(g_norm_t, bank_ma, "gn_turned", p.n(1), "gn_t_ready")
                rstd(2, "x2", p.n(1))
            if att:
                heads_copy(p, 1, bank_tb)
            if gla:
                two_blocks(x2n_t, bank_ta, "x2n_turned", p.n(1), "x2n_t_ready")
                wait(act, S["logits_done"], p.n(1))
                copy(logits[:, g.n(1), :] if isinstance(g.n(1), int) else
                     logits[:, bass.ds(g.n(1), 1), :].rearrange("p a e -> p (a e)"), bank_ma[:, 0:NE],
                     S["logits_ready"])
            if att:
                rstd(1, "x1", p.n(1, 1))

        act.preload_act_table_set("natural_log_exp_and_others")
        act.wait_ge(S["consts_loaded"], 16)
        zero = Step(0, 0)
        rstd(0, "x", 1)
        ctx_copies(zero)
        two_blocks(xn_t, bank_ta, "xn_turned", 1, "xn_t_ready")
        k_copies(zero)
        over_pairs(act, lambda p: step(p, gla=False), step, lambda p: step(p, nxt=False))
        step(Step(0, NPAIR), nxt=False, att=False)

        act.wait_ge(S["route_step"], 1)
        nc.scalar.activation(r_e, r_z, ACT.Exp, scale=-1.0).then_inc(S["route_exp"], 1)

        def rows_copy(t, k):
            wait(act, S["up_done"], t - 1)
            wait(act, S["rows_turned"], t + 1)
            copy(e_rows_t[k], ps[:, 0, 0:D].rearrange("p (k n) -> p k n", k=DK), S["rows_t_ready"])

        def silu(t):
            wait(act, S["up_done"], t + 1)
            wait(act, S["hid_ready"], t)
            nc.scalar.activation(e_silu.rearrange("p (c n) -> p c n", c=2), ps[:, 1:3, 0:HH], ACT.Silu)\
                .then_inc(S["silu_ready"], 1)

        def hidden_copy(t):
            wait(act, S["hid_turned"], t * 2 + 1)
            wait(act, S["down_done"], t)
            copy(e_hid_t[:, 0:3, :].rearrange("p c n -> p (c n)"), ps[:, 5, 0:3 * P], S["hid_t_lo"])

        rows_copy(0, 0)
        silu(0)
        rows_copy(1, 1)
        hidden_copy(0)

        def tile(t, k):
            silu(t)
            rows_copy(t + 1, 1 - k)
            hidden_copy(t)

        tile(1, 1)
        with act.Fori(1, NT // 2 - 1) as i:
            tile(i * 2, 0)
            tile(i * 2 + 1, 1)
        tile(NT - 2, 0)
        silu(NT - 1)
        hidden_copy(NT - 1)

    @block.vector
    def _(dve):
        v = nc.vector

        def copy(dst, src, done):
            v.tensor_copy(dst, src).then_inc(done, 1)

        def norm_stats(k, src, which, n):
            v.bn_stats(stats[k][:, 0:6], src).then_inc(S[which + "_bn"], 1)
            wait(dve, S[which + "_bn"], n)
            apart(dve)
            v.bn_aggr(stats[k][:, 6:8], stats[k][:, 0:6]).then_inc(S[which + "_stat_ready"], 1)

        def norm_apply(k, dst, src, which, done, n):
            wait(dve, S[which + "_rstd_ready"], n)
            v.tensor_scalar(dst, src, stats[k][:, 6:7], stats[k][:, 9:10], ALU.subtract, ALU.mult)\
                .then_inc(S[done], 1)

        def x_stats(j):
            wait(dve, x_loaded[j.par], j.half * 16 + 16)
            norm_stats(0, x_in[j.par], "x", j.n(1, 1))

        def x_norm(j):
            wait(dve, S["xn_turned"], j.n(1))
            norm_apply(0, xn, x_in[j.par], "x", "xn_ready", j.n(1, 1))

        def max_rows(p, b):
            wait(dve, S["scores_done"], p.n(2, b + 1))
            wait(dve, S["exp_done"], p.n(16, 8 * b - 8))
            nm = neg_max[b].rearrange("p (g r) -> p g r", g=2)
            for r in range(4):
                v.tensor_reduce(nm[:, :, r], ps[:, r, :].rearrange("p (g j) -> p g j", g=2), AX.X, ALU.max,
                                negate=True).then_inc(S["max_ready"], 1)

        def kv_bias(j, t):
            wait(dve, S["kv_done"], j.n(4, t + 1))
            wait(dve, S["k_swap_ready"], j.n(1))
            wait(dve, S["k_prod_ready"], j.n(1))
            wait(dve, S["v_lo_ready"], j.n(1))
            bank = (bank_ma, bank_mb)[t % 2]
            v.tensor_tensor(kv[:, t, :], bank, b_kv, ALU.add).then_inc(S["kv_ready"], 1)

        def k_cos(j):
            wait(dve, S["kv_ready"], j.n(4, 4))
            wait(dve, S["k_turned"], j.n(2))
            cos = const("cosk").rearrange("p (t c) -> p t c", t=2)
            for b in range(2):
                ins = v.tensor_tensor(k_rot[:, 2 * b:2 * b + 2, :].rearrange("p t (h c) -> p t h c", h=H),
                                      kv[:, 2 * b:2 * b + 2, 0:D].rearrange("p t (h c) -> p t h c", h=H),
                                      bc(cos, 2, H), ALU.mult)
            ins.then_inc(S["k_prod_ready"], 1)

        def k_add(j):
            wait(dve, S["k_swap_ready"], j.n(1, 1))
            wait(dve, S["k_prod_ready"], j.n(1, 1))
            v.tensor_tensor(k_rot, k_rot, k_swap, ALU.add).then_inc(S["k_rot_ready"], 1)

        def q_bias(j):
            wait(dve, S["q_done"], j.n(1, 1))
            wait(dve, S["q_swap_ready"], j.n(1))
            v.tensor_tensor(q_nat, bank_ta[:, 0:D], b_q, ALU.add).then_inc(S["q_nat_ready"], 1)
            wait(dve, S["q_nat_ready"], j.n(1, 1))
            wait(dve, S["q_turned"], j.n(1))
            v.tensor_tensor(q_rot.rearrange("p (h c) -> p h c", h=H), q_nat.rearrange("p (h c) -> p h c", h=H),
                            bc(const("cosq"), 1, H), ALU.mult).then_inc(S["q_prod_ready"], 1)

        def q_add(j):
            wait(dve, S["q_swap_ready"], j.n(1, 1))
            wait(dve, S["q_prod_ready"], j.n(1, 1))
            v.tensor_tensor(q_rot, q_rot, q_swap, ALU.add).then_inc(S["q_rot_ready"], 1)

        def q_heads_split(j):
            wait(dve, S["q_turned"], j.n(1, 1))
            wait(dve, S["scores_done"], j.n(2))
            for a in range(2):
                ins = v.tensor_scalar(q_t[:, :, :, a, :],
                                      bank_mb[:, 0:D].rearrange("p (g b i) -> p g b i", g=2, b=2),
                                      const("par")[:, a:a + 1], None, ALU.mult)
            ins.then_inc(S["q_t_ready"], 1)

        def probs_low(p, b):
            for r in range(4):
                wait(dve, S["probs_hi_ready"], p.n(8, 4 * b + r + 1))
                v.tensor_tensor(probs_s[1][:, r, :], probs_bank(b, r), probs_s[0][:, r, :], ALU.subtract)\
                    .then_inc(S["probs_lo_ready"], 1)

        def normalise(p, b, bank):
            wait(dve, S["exp_done"], p.n(16, 8 * b + 8))
            v.reciprocal(row_inv, row_sum[b]).then_inc(S["inv_ready"], 1)
            wait(dve, S["inv_ready"], p.n(2, b + 1))
            wait(dve, S["av_done"], p.n(2, b + 1))
            wait(dve, S["heads_turned"], p.n(2, b - 1))
            for a in range(2):
                rows = slice(SQ * a, SQ * a + SQ)
                src = bank[rows, 0:D].rearrange("p (h a c) -> p h a c", h=8, a=2)[:, :, a, :]
                ins = v.tensor_tensor(heads_out[b][rows], src, bc(row_inv[rows, :], 2, HC), ALU.mult)
            ins.then_inc(S["av_ready"], 1)

        def add_x1(p):
            wait(dve, S["proj_done"], p.n(1, 1))
            wait(dve, S["x_res_ready"], p.n(1, 1))
            v.tensor_tensor(x1, bank_mb[:, 0:D], x_res, ALU.add).then_inc(S["x1_ready"], 1)
            wait(dve, S["x1_ready"], p.n(1, 1))
            norm_stats(1, x1, "x1", p.n(1, 1))
            norm_apply(1, x1n, x1, "x1", "x1n_ready", p.n(1, 1))

        def step(p, nxt=True, gla=True, att=True):
            g, j = p.next(-1), p.next()
            n = p.n(1)
            if gla:
                wait(dve, S["x1n_hi_ready"], n)
                v.tensor_tensor(x1n_s[1], bank_ta[:, 0:D].rearrange("p (k n) -> p k n", k=DK), x1n_s[0], ALU.subtract)\
                    .then_inc(S["x1n_lo_ready"], 1)
            if nxt:
                x_stats(j)
            if att:
                max_rows(p, 0)
            if gla:
                wait(dve, S["vg_done"], n)
                v.tensor_scalar(g_v_s[0][:, 0, :], bank_tb[:, 0:D], V_SCALE / W_SCALE, None, ALU.mult)\
                    .then_inc(S["g_v_hi_ready"], 1)
                v.scalar_tensor_tensor(out=gate, in0=bank_tb[:, D:2 * D], scalar=1 / W_SCALE, in1=b_g, op0=ALU.mult,
                                       op1=ALU.add).then_inc(S["gate_ready"], 1)
                wait(dve, S["g_v_hi_ready"], n)
                v.scalar_tensor_tensor(out=g_v_s[1][:, 0, :], in0=bank_tb[:, 0:D], scalar=V_SCALE / W_SCALE,
                                       in1=g_v_s[0][:, 0, :], op0=ALU.mult, op1=ALU.subtract)\
                    .then_inc(S["g_v_ready"], 1)
            if nxt:
                x_norm(j)
                kv_bias(j, 0)
            if gla:
                wait(dve, S["kg_done"], n)
                v.tensor_scalar(kg_min, bank_tb[:, 0:P], 0.0, None, ALU.min).then_inc(S["kg_min_ready"], 1)
                wait(dve, S["kg_min_ready"], n)
                v.scalar_tensor_tensor(out=kg_abs, in0=kg_min, scalar=-2.0, in1=bank_tb[:, 0:P], op0=ALU.mult,
                                       op1=ALU.add).then_inc(S["kg_abs_ready"], 1)
            if nxt:
                kv_bias(j, 1)
            if gla:
                wait(dve, S["kg_ln_ready"], n)
                wait(dve, S["kg_min_ready"], n)
                v.tensor_tensor(log_gate, kg_min, kg_ln, ALU.subtract).then_inc(S["log_gate_ready"], 1)
                wait(dve, S["log_gate_ready"], n)
                for b in range(2):
                    ins = v.tensor_tensor_scan(cum[:, b, :], log_gate[:, b * SQ:(b + 1) * SQ],
                                               log_gate[:, b * SQ:(b + 1) * SQ], 0.0, ALU.add, ALU.bypass)
                ins.then_inc(S["cum_ready"], 1)
                wait(dve, S["cum_ready"], n)
                copy(ref[:, :, 1:NCH], cum.rearrange("p b (c t) -> p b c t", t=CH)[:, :, 0:NCH - 1, CH - 1],
                     S["ref_ready"])
                wait(dve, S["ref_ready"], n)
                v.tensor_tensor(q_dec.rearrange("p (b c t) -> p b c t", b=2, c=NCH),
                                cum.rearrange("p b (c t) -> p b c t", t=CH), bc(ref, 3, CH), ALU.subtract)\
                    .then_inc(S["dec_ready"], 1)
                v.tensor_tensor(k_dec, bc(ref.rearrange("p b c -> p c b"), 3, SQ), bc(cum, 1, NCH), ALU.subtract)\
                    .then_inc(S["dec_k_ready"], 1)
                wait(dve, S["dec_k_ready"], n)
                kd = k_dec.rearrange("p c b i -> p (c b i)")
                v.tensor_scalar(kd, kd, BOUND * GATE_NORM, None, ALU.min).then_inc(S["dec_min"], 1)
            if nxt:
                kv_bias(j, 2)
                kv_bias(j, 3)
            if gla:
                wait(dve, S["dec_exp_q"], n)
                v.tensor_tensor(qs_t, bank_ta[:, 0:P], q_dec, ALU.mult).then_inc(S["qs_ready"], 1)
                wait(dve, S["dec_exp_k"], n)
                v.tensor_tensor(k_heads, bc(bank_ta[:, P:2 * P].rearrange("p (b i) -> p b i", b=2), 1, NCH), k_dec,
                                ALU.mult).then_inc(S["k_heads_ready"], 1)
                wait(dve, S["qs_ready"], n)
                v.tensor_tensor(q_heads.rearrange("p b c h t -> p (b c) h t"),
                                bc(qs_t.rearrange("p (m t) -> p m t", t=CH), 2, 4),
                                bc(bc(const("head4"), 1, 2 * NCH), 3, CH), ALU.mult).then_inc(S["q_heads_ready"], 1)
            if att:
                probs_low(p, 0)
            if nxt:
                k_cos(j)
            if gla:
                wait(dve, S["a_done"], n)
                for r in range(4):
                    v.tensor_tensor(a_t[:, r].rearrange("p h c t -> p c h t"), ps[:, r, 0:256].rearrange("p (c h t) -> p c h t", c=NCH, h=4),
                                    bc(const("gla").rearrange("p (c t) -> p c t", c=NCH), 2, 4), ALU.mult)\
                        .then_inc(S["a_ready"], 1)
            if nxt:
                k_add(j)
            if att:
                normalise(p, 0, bank_mb)
            if gla:
                wait(dve, S["gate_inv"], n)
                v.tensor_tensor(gate_i, gate, gate_i, ALU.mult).then_inc(S["gate_silu"], 1)
            if att:
                max_rows(p, 1)
            if gla:
                wait(dve, S["go_ready"], n)
                heads = g_out.rearrange("p (h c) -> p h c", h=H)
                sq = g_sq.rearrange("p (h c) -> p h c", h=H)
                gn = g_norm.rearrange("p (h c) -> p h c", h=H)
                v.tensor_reduce(g_stat[:, 0, :], heads, AX.X, ALU.add).then_inc(S["gs_sum"], 1)
                wait(dve, S["gs_sum"], n)
                v.tensor_scalar(g_stat[:, 0, :], g_stat[:, 0, :], 1.0 / GV, None, ALU.mult).then_inc(S["gs_mean"], 1)
                wait(dve, S["gs_mean"], n)
                v.tensor_tensor(heads, heads, bc(g_stat[:, 0, :], 2, GV), ALU.subtract).then_inc(S["gs_cent"], 1)
                wait(dve, S["gs_cent"], n)
                v.tensor_tensor(sq, heads, heads, ALU.mult).then_inc(S["gs_sq"], 1)
                wait(dve, S["gs_sq"], n)
                v.tensor_reduce(g_stat[:, 1, :], sq, AX.X, ALU.add).then_inc(S["gs_var"], 1)
                wait(dve, S["gate_silu"], n)
                wait(dve, S["gs_var"], n)
                v.tensor_tensor(g_sq, g_out, gate_i, ALU.mult).then_inc(S["gn_scaled"], 1)
                wait(dve, S["gn_scaled"], n)
                wait(dve, S["gs_rstd"], n)
                v.tensor_tensor(gn, sq, bc(g_stat[:, 3, :], 2, GV), ALU.mult).then_inc(S["gn_ready"], 1)
            if nxt:
                q_bias(j)
            if nxt:
                q_add(j)
            if att:
                probs_low(p, 1)
            if gla:
                wait(dve, S["gproj_done"], n)
                gt = g.n(1)
                x2 = x2_all[:, gt, :] if isinstance(gt, int) else \
                    x2_all[:, bass.ds(gt, 1), :].rearrange("p a d -> p (a d)")
                v.tensor_tensor(x2, bank_mb[:, 0:D], x1, ALU.add).then_inc(S["x2_ready"], 1)
                wait(dve, S["x2_ready"], n)
                apart(dve)
                norm_stats(2, x2, "x2", n)
            if att:
                normalise(p, 1, bank_ma)
            if gla:
                wait(dve, x2n_stored[g.par], g.half * 16)
                norm_apply(2, x2n[g.par], x2, "x2", "x2n_ready", n)
            if nxt:
                q_heads_split(j)
            if att:
                add_x1(p)

        dve.wait_ge(S["consts_loaded"], 16)
        dve.wait_ge(S["weights_loaded"], 16 * WEIGHT_DMAS)
        v.memset(ref[:, :, 0:1], 0.0).then_inc(S["ref_zero"], 1)
        dve.wait_ge(S["ref_zero"], 1)
        zero = Step(0, 0)
        x_stats(zero)
        x_norm(zero)
        for t in range(4):
            kv_bias(zero, t)
        k_cos(zero)
        k_add(zero)
        q_bias(zero)
        q_add(zero)
        q_heads_split(zero)
        for k, (w, (high, low)) in enumerate(((w_gqk, w_gqk_s), (w_g1, w_g1_s), (w_gvg, w_gvg_s))):
            v.tensor_scalar(high, w, W_SCALE, None, ALU.mult).then_inc(S["gla_hi_ready"], 1)
            dve.wait_ge(S["gla_hi_ready"], k + 1)
            v.scalar_tensor_tensor(out=low, in0=w, scalar=W_SCALE, in1=high, op0=ALU.mult, op1=ALU.subtract)\
                .then_inc(S["gla_lo_ready"], 1)
        over_pairs(dve, lambda p: step(p, gla=False), step, lambda p: step(p, nxt=False))
        step(Step(0, NPAIR), nxt=False, att=False)

        count = [0]

        def link(ins):
            ins.then_inc(S["route_step"], 1)
            count[0] += 1
            dve.wait_ge(S["route_step"], count[0])

        dve.wait_ge(S["logits_ready"], NPAIR)
        dve.wait_ge(x2n_stored[0], 16 * NPAIR // 2)
        dve.wait_ge(x2n_stored[1], 16 * NPAIR // 2)
        v.memset(e_hid[:, HID:], 0.0).then_inc(S["tail_zero"], 1)
        dve.wait_ge(S["biasr_loaded"], 16)
        link(v.tensor_tensor(r_z, logits[:, :, :], bc(r_bias, 1, NTILE), ALU.mult))
        dve.wait_ge(S["route_exp"], 1)
        link(v.tensor_scalar(r_c, r_e, 1.0, None, ALU.add))
        link(v.reciprocal(r_p, r_c))
        desc = bc(const("desc"), 1, NTILE)
        for c in range(TOPK):
            link(v.tensor_reduce(r_m[:, c, :], r_p, AX.X, ALU.max))
            link(v.tensor_tensor(r_eq, r_p, bc(r_m[:, c, :], 2, NE), ALU.is_equal))
            link(v.tensor_tensor(r_c, r_eq, desc, ALU.mult))
            link(v.tensor_reduce(r_m[:, 2, :], r_c, AX.X, ALU.max))
            link(v.tensor_tensor(r_oh[c], r_c, bc(r_m[:, 2, :], 2, NE), ALU.is_equal))
            if c == 0:
                link(v.scalar_tensor_tensor(out=r_p, in0=r_oh[0], scalar=-4.0, in1=r_p, op0=ALU.mult, op1=ALU.add))
        link(v.memset(r_ones, 1.0))
        link(v.tensor_tensor(r_sel, r_oh[0], r_oh[1], ALU.add))
        assert count[0] == ROUTE_SELECTED
        link(v.tensor_tensor(r_m[:, 3, :], r_m[:, 0, :], r_m[:, 1, :], ALU.add))
        link(v.reciprocal(r_m[:, 4, :], r_m[:, 3, :]))
        for c in range(TOPK):
            link(v.tensor_tensor(w_tok[:, c, :], r_m[:, c, :], r_m[:, 4, :], ALU.mult))
        dve.wait_ge(S["route_mm"], 2)
        link(v.tensor_copy(r_in.rearrange("p t e -> p (t e)"), bank_ma[:, 0:L]))
        link(v.tensor_copy(r_tot.rearrange("p t e -> p (t e)"), bank_mb[:, 0:L]))
        for e in range(NE):
            link(v.tensor_tensor_scan(r_cum[:, :, e], r_tot[:, :, e], r_tot[:, :, e], 0.0, ALU.add, ALU.bypass))
        link(v.tensor_scalar(r_ni, r_cum[:, NTILE - 1, :], float(P - 1), None, ALU.add))
        link(v.tensor_scalar(r_ni, r_ni, 7, None, ALU.arith_shift_right))
        link(v.tensor_copy(r_n[:, 0, :], r_ni))
        link(v.tensor_tensor_scan(r_n[:, 1, :], r_n[:, 0, :], r_n[:, 0, :], 0.0, ALU.add, ALU.bypass))
        link(v.tensor_tensor(r_n[:, 2, :], r_n[:, 1, :], r_n[:, 0, :], ALU.subtract))
        link(v.tensor_scalar(r_n[:, 3, :], r_n[:, 2, :], float(P), float(NTILE * P), ALU.mult, ALU.add))
        link(v.tensor_tensor(r_pos, r_cum, r_tot, ALU.subtract))
        link(v.tensor_tensor(r_pos, r_pos, r_in, ALU.add))
        link(v.tensor_tensor(r_pos, r_pos, bc(r_n[:, 3, :], 1, NTILE), ALU.add))
        for c in range(TOPK):
            link(v.tensor_tensor(r_c, r_oh[c], r_pos, ALU.mult))
            link(v.tensor_reduce(r_m[:, 5, :], r_c, AX.X, ALU.add))
            link(v.tensor_copy(slot_i[:, c, :], r_m[:, 5, :]))
        link(v.tensor_tensor(r_t, bc(const("tile"), 2, NE), bc(r_n[:, 1, :], 1, NSLOT), ALU.is_ge))
        link(v.tensor_reduce(r_tf, r_t, AX.X, ALU.add))
        link(v.tensor_scalar(r_tf, r_tf, 1.0, float(NE), ALU.add, ALU.min))
        link(v.memset(tile_e[:, 0:NTILE], 0))
        link(v.tensor_copy(tile_e[:, NTILE:], r_tf))
        assert count[0] == ROUTE_DONE
        v.memset(r_ones[:, 0:1], 1.0).then_inc(S["table_ready"], 1)

        def hidden(t):
            wait(dve, S["silu_ready"], t + 1)
            wait(dve, S["hid_turned"], t * 2)
            v.tensor_tensor(e_hid[:, 0:HID].rearrange("p (c n) -> p c n", c=2), ps[:, 3:5, 0:HH],
                            e_silu.rearrange("p (c n) -> p c n", c=2), ALU.mult).then_inc(S["hid_ready"], 1)

        def hidden_copy(t):
            wait(dve, S["hid_turned"], t * 2 + 2)
            wait(dve, S["down_done"], t)
            copy(e_hid_t[:, 3:6, :].rearrange("p c n -> p (c n)"), ps[:, 6, 0:3 * P], S["hid_t_hi"])

        def result(t, k, n):
            wait(dve, S["down_done"], t + 1)
            wait(dve, y_stored[k], n * 16)
            copy(e_y[k], ps[:, 7, 0:D], S["y_ready"])

        hidden(0)
        hidden_copy(0)

        def tile(t, k, n):
            hidden(t)
            result(t - 1, 1 - k, n)
            hidden_copy(t)

        tile(1, 1, 0)
        tile(2, 0, 0)
        tile(3, 1, 1)
        with dve.Fori(2, NT // 2) as i:
            tile(i * 2, 0, i - 1)
            tile(i * 2 + 1, 1, i)
        result(NT - 1, 1, NT // 2 - 1)

        for t in range(NTILE):
            k = t % 2
            x2 = x2_all[:, t, :]
            dve.wait_ge(got_rows[k][2], 16 * (t // 2 + 1))
            v.tensor_tensor(x2, x2, got[k][2], ALU.add).then_inc(S["last_store"], 1)
            for c in range(TOPK):
                dve.wait_ge(got_rows[k][c], 16 * (t // 2 + 1))
                dve.wait_ge(S["last_store"], 2 * t + c + 1)
                v.scalar_tensor_tensor(out=x2, in0=got[k][c], scalar=w_tok[:, c, t:t + 1], in1=x2,
                                       op0=ALU.mult, op1=ALU.add)\
                    .then_inc(S["last_store" if c == 0 else "sum_ready"], 1)


WEIGHT_DMAS = 3 + 16 + 8 + 5
N_FILL = -(-NSLOT // 8)
BOUND = 60.0
ROUTE_SELECTED = 3 + 5 * TOPK + 1 + 2
ROUTE_DONE = ROUTE_SELECTED + 4 + 2 + NE + 6 + 3 + 3 * TOPK + 5


_INS = ["x", "ctx_1024", "mask_BxS2_bf0", "L0_xattn_Wq", "L0_xattn_bq", "L0_xattn_Wk", "L0_xattn_bk", "L0_xattn_Wv",
        "L0_xattn_bv", "L0_xattn_Wo", "L0_xattn_bo", "L0_attn_Wq", "L0_attn_Wk", "L0_attn_Wg1", "L0_attn_Wg2",
        "L0_attn_Wv", "L0_attn_Wg", "L0_attn_bg", "L0_attn_Wo", "L0_ffn_shared_gate", "L0_ffn_shared_up",
        "L0_ffn_shared_down", "L0_ffn_routed_gate", "L0_ffn_routed_up", "L0_ffn_routed_down", "L0_ffn_Wr",
        "L0_ffn_routing_bias"]


def kernel(**inputs):
    import concourse.bacc as bacc
    from concourse.bass_utils import run_bass_kernel_spmd

    nc = bacc.Bacc("TRN2", target_bir_lowering=False, num_devices=1)
    arrays, args = {}, []
    for name in _INS:
        a = np.ascontiguousarray(inputs[name])
        arrays["in_" + name] = a
        args.append(nc.dram_tensor("in_" + name, a.shape, mybir.dt.from_np(a.dtype), kind="ExternalInput").ap())
    arrays["constants"] = constants()
    args.append(nc.dram_tensor("constants", [P, NCONST], F32, kind="ExternalInput").ap())
    args.append(nc.dram_tensor("out", [NB, SQ, D], F32, kind="ExternalOutput").ap())
    build(nc, *args)
    result = run_bass_kernel_spmd(nc, [arrays], core_ids=[0])
    return result.results[0]["out"]
```

```python
from contextlib import ExitStack

import numpy as np
import concourse.bass as bass
from concourse import mybir

ALU = mybir.AluOpType
ACT = mybir.ActivationFunctionType
AX = mybir.AxisListType
F32 = mybir.dt.float32
BF16 = mybir.dt.bfloat16
F16 = mybir.dt.float16
I32 = mybir.dt.int32
U32 = mybir.dt.uint32
U8 = mybir.dt.uint8

P = 128
D = 256
DK = D // P
NB, SQ, SK = 64, 64, 256
NPAIR = NB // 2
H, HC = 16, 16
GK, GV = 8, 16
NCH, CH = 4, 16
GATE_NORM = 16.0
EPS = 1e-5
HID = 704
HT = (HID + P - 1) // P
HR = HID - (HT - 1) * P
HH = HID // 2
NE, TOPK = 7, 2
NTILE = NB * SQ // P
R = 2 * P
NSLOT = (NB * SQ * TOPK + NE * (R - 1)) // R
NT = NTILE * P // R + NSLOT
EW_UP, EW_DOWN = DK * 2 * HID, HT * D
EW = EW_UP + EW_DOWN
EARLY = 2
LAST = 6
FIRST = NTILE * P // R - LAST
MID = FIRST + NSLOT
CHUNKS = [(0, 2 * HID), (2 * HID, 4 * HID), (EW_UP, EW_UP + HT * D // 2), (EW_UP + HT * D // 2, EW)]
NCHUNK = len(CHUNKS)
HALF = HT * R // 2
GROUP = 4
W_SCALE = 2.0 ** 6
V_SCALE = 2.0 ** 4
A_SCALE = 2.0 ** 6
NEG = -(2.0 ** 127)

CONST = {}
_at = 0
for _name, _n in (("ident", P), ("causal", SK), ("cosk", 32), ("sink", 32), ("cosq", HC), ("sinq", HC),
                  ("par", 2), ("head4", 4), ("gla", NCH * CH), ("upper", P), ("eps", 1), ("lnscale", 1),
                  ("one", 1), ("tile", NSLOT), ("desc", NE)):
    CONST[_name] = (_at, _at + _n)
    _at += _n
NCONST = _at


def constants():
    c = np.zeros((P, NCONST), np.float32)
    p = np.arange(P)

    def put(name, a):
        lo, hi = CONST[name]
        c[:, lo:hi] = np.broadcast_to(np.asarray(a, np.float32).reshape(-1, hi - lo), (P, hi - lo))

    inv = (1.0 / 10000.0 ** (np.arange(0, HC, 2, dtype=np.float32) / np.float32(HC))).astype(np.float32)

    def rope(pos, scale):
        t = pos[..., None].astype(np.float32) * inv
        cos = np.repeat(np.cos(t), 2, axis=-1)
        sin = np.repeat(np.sin(t), 2, axis=-1)
        sin[..., ::2] *= -1.0
        return cos * scale, sin * scale

    ck, sk = rope(p[:, None] + P * np.arange(SK // P)[None, :], 1.0)
    cq, sq = rope(p % SQ, HC ** -0.5)
    put("ident", np.eye(P))
    put("causal", np.arange(SK)[None, :] <= (p % SQ)[:, None] + SK - SQ)
    put("cosk", ck.reshape(P, -1))
    put("sink", sk.reshape(P, -1))
    put("cosq", cq)
    put("sinq", sq)
    put("par", (p[:, None] // HC) % 2 == np.arange(2)[None, :])
    put("head4", (p[:, None] // GK) % 4 == np.arange(4)[None, :])
    put("gla", (np.arange(SQ)[None, :] >= (p % SQ)[:, None]) * (A_SCALE / W_SCALE ** 2))
    put("upper", p[:, None] < p[None, :])
    put("eps", np.full((P, 1), EPS))
    put("lnscale", np.full((P, 1), np.log(GK ** -0.5)))
    put("one", np.ones((P, 1)))
    put("tile", np.arange(NSLOT)[None, :])
    put("desc", np.arange(NE, 0, -1)[None, :])
    return c


def bc(ap, axis, n):
    v = ap.unsqueeze(axis)
    shape = list(v.shape)
    shape[axis] = n
    return v.to_broadcast(shape)


class Step:

    def __init__(self, i, off):
        self.i, self.off = i, off

    def n(self, per, add=0):
        return self.i * (2 * per) + (self.off * per + add)

    def next(self, k=1):
        return Step(self.i, self.off + k)

    @property
    def par(self):
        return self.off % 2

    @property
    def half(self):
        return self.i + self.off // 2


def wait(eng, sem, value):
    if isinstance(value, int) and value <= 0:
        return
    eng.wait_ge(sem, value)


def build(nc, x, ctx_in, pad, xWq, xbq, xWk, xbk, xWv, xbv, xWo, xbo, gWq, gWk, gWg1, gWg2, gWv, gWg, gbg, gWo,
          sgate, sup, sdown, rgate, rup, rdown, Wr, rbias, consts_in, out):
    with ExitStack() as stack:
        program(nc, stack, x, ctx_in, pad, xWq, xbq, xWk, xbk, xWv, xbv, xWo, xbo, gWq, gWk, gWg1, gWg2, gWv,
                gWg, gbg, gWo, sgate, sup, sdown, rgate, rup, rdown, Wr, rbias, consts_in, out)


def program(nc, stack, x, ctx_in, pad, xWq, xbq, xWk, xbk, xWv, xbv, xWo, xbo, gWq, gWk, gWg1, gWg2, gWv,
            gWg, gbg, gWo, sgate, sup, sdown, rgate, rup, rdown, Wr, rbias, consts_in, out):
    def sb(name, shape, dt=F32):
        return stack.enter_context(nc.sbuf_tensor(name, shape, dt))

    def sem(name):
        return stack.enter_context(nc.semaphore(name))

    token_in, token_out = (nc.dram_tensor(n, [NTILE * P, D], F32, kind="Internal").ap()
                           for n in ("token_in", "token_out"))
    slot_in, slot_out = (nc.dram_tensor(n, [NSLOT * R, D], F32, kind="Internal").ap()
                         for n in ("slot_in", "slot_out"))

    experts = sb("experts", [P, 1 + NE, EW])
    x2_all = sb("x2_all", [P, NTILE, D])
    cst = sb("cst", [P, NCONST])
    logits = sb("logits", [P, NTILE, NE])
    work = sb("work", [P, 8900])

    arenas = [[experts[:, EARLY:, :].rearrange("p e n -> p (e n)"), 0, (1 + NE - EARLY) * EW],
              [work[:, :], 0, 8900]]

    def place(n, which=None):
        for k, a in enumerate(arenas):
            if (which is None or k == which) and a[1] + n <= a[2]:
                a[1] += n
                return a[0][:, a[1] - n:a[1]]
        raise ValueError("no room")

    def const(name):
        lo, hi = CONST[name]
        return cst[:, lo:hi]

    ident = const("ident")
    w_q = place(DK * D).rearrange("p (k n) -> p k n", k=DK)
    w_kv = place(DK * 2 * D).rearrange("p (k n) -> p k n", k=DK)
    w_o = place(2 * D).rearrange("p (a n) -> p a n", a=2)
    w_gqk = place(DK * D).rearrange("p (k n) -> p k n", k=DK)
    w_g1 = place(DK * 16).rearrange("p (k n) -> p k n", k=DK)

    def halves(k, n):
        return [place(k * n // 2).bitcast(F16).rearrange("p (k n) -> p k n", k=k) for _ in range(2)]

    w_gqk_s, w_g1_s, w_gvg_s = halves(DK, D), halves(DK, 16), halves(DK, 2 * D)
    w_g2 = place(P)
    w_gvg = place(DK * 2 * D).rearrange("p (k n) -> p k n", k=DK)
    w_go = place(DK * D).rearrange("p (k n) -> p k n", k=DK)
    w_r = place(DK * NE).rearrange("p (k n) -> p k n", k=DK)
    b_kv = place(2 * D)
    b_q = place(D)
    b_o = place(D)
    b_g = place(D)
    ident_bf = place(P // 2).bitcast(BF16)
    x_in = [place(D) for _ in range(2)]
    x_res = place(D)
    pad_in = [place(2 * SK // 4).bitcast(U8).rearrange("p (b j) -> p b j", b=2) for _ in range(2)]
    keep = place(2 * SK).rearrange("p (b j) -> p b j", b=2)
    seen = place(2 * SK).rearrange("p (b j) -> p b j", b=2)
    masks = [place(2 * SK // 2).bitcast(BF16).rearrange("p (b j) -> p b j", b=2) for _ in range(2)]
    ctx_rows = place(4 * D).rearrange("p (t n) -> p t n", t=4)
    ctx_t = place(DK * 4 * P).rearrange("p (k n) -> p k n", k=DK)
    kv = place(4 * 2 * D).rearrange("p (t n) -> p t n", t=4)
    k_rot = place(4 * D).rearrange("p (t n) -> p t n", t=4)
    k_swap = place(4 * D).rearrange("p (t n) -> p t n", t=4)
    k_t = place(2 * 2 * SK).rearrange("p (g b j) -> p g b j", g=2, b=2)
    xn = place(D)
    xn_t = place(DK * P).rearrange("p (k n) -> p k n", k=DK)
    q_nat = place(D)
    q_rot = place(D)
    q_swap = place(D)
    q_t = place(2 * 2 * 2 * SQ).rearrange("p (g b a i) -> p g b a i", g=2, b=2, a=2)
    probs = [place(8 * SK).rearrange("p (s j) -> p s j", s=8) for _ in range(2)]
    probs_s = halves(4, 4 * P)
    v_s = [halves(4, D) for _ in range(2)]
    heads_out = [place(8 * HC).rearrange("p (h c) -> p h c", h=8) for _ in range(2)]
    heads_t = place(2 * 2 * SQ).rearrange("p (a b i) -> p a b i", a=2, b=2)
    neg_max = [place(8) for _ in range(2)]
    row_sum = [place(8) for _ in range(2)]
    row_inv = place(8)
    x1 = place(D)
    x1n = place(D)
    x1n_s = halves(DK, P)
    g_v_s = halves(1, D)
    gate = place(D)
    gate_e = place(D)
    gate_i = place(D)
    low_t = place(P)
    kg_abs = place(P)
    kg_min = place(P)
    kg_exp = place(P)
    kg_ln = place(P)
    log_gate = place(P)
    cum = place(2 * SQ).rearrange("p (b i) -> p b i", b=2)
    ref = place(2 * NCH).rearrange("p (b c) -> p b c", b=2)
    q_dec = place(2 * SQ)
    k_dec = place(NCH * 2 * SQ).rearrange("p (c b i) -> p c b i", c=NCH, b=2)
    qs_t = place(2 * SQ)
    q_heads = place(2 * NCH * 4 * CH).rearrange("p (b c h t) -> p b c h t", b=2, c=NCH, h=4)
    k_heads = place(NCH * 2 * SQ).rearrange("p (c b i) -> p c b i", c=NCH, b=2)
    a_t = w_gvg.rearrange("p k n -> p (k n)").rearrange("p (r h c t) -> p r h c t", r=4, h=4, c=NCH)
    a_s = [h.rearrange("p r (h c t) -> p r h c t", h=4, c=NCH) for h in halves(4, 4 * NCH * CH)]
    g_out = place(D)
    g_sq = place(D)
    g_norm = place(D)
    g_norm_t = place(DK * P).rearrange("p (k n) -> p k n", k=DK)
    g_stat = place(4 * H).rearrange("p (k h) -> p k h", k=4)
    x2n = [place(D) for _ in range(2)]
    x2n_s = [w_gqk[:, k, :] for k in range(2)]
    x2n_t = place(DK * P).rearrange("p (k n) -> p k n", k=DK)
    stats = [place(10) for _ in range(3)]

    warena = [0]

    def place2(n):
        warena[0] += n
        assert warena[0] <= 8900
        return work[:, warena[0] - n:warena[0]]

    ident_h = place2(P // 2).bitcast(F16)
    e_rows = place2(2 * D).rearrange("p (a d) -> p a d", a=2)
    e_rows_t = [place2(2 * DK * R // 2).bitcast(F16).rearrange("p (m n) -> p m n", n=R) for _ in range(2)]
    e_silu = place2(HALF)
    e_hid = place2(HALF)
    e_hid_s = [place2(HT * R // 2).bitcast(F16).rearrange("p (c n) -> p c n", c=HT) for _ in range(2)]
    e_y = place2(2 * D).rearrange("p (a d) -> p a d", a=2)
    stage_rows = [place2(D) for _ in range(2)]
    w_raw = [place2(2 * HID) for _ in range(2)]
    w_tok = place2(TOPK * NTILE).rearrange("p (c t) -> p c t", c=TOPK)
    slot_i = place2(TOPK * NTILE).bitcast(U32).rearrange("p (c t) -> p c t", c=TOPK)
    tile_e = place2(NT).bitcast(I32)
    experts_h = experts[:, :, :].bitcast(F16)
    results = experts[:, 1:, :].rearrange("p e n -> p (e n)")[:, 0:3 * NTILE * D]\
        .rearrange("p (c t d) -> p c t d", c=3, t=NTILE)
    rt = [0]

    def place3(n):
        rt[0] += n
        assert rt[0] <= EW
        return experts[:, NE, rt[0] - n:rt[0]]

    L = NTILE * NE
    te = lambda a: a.rearrange("p (t e) -> p t e", e=NE)
    et = lambda a: a.rearrange("p (e t) -> p e t", e=NE)
    r_z, r_e, r_p, r_c, r_eq = (te(place3(L)) for _ in range(5))
    r_oh = [te(place3(L)) for _ in range(TOPK)]
    r_sel = te(place3(L))
    r_in, r_tot = te(place3(L)), te(place3(L))
    r_cum, r_pos = te(place3(L)), te(place3(L))
    r_m = place3(6 * NTILE).rearrange("p (k t) -> p k t", k=6)
    r_n = place3(6 * NE).rearrange("p (k e) -> p k e", k=6)
    r_ni = place3(NE).bitcast(I32)
    r_t = place3(NSLOT * NE).rearrange("p (j e) -> p j e", e=NE)
    r_tf = place3(NSLOT)
    r_bias = place3(NE)
    r_ones = place3(P)

    ps = stack.enter_context(nc.psum_tensor("ps", [P, 8, 512], F32))
    ps_flat = ps[:, :, :].rearrange("p b n -> p (b n)")
    bank_ta, bank_tb, bank_ma, bank_mb = (ps[:, k, :] for k in range(4, 8))

    def probs_bank(b, r):
        return ((bank_ma, bank_mb), (bank_ta, bank_tb))[b][r % 2]

    S = {}
    for name in """
        consts_loaded weights_loaded waits_met fill_ready slots_filled biasr_loaded ctx_loaded ctx_turned
        ctx_t_ready kv_done kv_ready k_prod_ready k_swap_ready k_rot_ready k_turned k_t_ready x_stat_ready
        x_log_ready x_rstd_ready xn_ready xn_turned xn_t_ready q_done q_nat_ready q_prod_ready q_swap_ready
        q_rot_ready q_turned q_t_ready pad_read seen_ready masks_ready x_res_ready x_bn scores_done max_ready
        exp_done probs_turned probs_hi_ready probs_lo_ready v_split g_v_hi_ready av_done inv_ready av_ready
        heads_turned heads_t_ready proj_done x1_ready x1_bn x1_stat_ready x1_log_ready x1_rstd_ready x1n_ready
        x1n_turned x1n_hi_ready x1n_lo_ready vg_done g_v_ready gate_ready qkl_done low_t_ready kg_done
        kg_abs_ready kg_min_ready gate_inv gate_silu kg_exp_ready kg_ln_ready ref_zero dec_ready dec_k_ready
        dec_min dec_exp_q dec_exp_k qs_ready q_heads_ready k_heads_ready a_done a_ready go_done go_ready gs_var
        gs_log gs_rstd gn_scaled gn_ready gn_turned gn_t_ready gproj_done x2_ready x2_bn x2_stat_ready
        x2_log_ready x2_rstd_ready x2n_ready x2n_turned x2n_t_ready logits_done logits_ready x2n_split
        tail_zero_raw shared_loaded shared_hi shared_lo chunk_hi_ready chunk_lo_ready gate_done hid_hi_ready
        hid_lo_ready ident_h_ready route_step route_exp route_mm table_ready rows_turned rows_t_ready up_done
        silu_ready hid_ready down_done y_ready a_split gla_hi_ready gla_lo_ready sum_ready gs_step decay_step
        gate_step sum_step last_store first_shared_loaded rows_loaded y_stored
        last_shared_loaded
    """.split():
        S[name] = sem(name)
    x_loaded = [sem(f"x_loaded{k}") for k in range(2)]
    pad_loaded = [sem(f"pad_loaded{k}") for k in range(2)]
    x2n_stored = [sem(f"x2n_stored{k}") for k in range(2)]
    staged = [sem(f"staged{k}") for k in range(2)]
    scattered = [sem(f"scattered{k}") for k in range(2)]
    chunk_loaded = [sem(f"chunk_loaded{k}") for k in range(2)]
    group_loaded = [sem(f"group_loaded{k}") for k in range(NTILE // GROUP)]

    pairs = x.rearrange("(q b) s d -> q (b s) d", b=2)
    ctx_pairs = ctx_in.rearrange("(q b) (t p) d -> q p (b t) d", b=2, p=P)
    pad_pairs = pad.rearrange("(q b) j -> q (b j)", b=2)
    out_tiles = out.rearrange("(q b) s d -> q (b s) d", b=2)
    token_in_t, token_out_t, slot_in_t = (a.rearrange("(t p) d -> t p d", p=P) for a in
                                          (token_in, token_out, slot_in))
    tokens, token_results, slots, slot_results = (a.rearrange("(t a p) d -> t p a d", a=2, p=P) for a in
                                                  (token_in, token_out, slot_in, slot_out))

    def over_pairs(eng, first, body, last, third=None):
        first(Step(0, 0))
        body(Step(0, 1))
        (third or body)(Step(0, 2))
        with eng.Fori(1, (NPAIR - 2) // 2) as i:
            body(Step(i, 1))
            body(Step(i, 2))
        last(Step(0, NPAIR - 1))

    block = stack.enter_context(nc.Block())

    def apart(eng):
        eng.sem_inc(S["waits_met"], 1)

    @block.sync
    def _(sp):
        sp.dma_start(cst[:, :], consts_in).then_inc(S["consts_loaded"], 16)

        def load_x(j):
            wait(sp, S["x_res_ready"], j.n(1, -1))
            wait(sp, S["xn_ready"], j.n(1, -1))
            apart(sp)
            sp.dma_start(x_in[j.par], pairs[j.n(1)]).then_inc(x_loaded[j.par], 16)
            wait(sp, S["pad_read"], j.n(1, -1))
            apart(sp)
            sp.dma_start(pad_in[j.par].rearrange("p b j -> p (b j)"),
                         pad_pairs[j.n(1)].partition_broadcast(P)).then_inc(pad_loaded[j.par], 16)

        def load_ctx(j):
            wait(sp, S["ctx_turned"], j.n(2))
            apart(sp)
            sp.dma_start(ctx_rows, ctx_pairs[j.n(1)]).then_inc(S["ctx_loaded"], 16)

        def store_x2n(g):
            wait(sp, S["x2n_split"], g.n(2, 2))
            apart(sp)
            sp.dma_start(token_in_t[g.n(1)], x2n_s[g.par]).then_inc(x2n_stored[g.par], 16)

        load_ctx(Step(0, 0))
        load_x(Step(0, 0))
        load_x(Step(0, 1))
        wl = S["weights_loaded"]

        def kmaj(w):
            return w.rearrange("(k p) n -> p k n", p=P)

        count = [0]

        def wload(dst, src):
            sp.dma_start(dst, src).then_inc(wl, 16)
            count[0] += 1

        wload(w_kv[:, :, 0:D], kmaj(xWk))
        wload(w_kv[:, :, D:2 * D], kmaj(xWv))
        wload(w_q, kmaj(xWq))
        for hp in range(8):
            for a in range(2):
                row = (2 * hp + a) * HC
                wload(w_o[hp * HC:(hp + 1) * HC, a, :], xWo[row:row + HC, :])
        wload(w_gqk[:, :, 0:P], kmaj(gWq))
        wload(w_gqk[:, :, P:2 * P], kmaj(gWk))
        wload(w_g1, kmaj(gWg1))
        wload(w_g2[0:16, :], gWg2)
        wload(w_gvg[:, :, 0:D], kmaj(gWv))
        wload(w_gvg[:, :, D:2 * D], kmaj(gWg))
        wload(w_go, kmaj(gWo))
        wload(w_r, kmaj(Wr))
        wload(b_kv[:, 0:D], xbk.partition_broadcast(P))
        wload(b_kv[:, D:2 * D], xbv.partition_broadcast(P))
        wload(b_q, xbq.partition_broadcast(P))
        wload(b_o, xbo.partition_broadcast(P))
        wload(b_g, gbg.partition_broadcast(P))
        assert count[0] == WEIGHT_DMAS
        load_ctx(Step(0, 1))

        def step(p, nxt2=True):
            if nxt2:
                load_x(p.next(2))
                load_ctx(p.next(2))
            store_x2n(p.next(-1))

        def first(p):
            load_x(p.next(2))
            load_ctx(p.next(2))

        first(Step(0, 0))
        step(Step(0, 1))
        step(Step(0, 2))
        with sp.Fori(1, (NPAIR - 4) // 2) as i:
            step(Step(i, 1))
            step(Step(i, 2))
        step(Step(0, NPAIR - 3))
        step(Step(0, NPAIR - 2), False)
        step(Step(0, NPAIR - 1), False)
        store_x2n(Step(0, NPAIR - 1))

        sp.wait_ge(x2n_stored[0], 16 * NPAIR // 2)
        sp.wait_ge(x2n_stored[1], 16 * NPAIR // 2)
        sp.wait_ge(S["logits_ready"], NPAIR)

        def load_rows(t, rows):
            wait(sp, S["rows_turned"], t)
            apart(sp)
            sp.dma_start(e_rows, rows).then_inc(S["rows_loaded"], 16)

        def stage(t):
            if t >= 2:
                sp.wait_ge(scattered[t % 2], 32 * (t // 2))
            sp.dma_start(stage_rows[t % 2], token_in_t[t]).then_inc(staged[t % 2], 16)

        def store_y(t, rows):
            wait(sp, S["y_ready"], t + 1)
            apart(sp)
            sp.dma_start(rows, e_y).then_inc(S["y_stored"], 16)

        def load_chunk(n):
            wait(sp, S["chunk_lo_ready"], n - 1)
            e, c = n // NCHUNK, n % NCHUNK
            raw, done = w_raw[n % 2], chunk_loaded[n % 2]
            if c < DK:
                sp.dma_start(raw[:, 0:HID], rgate[e, c * P:(c + 1) * P, :]).then_inc(done, 16)
                sp.dma_start(raw[:, HID:2 * HID], rup[e, c * P:(c + 1) * P, :]).then_inc(done, 16)
            else:
                k = HT // 2
                lo, hi = (c - DK) * k * P, min((c - DK + 1) * k * P, HID)
                full = (hi - lo) // P
                sp.dma_start(raw[:, 0:full * D].rearrange("p (c n) -> p c n", n=D),
                             rdown[e, lo:lo + full * P, :].rearrange("(c p) n -> p c n", p=P)).then_inc(done, 16)
                if full < k:
                    sp.dma_start(raw[0:HR, full * D:k * D], rdown[e, lo + full * P:hi, :]).then_inc(done, 16)

        sp.dma_start(r_bias, rbias.partition_broadcast(P)).then_inc(S["biasr_loaded"], 16)
        load_rows(0, tokens[0])
        sp.wait_ge(S["tail_zero_raw"], 1)
        load_chunk(0)
        load_chunk(1)
        staged_tiles = 0
        for t in range(1, FIRST):
            load_rows(t, tokens[t])
            if t >= 3:
                store_y(t - 3, token_results[t - 3])
            for n in chunks_of(t - 2):
                if n + 2 < NCHUNK * NE:
                    load_chunk(n + 2)
            while t >= 3 and staged_tiles < NTILE * (t - 2) // (FIRST - 3):
                stage(staged_tiles)
                staged_tiles += 1
        assert FIRST - 3 >= SPLIT_TILES - 1 and staged_tiles == NTILE
        for k in range(2):
            sp.wait_ge(scattered[k], 32 * (NTILE // 2))
        for t in range(FIRST, FIRST + 3):
            load_rows(t, slots[t - FIRST])
            store_y(t - 3, token_results[t - 3])
        with sp.Fori(FIRST + 3, MID) as t:
            load_rows(t, slots[t - FIRST])
            store_y(t - 3, slot_results[t - (FIRST + 3)])
        for t in range(MID, NT + 3):
            if t < NT:
                load_rows(t, tokens[t - NSLOT])
            store_y(t - 3, slot_results[t - 3 - FIRST] if t - 3 < MID else token_results[t - 3 - NSLOT])

        sp.wait_ge(S["y_stored"], 16 * NT)
        sp.dma_start(results[:, 2, 2 * FIRST:, :], token_out_t[2 * FIRST:].rearrange("t p d -> p t d"))\
            .then_inc(S["last_shared_loaded"], 16)
        for m in range(NTILE // GROUP):
            tiles = slice(m * GROUP, (m + 1) * GROUP)
            sp.wait_ge(S["sum_ready"], m + 1)
            sp.dma_start(out_tiles[tiles].rearrange("t p d -> p t d"), x2_all[:, tiles, :])\
                .then_inc(S["last_store"], 16)
        sp.wait_ge(S["last_store"], 16 * NTILE // GROUP)

    @block.gpsimd
    def _(pool):
        zeros = experts[:, 0, 0:8 * D].rearrange("p (t d) -> p t d", t=8)
        nc.gpsimd.memset(zeros, 0.0).then_inc(S["fill_ready"], 1)
        nc.gpsimd.memset(experts[:, 1, EW - D:], 0.0).then_inc(S["fill_ready"], 1)
        pool.wait_ge(S["consts_loaded"], 16)
        nc.gpsimd.tensor_copy(ident_bf, ident).then_inc(S["fill_ready"], 1)
        pool.wait_ge(S["fill_ready"], 3)

        def fill_slots():
            for t in range(0, 2 * NSLOT, 8):
                m = min(8, 2 * NSLOT - t)
                pool.dma_start(slot_in_t[t:t + m].rearrange("t p d -> p t d"), zeros[:, 0:m, :])\
                    .then_inc(S["slots_filled"], 16)

        def load_shared():
            w, s = experts[:, 1, :], S["shared_loaded"]
            up = w[:, 0:EW_UP].rearrange("p (k c n) -> p k c n", k=DK, c=2)
            down = w[:, EW_UP:].rearrange("p (c n) -> p c n", c=HT)
            main = (HT - 1) * P
            pool.dma_start(up[:, :, 0, :], sgate.rearrange("(k p) n -> p k n", p=P)).then_inc(s, 16)
            pool.dma_start(up[:, :, 1, :], sup.rearrange("(k p) n -> p k n", p=P)).then_inc(s, 16)
            pool.dma_start(down[:, 0:HT - 1, :], sdown[0:main, :].rearrange("(c p) n -> p c n", p=P)).then_inc(s, 16)
            pool.dma_start(down[0:HR, HT - 1, :], sdown[main:, :]).then_inc(s, 16)

        def split_x2(g):
            wait(pool, S["x2n_ready"], g.n(1, 1))
            wait(pool, x2n_stored[g.par], g.half * 16)
            apart(pool)
            both = x2n_s[g.par].bitcast(F16)
            nc.gpsimd.tensor_scalar(both[:, 0:D], x2n[g.par], 1.0, None, ALU.mult).then_inc(S["x2n_split"], 1)
            wait(pool, S["x2n_split"], g.n(2, 1))
            nc.gpsimd.tensor_tensor(both[:, D:2 * D], x2n[g.par], both[:, 0:D], ALU.subtract)\
                .then_inc(S["x2n_split"], 1)

        def masks_of(j):
            wait(pool, pad_loaded[j.par], j.half * 16 + 16)
            wait(pool, S["scores_done"], j.n(2, -2))
            wait(pool, S["masks_ready"], j.n(1))
            apart(pool)
            nc.gpsimd.tensor_scalar(keep, pad_in[j.par], -1.0, 1.0, ALU.mult, ALU.add).then_inc(S["pad_read"], 1)
            wait(pool, S["pad_read"], j.n(1, 1))
            nc.gpsimd.tensor_tensor(seen, keep, bc(const("causal"), 1, 2), ALU.mult).then_inc(S["seen_ready"], 1)
            wait(pool, S["seen_ready"], j.n(1, 1))
            apart(pool)
            nc.gpsimd.tensor_scalar(masks[j.par], seen, -NEG, NEG, ALU.mult, ALU.add).then_inc(S["masks_ready"], 1)

        def rope_k(j):
            kb = kv
            wait(pool, S["kv_ready"], j.n(4, 4))
            wait(pool, S["k_rot_ready"], j.n(1))
            sin = const("sink").rearrange("p (t i e) -> p t i e", t=2, e=2)
            for b in range(2):
                for e in range(2):
                    for t in range(2):
                        src = kb[:, 2 * b + t, 0:D].rearrange("p (h i e) -> p h i e", h=H, e=2)
                        dst = k_swap[:, 2 * b + t, :].rearrange("p (h i e) -> p h i e", h=H, e=2)
                        ins = nc.gpsimd.tensor_tensor(dst[:, :, :, e], src[:, :, :, 1 - e],
                                                      bc(sin[:, t, :, e], 1, H), ALU.mult)
            ins.then_inc(S["k_swap_ready"], 1)

        def split_v(j):
            wait(pool, S["av_done"], j.n(2, -2))
            high, low = v_s[j.par]
            values = kv[:, :, D:2 * D]
            apart(pool)
            nc.gpsimd.tensor_scalar(high, values, 1.0, None, ALU.mult).then_inc(S["v_split"], 1)
            wait(pool, S["v_split"], j.n(2, 1))
            nc.gpsimd.tensor_tensor(low, values, high, ALU.subtract).then_inc(S["v_split"], 1)

        def split_a(g):
            wait(pool, S["a_ready"], g.n(4, 4))
            apart(pool)
            nc.gpsimd.tensor_scalar(a_s[0], a_t, 1.0, None, ALU.mult).then_inc(S["a_split"], 1)
            wait(pool, S["a_split"], g.n(2, 1))
            nc.gpsimd.tensor_tensor(a_s[1], a_t, a_s[0], ALU.subtract).then_inc(S["a_split"], 1)

        def rope_q(j):
            wait(pool, S["q_nat_ready"], j.n(1, 1))
            sin = const("sinq").rearrange("p (i e) -> p i e", e=2)
            src = q_nat.rearrange("p (h i e) -> p h i e", h=H, e=2)
            dst = q_swap.rearrange("p (h i e) -> p h i e", h=H, e=2)
            for e in range(2):
                ins = nc.gpsimd.tensor_tensor(dst[:, :, :, e], src[:, :, :, 1 - e], bc(sin[:, :, e], 1, H), ALU.mult)
            ins.then_inc(S["q_swap_ready"], 1)

        def residual(p):
            wait(pool, x_loaded[p.par], p.half * 16 + 16)
            wait(pool, S["x1_ready"], p.n(1))
            nc.gpsimd.tensor_tensor(x_res, x_in[p.par], b_o, ALU.add).then_inc(S["x_res_ready"], 1)

        def step(p, nxt=True, gla=True):
            residual(p)
            if nxt:
                masks_of(p.next())
                rope_k(p.next())
            if gla:
                split_a(p.next(-1))
            if nxt:
                split_v(p.next())
                rope_q(p.next())
            if gla:
                split_x2(p.next(-1))

        pool.wait_ge(S["weights_loaded"], 16 * WEIGHT_DMAS)
        masks_of(Step(0, 0))
        rope_k(Step(0, 0))
        split_v(Step(0, 0))
        rope_q(Step(0, 0))

        def first(p):
            step(p, gla=False)
            load_shared()
            fill_slots()

        over_pairs(pool, first, step, lambda p: step(p, False))
        split_a(Step(0, NPAIR - 1))
        split_x2(Step(0, NPAIR - 1))

        pool.wait_ge(S["slots_filled"], 16 * N_FILL)
        pool.wait_ge(S["table_ready"], 1)
        for t in range(NTILE):
            pool.wait_ge(staged[t % 2], 16 * (t // 2 + 1))
            for c in range(TOPK):
                pool.indirect_dma_start(
                    out=slot_in, out_offset=bass.IndirectOffsetOnAxis(ap=slot_i[:, c, t:t + 1], axis=0),
                    in_=stage_rows[t % 2], in_offset=None).then_inc(scattered[t % 2], 16)
        pool.wait_ge(S["y_stored"], 16 * MID)
        pool.wait_ge(S["down_done"], MID)
        pool.dma_start(results[:, 2, 0:2 * FIRST, :], token_out_t[0:2 * FIRST].rearrange("t p d -> p t d"))\
            .then_inc(S["first_shared_loaded"], 16)
        for m in range(NTILE // GROUP):
            for t in range(m * GROUP, (m + 1) * GROUP):
                for c in range(TOPK):
                    pool.indirect_dma_start(
                        out=results[:, c, t, :], out_offset=None, in_=slot_out,
                        in_offset=bass.IndirectOffsetOnAxis(ap=slot_i[:, c, t:t + 1], axis=0))\
                        .then_inc(group_loaded[m], 16)

    @block.tensor
    def _(pe):
        def turn(bank, src, done):
            n = len(src)
            for k, a in enumerate(src):
                ins = pe.transpose(bank[:, k * P:(k + 1) * P], a, ident)
            ins.then_inc(done, 1)

        def product(bank, lhs, rhs, done, last=True):
            for k in range(len(lhs)):
                ins = pe.matmul(bank, lhs[k], rhs[k], start=(k == 0), stop=(k == len(lhs) - 1))
            if done is not None:
                ins.then_inc(done, 1)

        def split_product(bank, lhs, rhs, done, last=True):
            for k in range(len(lhs[0])):
                for a, b in ((0, 0), (0, 1), (1, 0)):
                    ins = pe.matmul(bank, lhs[a][k], rhs[b][k], start=(k == 0 and a + b == 0),
                                    stop=(k == len(lhs[0]) - 1 and a == 1))
            if done is not None:
                ins.then_inc(done, 1)

        def blocks(halves, lo=None, hi=None):
            return [[h[:, k, lo:hi] for k in range(h.shape[1])] for h in halves]

        def turn_ctx(j):
            wait(pe, S["ctx_loaded"], j.n(16, 16))
            for k, bank in enumerate((bank_ma, bank_mb)):
                turn(bank, [ctx_rows[:, t, k * P:(k + 1) * P] for t in range(4)], S["ctx_turned"])

        def project_kv(j, t):
            wait(pe, S["ctx_t_ready"], j.n(2, 2))
            if t >= 2:
                wait(pe, S["kv_ready"], j.n(4, t - 1))
            bank = (bank_ma, bank_mb)[t % 2]
            product(bank, [ctx_t[:, k, t * P:(t + 1) * P] for k in range(DK)],
                    [w_kv[:, k, :] for k in range(DK)], S["kv_done"])

        def turn_k(j):
            wait(pe, S["k_rot_ready"], j.n(1, 1))
            for g, bank in enumerate((bank_tb, bank_mb)):
                turn(bank, [k_rot[:, t, g * P:(g + 1) * P] for t in range(4)], S["k_turned"])

        def turn_xn(j):
            wait(pe, S["xn_ready"], j.n(1, 1))
            turn(bank_ta, [xn[:, k * P:(k + 1) * P] for k in range(DK)], S["xn_turned"])

        def project_q(j):
            wait(pe, S["xn_t_ready"], j.n(1, 1))
            product(bank_ta[:, 0:D], [xn_t[:, k, :] for k in range(DK)], [w_q[:, k, :] for k in range(DK)],
                    S["q_done"])

        def turn_q(j):
            wait(pe, S["q_rot_ready"], j.n(1, 1))
            turn(bank_mb, [q_rot[:, g * P:(g + 1) * P] for g in range(2)], S["q_turned"])

        def scores(p, b):
            wait(pe, S["masks_ready"], p.n(1, 1))
            wait(pe, S["k_t_ready"], p.n(2, 2))
            wait(pe, S["q_t_ready"], p.n(1, 1))
            for r in range(4):
                pe.matmul(ps[:, r, :].rearrange("p (g j) -> p g j", g=2), ident_bf, bc(masks[p.par][:, b, :], 1, 2),
                          start=True, stop=False)
            for g in range(2):
                for r in range(4):
                    q = slice(32 * r, 32 * r + 32)
                    ins = pe.matmul(ps[:, r, g * SK:(g + 1) * SK], q_t[q, g, b, :, :].rearrange("p a i -> p (a i)"),
                                    k_t[q, g, b, :], start=False, stop=(g == 1))
            ins.then_inc(S["scores_done"], 1)

        def turn_probs(p, b):
            for r in range(4):
                wait(pe, S["exp_done"], p.n(16, 8 * b + 2 * r + 2))
                if r >= 2:
                    wait(pe, S["probs_lo_ready"], p.n(8, 4 * b + r - 1))
                turn(probs_bank(b, r),
                     [probs[b][:, 2 * r + g, t * P:(t + 1) * P] for g in range(2) for t in range(2)],
                     S["probs_turned"])

        def weigh_values(p, b, bank):
            wait(pe, S["probs_lo_ready"], p.n(8, 4 * b + 4))
            wait(pe, S["v_split"], p.n(2, 2))
            for hp in range(8):
                g, r = hp // 4, hp % 4
                split_product(bank[:, hp * 32:hp * 32 + 32],
                              [[h[:, r, (2 * g + t) * P:(2 * g + t + 1) * P] for t in range(2)] for h in probs_s],
                              [[h[:, 2 * b + t, hp * 32:hp * 32 + 32] for t in range(2)] for h in v_s[p.par]],
                              S["av_done"] if hp == 7 else None)

        def turn_heads(p, b, bank):
            wait(pe, S["av_ready"], p.n(2, b + 1))
            turn(bank, [heads_out[b].rearrange("p h c -> p (h c)")], S["heads_turned"])

        def project_out(p):
            wait(pe, S["heads_t_ready"], p.n(2, 2))
            product(bank_mb[:, 0:D], [heads_t[:, a, :, :].rearrange("p b i -> p (b i)") for a in range(2)],
                    [w_o[:, a, :] for a in range(2)], S["proj_done"])

        def g_turn_x(g):
            wait(pe, S["x1n_ready"], g.n(1, 1))
            turn(bank_ta, [x1n[:, k * P:(k + 1) * P] for k in range(DK)], S["x1n_turned"])

        def g_project(g):
            wait(pe, S["x1n_lo_ready"], g.n(1, 1))
            wait(pe, S["gla_lo_ready"], 3)
            split_product(bank_tb, blocks(x1n_s), blocks(w_gvg_s), S["vg_done"])
            for c in range(2):
                split_product(bank_ta[:, c * P:(c + 1) * P], blocks(w_gqk_s, c * P, (c + 1) * P), blocks(x1n_s), None)
            split_product(bank_ta[0:16, 2 * P:3 * P], blocks(w_g1_s), blocks(x1n_s), S["qkl_done"])

        def g_gate(g):
            wait(pe, S["low_t_ready"], g.n(1, 1))
            wait(pe, S["g_v_ready"], g.n(1, 1))
            product(bank_tb[:, 0:P], [w_g2[0:16, :]], [low_t[0:16, :]], S["kg_done"])

        def g_scores(g):
            wait(pe, S["k_heads_ready"], g.n(1, 1))
            wait(pe, S["q_heads_ready"], g.n(1, 1))
            for r in range(4):
                q = slice(32 * r, 32 * r + 32)
                for b in range(2):
                    for c in range(NCH):
                        ins = pe.matmul(ps[SQ * b:SQ * b + SQ, r, c * 64:(c + 1) * 64], k_heads[q, c, b, :],
                                        q_heads[q, b, c, :, :].rearrange("p h t -> p (h t)"), start=True, stop=True)
            ins.then_inc(S["a_done"], 1)

        def g_values(g):
            wait(pe, S["a_split"], g.n(2, 2))
            wait(pe, S["g_v_ready"], g.n(1, 1))
            apart(pe)
            for b in range(2):
                rows = slice(SQ * b, SQ * b + SQ)
                for h in range(H):
                    split_product(bank_ma[rows, h * GV:(h + 1) * GV],
                                  [[a[rows, h // 4, h % 4, :, :].rearrange("p c t -> p (c t)")] for a in a_s],
                                  [[a[rows, 0, h * GV:(h + 1) * GV]] for a in g_v_s],
                                  S["go_done"] if (b, h) == (1, H - 1) else None)

        def g_turn_out(g):
            wait(pe, S["gn_ready"], g.n(1, 1))
            turn(bank_ma, [g_norm[:, k * P:(k + 1) * P] for k in range(DK)], S["gn_turned"])

        def g_project_out(g):
            wait(pe, S["gn_t_ready"], g.n(1, 1))
            product(bank_mb[:, 0:D], [g_norm_t[:, k, :] for k in range(DK)], [w_go[:, k, :] for k in range(DK)],
                    S["gproj_done"])

        def g_turn_x2(g):
            wait(pe, S["x2n_ready"], g.n(1, 1))
            turn(bank_ta, [x2n[g.par][:, k * P:(k + 1) * P] for k in range(DK)], S["x2n_turned"])

        def g_logits(g):
            wait(pe, S["x2n_t_ready"], g.n(1, 1))
            product(bank_ma[:, 0:NE], [x2n_t[:, k, :] for k in range(DK)], [w_r[:, k, :] for k in range(DK)],
                    S["logits_done"])

        def step(p, nxt=True, gla=True, att=True):
            g, j = p.next(-1), p.next()
            if att:
                wait(pe, S["exp_done"], p.n(16))
                scores(p, 0)
            if gla:
                wait(pe, S["probs_lo_ready"], p.n(8))
                wait(pe, S["x2n_t_ready"], g.n(1))
                g_turn_x(g)
            if nxt:
                wait(pe, S["av_ready"], p.n(2))
                wait(pe, S["logits_ready"], g.n(1))
                wait(pe, S["x1_ready"], p.n(1))
                turn_ctx(j)
            if gla:
                wait(pe, S["heads_t_ready"], p.n(2))
                g_project(g)
            if nxt:
                project_kv(j, 0)
            if gla:
                g_gate(g)
            if nxt:
                for t in range(1, 4):
                    project_kv(j, t)
            if att:
                wait(pe, S["kv_ready"], (j if nxt else p).n(4, 4))
                wait(pe, S["av_ready"], p.n(2))
                wait(pe, S["x1_ready"], p.n(1))
                wait(pe, S["q_t_ready"], p.n(1, 1))
                if gla:
                    wait(pe, S["logits_ready"], g.n(1))
                turn_probs(p, 0)
            if gla:
                wait(pe, S["exp_done"], p.n(16, 8 if att else 0))
                g_scores(g)
            if nxt:
                wait(pe, S["k_heads_ready"], p.n(1))
                wait(pe, S["q_nat_ready"], p.n(1, 1))
                turn_xn(j)
            if att:
                weigh_values(p, 0, bank_mb)
                wait(pe, S["exp_done"], p.n(16, 8))
                wait(pe, S["a_ready"], p.n(4))
                scores(p, 1)
            if gla:
                if not att:
                    wait(pe, S["logits_ready"], g.n(1))
                    wait(pe, S["av_ready"], p.n(2))
                g_values(g)
            if att:
                wait(pe, S["go_ready"], p.n(1))
                turn_heads(p, 0, bank_ma)
            if nxt:
                wait(pe, S["av_ready"], p.n(2, 1))
                wait(pe, S["kg_abs_ready"], p.n(1))
                turn_k(j)
                project_q(j)
            if att:
                if nxt:
                    wait(pe, S["q_nat_ready"], j.n(1, 1))
                    wait(pe, S["k_t_ready"], j.n(2, 1))
                else:
                    wait(pe, S["k_heads_ready"], p.n(1))
                    wait(pe, S["kg_abs_ready"], p.n(1))
                turn_probs(p, 1)
            if gla:
                if att:
                    wait(pe, S["heads_t_ready"], p.n(2, 1))
                g_turn_out(g)
                if nxt:
                    wait(pe, S["k_t_ready"], j.n(2, 2))
                elif att:
                    wait(pe, S["av_ready"], p.n(2, 1))
                else:
                    wait(pe, S["x1_ready"], p.n(1))
                g_project_out(g)
            if att:
                wait(pe, S["gn_t_ready"], p.n(1))
                wait(pe, S["heads_t_ready"], p.n(2, 1))
                weigh_values(p, 1, bank_ma)
            if nxt:
                wait(pe, S["x2_ready"], p.n(1))
                wait(pe, S["k_t_ready"], j.n(2, 2))
                turn_q(j)
            if att:
                turn_heads(p, 1, bank_tb)
            if gla:
                if att:
                    wait(pe, S["probs_lo_ready"], p.n(8, 8))
                g_turn_x2(g)
            if att:
                if nxt:
                    wait(pe, S["q_t_ready"], j.n(1, 1))
                wait(pe, S["x2_ready"], p.n(1))
                project_out(p)
            if gla:
                if att:
                    wait(pe, S["av_ready"], p.n(2, 2))
                g_logits(g)

        pe.wait_ge(S["consts_loaded"], 16)
        pe.wait_ge(S["weights_loaded"], 16 * WEIGHT_DMAS)
        pe.wait_ge(S["fill_ready"], 3)
        zero = Step(0, 0)
        turn_ctx(zero)
        for t in range(4):
            project_kv(zero, t)
        turn_xn(zero)
        pe.wait_ge(S["kv_ready"], 4)
        turn_k(zero)
        project_q(zero)
        pe.wait_ge(S["k_t_ready"], 2)
        turn_q(zero)
        over_pairs(pe, lambda p: step(p, gla=False), step, lambda p: step(p, nxt=False))
        step(Step(0, NPAIR), nxt=False, att=False)

        pe.wait_ge(S["logits_ready"], NPAIR)
        pe.wait_ge(S["route_step"], ROUTE_SELECTED)
        sel = r_sel.rearrange("p t e -> p (t e)")
        pe.matmul(bank_ma[:, 0:L], const("upper"), sel, start=True, stop=True).then_inc(S["route_mm"], 1)
        pe.matmul(bank_mb[:, 0:L], r_ones, sel, start=True, stop=True).then_inc(S["route_mm"], 1)

        turned = ps[:, 0, :].bitcast(F16)

        def turn_rows(t):
            wait(pe, S["rows_loaded"], t * 16 + 16)
            wait(pe, S["rows_t_ready"], t)
            rows = e_rows.rearrange("p a d -> p (a d)").bitcast(F16)
            for m in range(2 * DK):
                for a in range(2):
                    ins = pe.transpose(turned[:, m * R + a * P:m * R + (a + 1) * P],
                                       rows[:, (a * 2 * DK + m) * P:(a * 2 * DK + m + 1) * P], ident_h)
            ins.then_inc(S["rows_turned"], 1)

        def up(t, k, e, half):
            wait(pe, S["rows_t_ready"], t + 1)
            for part, (free, done) in enumerate((("silu_ready", "gate_done"), ("hid_ready", "up_done"))):
                wait(pe, S[free], t * 2 + half)
                for c in range(half * HT // 2, (half + 1) * HT // 2):
                    for kk in range(DK):
                        for a, b in ((0, 0), (0, 1), (1, 0)):
                            at = a * EW + (2 * kk + part) * HID + c * P
                            ins = pe.matmul(ps[:, 1 + 3 * part + c // 2, (c % 2) * R:(c % 2 + 1) * R],
                                            experts_h[:, e, at:at + P], e_rows_t[k][:, b * DK + kk, :],
                                            start=(kk == 0 and a + b == 0), stop=(kk == DK - 1 and a == 1))
                ins.then_inc(S[done], 1)

        def down(t, e):
            wait(pe, S["hid_lo_ready"], t * 2 + 2)
            wait(pe, S["y_ready"], t)
            for r in range(2):
                for c in range(HT):
                    n = P if c < HT - 1 else HR
                    for a, b in ((0, 0), (0, 1), (1, 0)):
                        at = b * EW + EW_UP + c * D
                        ins = pe.matmul(ps[:, 7, r * D:(r + 1) * D], e_hid_s[a][0:n, c, r * P:(r + 1) * P],
                                        experts_h[0:n, e, at:at + D],
                                        start=(c == 0 and a + b == 0), stop=(c == HT - 1 and a == 1))
            ins.then_inc(S["down_done"], 1)

        pe.wait_ge(S["shared_lo"], 1)
        pe.wait_ge(S["ident_h_ready"], 1)
        pe.wait_ge(S["a_ready"], 4 * NPAIR)
        pe.wait_ge(S["x2n_t_ready"], NPAIR)
        pe.wait_ge(S["gn_t_ready"], NPAIR)
        turn_rows(0)
        up(0, 0, 0, 0)
        pe.wait_ge(S["route_step"], ROUTE_DONE)
        turn_rows(1)
        up(0, 0, 0, 1)

        def tile(t, k, e, e_before):
            up(t, k, e, 0)
            down(t - 1, e_before)
            turn_rows(t + 1)
            up(t, k, e, 1)

        tile(1, 1, 0, 0)
        with pe.Fori(1, FIRST // 2) as i:
            tile(i * 2, 0, 0, 0)
            tile(i * 2 + 1, 1, 0, 0)
        pe.wait_ge(S["chunk_lo_ready"], NCHUNK * NE)
        with pe.Fori(FIRST // 2, NT // 2 - 1) as i:
            e = [pe.value_load(tile_e[0:1, bass.ds(i * 2 + m, 1)], min_val=0, max_val=NE) for m in range(-1, 2)]
            tile(i * 2, 0, e[1], e[0])
            tile(i * 2 + 1, 1, e[2], e[1])
        tile(NT - 2, 0, 0, 0)
        up(NT - 1, 1, 0, 0)
        down(NT - 2, 0)
        up(NT - 1, 1, 0, 1)
        down(NT - 1, 0)

    @block.scalar
    def _(act):
        def copy(dst, src, done):
            nc.scalar.activation(dst, src, ACT.Copy).then_inc(done, 1)

        def rstd(k, which, n):
            wait(act, S[which + "_stat_ready"], n)
            nc.scalar.activation(stats[k][:, 8:9], stats[k][:, 7:8], ACT.Ln, bias=const("eps"))\
                .then_inc(S[which + "_log_ready"], 1)
            wait(act, S[which + "_log_ready"], n)
            nc.scalar.activation(stats[k][:, 9:10], stats[k][:, 8:9], ACT.Exp, scale=-0.5)\
                .then_inc(S[which + "_rstd_ready"], 1)

        def ctx_copies(j):
            for k, bank in enumerate((bank_ma, bank_mb)):
                wait(act, S["ctx_turned"], j.n(2, k + 1))
                copy(ctx_t[:, k, :], bank, S["ctx_t_ready"])

        def k_copies(j):
            wait(act, S["scores_done"], j.n(2))
            for g, bank in enumerate((bank_tb, bank_mb)):
                wait(act, S["k_turned"], j.n(2, g + 1))
                copy(k_t[:, g, :, :].rearrange("p b j -> p (b j)"), bank, S["k_t_ready"])

        def exps(p, b, r):
            wait(act, S["max_ready"], p.n(8, 4 * b + r + 1))
            wait(act, S["probs_turned"], p.n(8, 4 * b - 4))
            wait(act, S["inv_ready"], p.n(2, b - 1))
            for g in range(2):
                hp = 4 * g + r
                nc.scalar.activation(probs[b][:, 2 * r + g, :], ps[:, r, g * SK:(g + 1) * SK], ACT.Exp,
                                     bias=neg_max[b][:, hp:hp + 1], accum_out=row_sum[b][:, hp:hp + 1])\
                    .then_inc(S["exp_done"], 1)

        def probs_high(p, b):
            wait(act, S["av_done"], p.n(2, b))
            for r in range(4):
                wait(act, S["probs_turned"], p.n(8, 4 * b + r + 1))
                copy(probs_s[0][:, r, :], probs_bank(b, r), S["probs_hi_ready"])

        def heads_copy(p, b, bank):
            wait(act, S["heads_turned"], p.n(2, b + 1))
            wait(act, S["proj_done"], p.n(1))
            copy(heads_t[:, :, b, :], bank[:, 0:P].rearrange("p (a i) -> p a i", a=2), S["heads_t_ready"])

        def two_blocks(dst, bank, turned, n, done):
            wait(act, S[turned], n)
            copy(dst, bank[:, 0:D].rearrange("p (k n) -> p k n", k=DK), S[done])

        def step(p, nxt=True, gla=True, att=True):
            g, j = p.next(-1), p.next()
            if gla:
                two_blocks(x1n_s[0], bank_ta, "x1n_turned", p.n(1), "x1n_hi_ready")
            if nxt:
                rstd(0, "x", j.n(1, 1))
                ctx_copies(j)
            if att:
                exps(p, 0, 0)
            if gla:
                wait(act, S["qkl_done"], p.n(1))
                nc.scalar.activation(low_t[0:16, :], bank_ta[0:16, 2 * P:3 * P], ACT.Copy, scale=1 / W_SCALE)\
                    .then_inc(S["low_t_ready"], 1)
            if att:
                for r in range(1, 4):
                    exps(p, 0, r)
            if gla:
                wait(act, S["kg_abs_ready"], p.n(1))
                nc.scalar.activation(kg_exp, kg_abs, ACT.Exp, scale=-1.0).then_inc(S["kg_exp_ready"], 1)
                wait(act, S["kg_exp_ready"], p.n(1))
                nc.scalar.activation(kg_ln, kg_exp, ACT.Ln, bias=const("one")).then_inc(S["kg_ln_ready"], 1)
                wait(act, S["dec_ready"], p.n(1))
                nc.scalar.activation(q_dec, q_dec, ACT.Exp, scale=1.0 / GATE_NORM).then_inc(S["dec_exp_q"], 1)
                wait(act, S["dec_min"], p.n(1))
                nc.scalar.activation(k_dec.rearrange("p c b i -> p (c b i)"), k_dec.rearrange("p c b i -> p (c b i)"),
                                     ACT.Exp, bias=const("lnscale"), scale=1.0 / GATE_NORM).then_inc(S["dec_exp_k"], 1)
            if att:
                probs_high(p, 0)
            if gla:
                wait(act, S["gate_ready"], p.n(1))
                nc.scalar.activation(gate_e, gate, ACT.Exp, scale=-1.0).then_inc(S["gate_step"], 1)
                wait(act, S["gate_step"], g.n(2, 1))
                nc.scalar.activation(gate_e, gate_e, ACT.Ln, bias=const("one")).then_inc(S["gate_step"], 1)
                wait(act, S["gate_step"], g.n(2, 2))
                wait(act, S["gn_scaled"], g.n(1))
                nc.scalar.activation(gate_i, gate_e, ACT.Exp, scale=-1.0).then_inc(S["gate_inv"], 1)
            if nxt:
                two_blocks(xn_t, bank_ta, "xn_turned", j.n(1, 1), "xn_t_ready")
            if att:
                exps(p, 1, 0)
            if gla:
                wait(act, S["go_done"], p.n(1))
                nc.scalar.activation(g_out, bank_ma[:, 0:D], ACT.Copy, scale=1 / (A_SCALE * V_SCALE))\
                    .then_inc(S["go_ready"], 1)
            if att:
                exps(p, 1, 1)
                heads_copy(p, 0, bank_ma)
                exps(p, 1, 2)
            if nxt:
                k_copies(j)
            if att:
                exps(p, 1, 3)
            if gla:
                wait(act, S["gs_var"], p.n(1))
                nc.scalar.activation(g_stat[:, 2, :], g_stat[:, 1, :], ACT.Ln, bias=const("eps"), scale=1.0 / GV)\
                    .then_inc(S["gs_log"], 1)
                wait(act, S["gs_log"], p.n(1))
                nc.scalar.activation(g_stat[:, 3, :], g_stat[:, 2, :], ACT.Exp, scale=-0.5).then_inc(S["gs_rstd"], 1)
            if att:
                probs_high(p, 1)
            if gla:
                two_blocks(g_norm_t, bank_ma, "gn_turned", p.n(1), "gn_t_ready")
                rstd(2, "x2", p.n(1))
            if att:
                heads_copy(p, 1, bank_tb)
            if gla:
                two_blocks(x2n_t, bank_ta, "x2n_turned", p.n(1), "x2n_t_ready")
                wait(act, S["logits_done"], p.n(1))
                copy(logits[:, g.n(1), :] if isinstance(g.n(1), int) else
                     logits[:, bass.ds(g.n(1), 1), :].rearrange("p a e -> p (a e)"), bank_ma[:, 0:NE],
                     S["logits_ready"])
            if att:
                rstd(1, "x1", p.n(1, 1))

        act.preload_act_table_set("natural_log_exp_and_others")
        act.wait_ge(S["consts_loaded"], 16)
        zero = Step(0, 0)
        rstd(0, "x", 1)
        ctx_copies(zero)
        two_blocks(xn_t, bank_ta, "xn_turned", 1, "xn_t_ready")
        k_copies(zero)

        def third(p):
            step(p)
            act.wait_ge(S["shared_loaded"], 64)
            act.wait_ge(S["slots_filled"], 16 * N_FILL)
            nc.scalar.activation(experts_h[:, 0, 0:EW], experts[:, 1, :], ACT.Copy, scale=W_SCALE)\
                .then_inc(S["shared_hi"], 1)

        over_pairs(act, lambda p: step(p, gla=False), step, lambda p: step(p, nxt=False), third)
        step(Step(0, NPAIR), nxt=False, att=False)

        act.wait_ge(S["route_step"], 1)
        nc.scalar.activation(r_e, r_z, ACT.Exp, scale=-1.0).then_inc(S["route_exp"], 1)

        def rows_copy(t, k):
            wait(act, S["up_done"], t * 2 - 2)
            wait(act, S["rows_turned"], t + 1)
            copy(e_rows_t[k].rearrange("p m n -> p (m n)"), ps[:, 0, :].bitcast(F16), S["rows_t_ready"])

        def silu(t, half):
            wait(act, S["gate_done"], t * 2 + half + 1)
            wait(act, S["hid_ready"], t * 2 + half)
            nc.scalar.activation(e_silu, ps_flat[:, 512 + half * HALF:512 + (half + 1) * HALF], ACT.Silu,
                                 scale=1 / W_SCALE).then_inc(S["silu_ready"], 1)

        def hidden_high(t, half):
            wait(act, S["hid_ready"], t * 2 + half + 1)
            wait(act, S["down_done"], t)
            c = slice(half * HT // 2, (half + 1) * HT // 2)
            copy(e_hid_s[0][:, c, :].rearrange("p c n -> p (c n)"), e_hid, S["hid_hi_ready"])

        def chunk_high(n):
            e, c = n // NCHUNK, n % NCHUNK
            if n % 2 == 0:
                act.wait_ge(chunk_loaded[0], 48 * e + (32 if c == 0 else 48))
            else:
                act.wait_ge(chunk_loaded[1], 64 * e + (32 if c == 1 else 64))
            if n == NCHUNK:
                act.wait_ge(S["table_ready"], 1)
            lo, hi = CHUNKS[c]
            nc.scalar.activation(experts_h[:, 1 + e, lo:hi], w_raw[n % 2][:, 0:hi - lo], ACT.Copy, scale=W_SCALE)\
                .then_inc(S["chunk_hi_ready"], 1)

        def tile(t, k):
            silu(t, 0)
            hidden_high(t, 0)
            rows_copy(t + 1, 1 - k)
            silu(t, 1)
            hidden_high(t, 1)

        rows_copy(0, 0)
        for t in range(FIRST):
            tile(t, t % 2)
            for n in chunks_of(t):
                chunk_high(n)
        with act.Fori(FIRST // 2, NT // 2 - 1) as i:
            tile(i * 2, 0)
            tile(i * 2 + 1, 1)
        tile(NT - 2, 0)
        for half in range(2):
            silu(NT - 1, half)
            hidden_high(NT - 1, half)

    @block.vector
    def _(dve):
        v = nc.vector

        def copy(dst, src, done):
            v.tensor_copy(dst, src).then_inc(done, 1)

        def norm_stats(k, src, which, n):
            v.bn_stats(stats[k][:, 0:6], src).then_inc(S[which + "_bn"], 1)
            wait(dve, S[which + "_bn"], n)
            apart(dve)
            v.bn_aggr(stats[k][:, 6:8], stats[k][:, 0:6]).then_inc(S[which + "_stat_ready"], 1)

        def norm_apply(k, dst, src, which, done, n):
            wait(dve, S[which + "_rstd_ready"], n)
            v.tensor_scalar(dst, src, stats[k][:, 6:7], stats[k][:, 9:10], ALU.subtract, ALU.mult)\
                .then_inc(S[done], 1)

        def x_stats(j):
            wait(dve, x_loaded[j.par], j.half * 16 + 16)
            norm_stats(0, x_in[j.par], "x", j.n(1, 1))

        def x_norm(j):
            wait(dve, S["xn_turned"], j.n(1))
            norm_apply(0, xn, x_in[j.par], "x", "xn_ready", j.n(1, 1))

        def max_rows(p, b):
            wait(dve, S["scores_done"], p.n(2, b + 1))
            wait(dve, S["exp_done"], p.n(16, 8 * b - 8))
            nm = neg_max[b].rearrange("p (g r) -> p g r", g=2)
            for r in range(4):
                v.tensor_reduce(nm[:, :, r], ps[:, r, :].rearrange("p (g j) -> p g j", g=2), AX.X, ALU.max,
                                negate=True).then_inc(S["max_ready"], 1)

        def kv_bias(j, t):
            wait(dve, S["kv_done"], j.n(4, t + 1))
            wait(dve, S["k_swap_ready"], j.n(1))
            wait(dve, S["k_prod_ready"], j.n(1))
            wait(dve, S["v_split"], j.n(2))
            bank = (bank_ma, bank_mb)[t % 2]
            v.tensor_tensor(kv[:, t, :], bank, b_kv, ALU.add).then_inc(S["kv_ready"], 1)

        def k_cos(j):
            wait(dve, S["kv_ready"], j.n(4, 4))
            wait(dve, S["k_turned"], j.n(2))
            cos = const("cosk").rearrange("p (t c) -> p t c", t=2)
            for b in range(2):
                ins = v.tensor_tensor(k_rot[:, 2 * b:2 * b + 2, :].rearrange("p t (h c) -> p t h c", h=H),
                                      kv[:, 2 * b:2 * b + 2, 0:D].rearrange("p t (h c) -> p t h c", h=H),
                                      bc(cos, 2, H), ALU.mult)
            ins.then_inc(S["k_prod_ready"], 1)

        def k_add(j):
            wait(dve, S["k_swap_ready"], j.n(1, 1))
            wait(dve, S["k_prod_ready"], j.n(1, 1))
            v.tensor_tensor(k_rot, k_rot, k_swap, ALU.add).then_inc(S["k_rot_ready"], 1)

        def q_bias(j):
            wait(dve, S["q_done"], j.n(1, 1))
            wait(dve, S["q_swap_ready"], j.n(1))
            v.tensor_tensor(q_nat, bank_ta[:, 0:D], b_q, ALU.add).then_inc(S["q_nat_ready"], 1)
            wait(dve, S["q_nat_ready"], j.n(1, 1))
            wait(dve, S["q_turned"], j.n(1))
            v.tensor_tensor(q_rot.rearrange("p (h c) -> p h c", h=H), q_nat.rearrange("p (h c) -> p h c", h=H),
                            bc(const("cosq"), 1, H), ALU.mult).then_inc(S["q_prod_ready"], 1)

        def q_add(j):
            wait(dve, S["q_swap_ready"], j.n(1, 1))
            wait(dve, S["q_prod_ready"], j.n(1, 1))
            v.tensor_tensor(q_rot, q_rot, q_swap, ALU.add).then_inc(S["q_rot_ready"], 1)

        def q_heads_split(j):
            wait(dve, S["q_turned"], j.n(1, 1))
            wait(dve, S["scores_done"], j.n(2))
            for a in range(2):
                ins = v.tensor_scalar(q_t[:, :, :, a, :],
                                      bank_mb[:, 0:D].rearrange("p (g b i) -> p g b i", g=2, b=2),
                                      const("par")[:, a:a + 1], None, ALU.mult)
            ins.then_inc(S["q_t_ready"], 1)

        def probs_low(p, b):
            for r in range(4):
                wait(dve, S["probs_hi_ready"], p.n(8, 4 * b + r + 1))
                v.tensor_tensor(probs_s[1][:, r, :], probs_bank(b, r), probs_s[0][:, r, :], ALU.subtract)\
                    .then_inc(S["probs_lo_ready"], 1)

        def normalise(p, b, bank):
            wait(dve, S["exp_done"], p.n(16, 8 * b + 8))
            v.reciprocal(row_inv, row_sum[b]).then_inc(S["inv_ready"], 1)
            wait(dve, S["inv_ready"], p.n(2, b + 1))
            wait(dve, S["av_done"], p.n(2, b + 1))
            wait(dve, S["heads_turned"], p.n(2, b - 1))
            for a in range(2):
                rows = slice(SQ * a, SQ * a + SQ)
                src = bank[rows, 0:D].rearrange("p (h a c) -> p h a c", h=8, a=2)[:, :, a, :]
                ins = v.tensor_tensor(heads_out[b][rows], src, bc(row_inv[rows, :], 2, HC), ALU.mult)
            ins.then_inc(S["av_ready"], 1)

        def add_x1(p):
            wait(dve, S["proj_done"], p.n(1, 1))
            wait(dve, S["x_res_ready"], p.n(1, 1))
            v.tensor_tensor(x1, bank_mb[:, 0:D], x_res, ALU.add).then_inc(S["x1_ready"], 1)
            wait(dve, S["x1_ready"], p.n(1, 1))
            norm_stats(1, x1, "x1", p.n(1, 1))
            norm_apply(1, x1n, x1, "x1", "x1n_ready", p.n(1, 1))

        def step(p, nxt=True, gla=True, att=True):
            g, j = p.next(-1), p.next()
            n = p.n(1)
            if gla:
                wait(dve, S["x1n_hi_ready"], n)
                v.tensor_tensor(x1n_s[1], bank_ta[:, 0:D].rearrange("p (k n) -> p k n", k=DK), x1n_s[0], ALU.subtract)\
                    .then_inc(S["x1n_lo_ready"], 1)
            if nxt:
                x_stats(j)
            if att:
                max_rows(p, 0)
            if gla:
                wait(dve, S["vg_done"], n)
                v.tensor_scalar(g_v_s[0][:, 0, :], bank_tb[:, 0:D], V_SCALE / W_SCALE, None, ALU.mult)\
                    .then_inc(S["g_v_hi_ready"], 1)
                v.scalar_tensor_tensor(out=gate, in0=bank_tb[:, D:2 * D], scalar=1 / W_SCALE, in1=b_g, op0=ALU.mult,
                                       op1=ALU.add).then_inc(S["gate_ready"], 1)
                wait(dve, S["g_v_hi_ready"], n)
                v.scalar_tensor_tensor(out=g_v_s[1][:, 0, :], in0=bank_tb[:, 0:D], scalar=V_SCALE / W_SCALE,
                                       in1=g_v_s[0][:, 0, :], op0=ALU.mult, op1=ALU.subtract)\
                    .then_inc(S["g_v_ready"], 1)
            if nxt:
                x_norm(j)
                kv_bias(j, 0)
            if gla:
                wait(dve, S["kg_done"], n)
                v.tensor_scalar(kg_min, bank_tb[:, 0:P], 0.0, None, ALU.min).then_inc(S["kg_min_ready"], 1)
                wait(dve, S["kg_min_ready"], n)
                v.scalar_tensor_tensor(out=kg_abs, in0=kg_min, scalar=-2.0, in1=bank_tb[:, 0:P], op0=ALU.mult,
                                       op1=ALU.add).then_inc(S["kg_abs_ready"], 1)
            if nxt:
                kv_bias(j, 1)
            if gla:
                wait(dve, S["kg_ln_ready"], n)
                wait(dve, S["kg_min_ready"], n)
                v.tensor_tensor(log_gate, kg_min, kg_ln, ALU.subtract).then_inc(S["decay_step"], 1)
                wait(dve, S["decay_step"], g.n(3, 1))
                for b in range(2):
                    ins = v.tensor_tensor_scan(cum[:, b, :], log_gate[:, b * SQ:(b + 1) * SQ],
                                               log_gate[:, b * SQ:(b + 1) * SQ], 0.0, ALU.add, ALU.bypass)
                ins.then_inc(S["decay_step"], 1)
                wait(dve, S["decay_step"], g.n(3, 2))
                copy(ref[:, :, 1:NCH], cum.rearrange("p b (c t) -> p b c t", t=CH)[:, :, 0:NCH - 1, CH - 1],
                     S["decay_step"])
                wait(dve, S["decay_step"], g.n(3, 3))
                v.tensor_tensor(q_dec.rearrange("p (b c t) -> p b c t", b=2, c=NCH),
                                cum.rearrange("p b (c t) -> p b c t", t=CH), bc(ref, 3, CH), ALU.subtract)\
                    .then_inc(S["dec_ready"], 1)
                v.tensor_tensor(k_dec, bc(ref.rearrange("p b c -> p c b"), 3, SQ), bc(cum, 1, NCH), ALU.subtract)\
                    .then_inc(S["dec_k_ready"], 1)
                wait(dve, S["dec_k_ready"], n)
                kd = k_dec.rearrange("p c b i -> p (c b i)")
                v.tensor_scalar(kd, kd, BOUND * GATE_NORM, None, ALU.min).then_inc(S["dec_min"], 1)
            if nxt:
                kv_bias(j, 2)
                kv_bias(j, 3)
            if gla:
                wait(dve, S["dec_exp_q"], n)
                v.tensor_tensor(qs_t, bank_ta[:, 0:P], q_dec, ALU.mult).then_inc(S["qs_ready"], 1)
                wait(dve, S["dec_exp_k"], n)
                v.tensor_tensor(k_heads, bc(bank_ta[:, P:2 * P].rearrange("p (b i) -> p b i", b=2), 1, NCH), k_dec,
                                ALU.mult).then_inc(S["k_heads_ready"], 1)
                wait(dve, S["qs_ready"], n)
                v.tensor_tensor(q_heads.rearrange("p b c h t -> p (b c) h t"),
                                bc(qs_t.rearrange("p (m t) -> p m t", t=CH), 2, 4),
                                bc(bc(const("head4"), 1, 2 * NCH), 3, CH), ALU.mult).then_inc(S["q_heads_ready"], 1)
            if att:
                probs_low(p, 0)
            if nxt:
                k_cos(j)
            if gla:
                wait(dve, S["a_done"], n)
                for r in range(4):
                    v.tensor_tensor(a_t[:, r].rearrange("p h c t -> p c h t"), ps[:, r, 0:256].rearrange("p (c h t) -> p c h t", c=NCH, h=4),
                                    bc(const("gla").rearrange("p (c t) -> p c t", c=NCH), 2, 4), ALU.mult)\
                        .then_inc(S["a_ready"], 1)
            if nxt:
                k_add(j)
            if att:
                normalise(p, 0, bank_mb)
            if gla:
                wait(dve, S["gate_inv"], n)
                v.tensor_tensor(gate_i, gate, gate_i, ALU.mult).then_inc(S["gate_silu"], 1)
            if att:
                max_rows(p, 1)
            if gla:
                wait(dve, S["go_ready"], n)
                heads = g_out.rearrange("p (h c) -> p h c", h=H)
                sq = g_sq.rearrange("p (h c) -> p h c", h=H)
                gn = g_norm.rearrange("p (h c) -> p h c", h=H)
                v.tensor_reduce(g_stat[:, 0, :], heads, AX.X, ALU.add).then_inc(S["gs_step"], 1)
                wait(dve, S["gs_step"], g.n(4, 1))
                v.tensor_scalar(g_stat[:, 0, :], g_stat[:, 0, :], 1.0 / GV, None, ALU.mult).then_inc(S["gs_step"], 1)
                wait(dve, S["gs_step"], g.n(4, 2))
                v.tensor_tensor(heads, heads, bc(g_stat[:, 0, :], 2, GV), ALU.subtract).then_inc(S["gs_step"], 1)
                wait(dve, S["gs_step"], g.n(4, 3))
                v.tensor_tensor(sq, heads, heads, ALU.mult).then_inc(S["gs_step"], 1)
                wait(dve, S["gs_step"], g.n(4, 4))
                v.tensor_reduce(g_stat[:, 1, :], sq, AX.X, ALU.add).then_inc(S["gs_var"], 1)
                wait(dve, S["gate_silu"], n)
                wait(dve, S["gs_var"], n)
                v.tensor_tensor(g_sq, g_out, gate_i, ALU.mult).then_inc(S["gn_scaled"], 1)
                wait(dve, S["gn_scaled"], n)
                wait(dve, S["gs_rstd"], n)
                v.tensor_tensor(gn, sq, bc(g_stat[:, 3, :], 2, GV), ALU.mult).then_inc(S["gn_ready"], 1)
            if nxt:
                q_bias(j)
            if nxt:
                q_add(j)
            if att:
                probs_low(p, 1)
            if gla:
                wait(dve, S["gproj_done"], n)
                gt = g.n(1)
                x2 = x2_all[:, gt, :] if isinstance(gt, int) else \
                    x2_all[:, bass.ds(gt, 1), :].rearrange("p a d -> p (a d)")
                v.tensor_tensor(x2, bank_mb[:, 0:D], x1, ALU.add).then_inc(S["x2_ready"], 1)
                wait(dve, S["x2_ready"], n)
                apart(dve)
                norm_stats(2, x2, "x2", n)
            if att:
                normalise(p, 1, bank_ma)
            if gla:
                wait(dve, S["x2n_split"], g.n(2, -2))
                norm_apply(2, x2n[g.par], x2, "x2", "x2n_ready", n)
            if nxt:
                q_heads_split(j)
            if att:
                add_x1(p)

        dve.wait_ge(S["consts_loaded"], 16)
        dve.wait_ge(S["weights_loaded"], 16 * WEIGHT_DMAS)
        v.memset(ref[:, :, 0:1], 0.0).then_inc(S["ref_zero"], 1)
        dve.wait_ge(S["ref_zero"], 1)
        zero = Step(0, 0)
        x_stats(zero)
        x_norm(zero)
        for t in range(4):
            kv_bias(zero, t)
        k_cos(zero)
        k_add(zero)
        q_bias(zero)
        q_add(zero)
        q_heads_split(zero)
        for k, (w, (high, low)) in enumerate(((w_gqk, w_gqk_s), (w_g1, w_g1_s), (w_gvg, w_gvg_s))):
            v.tensor_scalar(high, w, W_SCALE, None, ALU.mult).then_inc(S["gla_hi_ready"], 1)
            dve.wait_ge(S["gla_hi_ready"], k + 1)
            v.scalar_tensor_tensor(out=low, in0=w, scalar=W_SCALE, in1=high, op0=ALU.mult, op1=ALU.subtract)\
                .then_inc(S["gla_lo_ready"], 1)

        def third(p):
            step(p)
            dve.wait_ge(S["shared_hi"], 1)
            v.scalar_tensor_tensor(out=experts_h[:, 0, EW:], in0=experts[:, 1, :], scalar=W_SCALE,
                                   in1=experts_h[:, 0, 0:EW], op0=ALU.mult, op1=ALU.subtract)\
                .then_inc(S["shared_lo"], 1)

        over_pairs(dve, lambda p: step(p, gla=False), step, lambda p: step(p, nxt=False), third)
        step(Step(0, NPAIR), nxt=False, att=False)

        count = [0]

        def link(ins):
            ins.then_inc(S["route_step"], 1)
            count[0] += 1
            dve.wait_ge(S["route_step"], count[0])

        dve.wait_ge(S["logits_ready"], NPAIR)
        dve.wait_ge(x2n_stored[0], 16 * NPAIR // 2)
        dve.wait_ge(x2n_stored[1], 16 * NPAIR // 2)
        for raw in w_raw:
            ins = v.memset(raw, 0.0)
        ins.then_inc(S["tail_zero_raw"], 1)
        v.tensor_copy(ident_h, ident).then_inc(S["ident_h_ready"], 1)
        dve.wait_ge(S["biasr_loaded"], 16)
        link(v.tensor_tensor(r_z, logits[:, :, :], bc(r_bias, 1, NTILE), ALU.mult))
        dve.wait_ge(S["route_exp"], 1)
        link(v.tensor_scalar(r_c, r_e, 1.0, None, ALU.add))
        link(v.reciprocal(r_p, r_c))
        desc = bc(const("desc"), 1, NTILE)
        for c in range(TOPK):
            link(v.tensor_reduce(r_m[:, c, :], r_p, AX.X, ALU.max))
            link(v.tensor_tensor(r_eq, r_p, bc(r_m[:, c, :], 2, NE), ALU.is_equal))
            link(v.tensor_tensor(r_c, r_eq, desc, ALU.mult))
            link(v.tensor_reduce(r_m[:, 2, :], r_c, AX.X, ALU.max))
            link(v.tensor_tensor(r_oh[c], r_c, bc(r_m[:, 2, :], 2, NE), ALU.is_equal))
            if c == 0:
                link(v.scalar_tensor_tensor(out=r_p, in0=r_oh[0], scalar=-4.0, in1=r_p, op0=ALU.mult, op1=ALU.add))
        link(v.memset(r_ones, 1.0))
        link(v.tensor_tensor(r_sel, r_oh[0], r_oh[1], ALU.add))
        assert count[0] == ROUTE_SELECTED
        link(v.tensor_tensor(r_m[:, 3, :], r_m[:, 0, :], r_m[:, 1, :], ALU.add))
        link(v.reciprocal(r_m[:, 4, :], r_m[:, 3, :]))
        for c in range(TOPK):
            link(v.tensor_tensor(w_tok[:, c, :], r_m[:, c, :], r_m[:, 4, :], ALU.mult))
        dve.wait_ge(S["route_mm"], 2)
        link(v.tensor_copy(r_in.rearrange("p t e -> p (t e)"), bank_ma[:, 0:L]))
        link(v.tensor_copy(r_tot.rearrange("p t e -> p (t e)"), bank_mb[:, 0:L]))
        for e in range(NE):
            link(v.tensor_tensor_scan(r_cum[:, :, e], r_tot[:, :, e], r_tot[:, :, e], 0.0, ALU.add, ALU.bypass))
        link(v.tensor_scalar(r_ni, r_cum[:, NTILE - 1, :], float(R - 1), None, ALU.add))
        link(v.tensor_scalar(r_ni, r_ni, R.bit_length() - 1, None, ALU.arith_shift_right))
        link(v.tensor_copy(r_n[:, 0, :], r_ni))
        link(v.tensor_tensor_scan(r_n[:, 1, :], r_n[:, 0, :], r_n[:, 0, :], 0.0, ALU.add, ALU.bypass))
        link(v.tensor_tensor(r_n[:, 2, :], r_n[:, 1, :], r_n[:, 0, :], ALU.subtract))
        link(v.tensor_scalar(r_n[:, 3, :], r_n[:, 2, :], float(R), None, ALU.mult))
        link(v.tensor_tensor(r_pos, r_cum, r_tot, ALU.subtract))
        link(v.tensor_tensor(r_pos, r_pos, r_in, ALU.add))
        link(v.tensor_tensor(r_pos, r_pos, bc(r_n[:, 3, :], 1, NTILE), ALU.add))
        for c in range(TOPK):
            link(v.tensor_tensor(r_c, r_oh[c], r_pos, ALU.mult))
            link(v.tensor_reduce(r_m[:, 5, :], r_c, AX.X, ALU.add))
            link(v.tensor_copy(slot_i[:, c, :], r_m[:, 5, :]))
        link(v.tensor_tensor(r_t, bc(const("tile"), 2, NE), bc(r_n[:, 1, :], 1, NSLOT), ALU.is_ge))
        link(v.tensor_reduce(r_tf, r_t, AX.X, ALU.add))
        link(v.tensor_scalar(r_tf, r_tf, 1.0, float(NE), ALU.add, ALU.min))
        link(v.memset(tile_e, 0))
        link(v.tensor_copy(tile_e[:, FIRST:MID], r_tf))
        assert count[0] == ROUTE_DONE
        v.memset(r_ones[:, 0:1], 1.0).then_inc(S["table_ready"], 1)

        def hidden(t, half):
            wait(dve, S["up_done"], t * 2 + half + 1)
            wait(dve, S["silu_ready"], t * 2 + half + 1)
            wait(dve, S["hid_lo_ready"], t * 2 + half)
            v.scalar_tensor_tensor(out=e_hid, in0=ps_flat[:, 2048 + half * HALF:2048 + (half + 1) * HALF],
                                   scalar=1 / W_SCALE, in1=e_silu, op0=ALU.mult, op1=ALU.mult)\
                .then_inc(S["hid_ready"], 1)

        def hidden_low(t, half):
            wait(dve, S["hid_hi_ready"], t * 2 + half + 1)
            c = slice(half * HT // 2, (half + 1) * HT // 2)
            high, low = (h[:, c, :].rearrange("p c n -> p (c n)") for h in e_hid_s)
            v.tensor_tensor(low, e_hid, high, ALU.subtract).then_inc(S["hid_lo_ready"], 1)

        def result(t):
            wait(dve, S["down_done"], t + 1)
            wait(dve, S["y_stored"], t * 16)
            v.tensor_scalar(e_y.rearrange("p a d -> p (a d)"), ps[:, 7, :], 1 / W_SCALE, None, ALU.mult)\
                .then_inc(S["y_ready"], 1)

        def chunk_low(n):
            dve.wait_ge(S["chunk_hi_ready"], n + 1)
            e, c = n // NCHUNK, n % NCHUNK
            lo, hi = CHUNKS[c]
            w = experts_h[:, 1 + e, :]
            v.scalar_tensor_tensor(out=w[:, EW + lo:EW + hi], in0=w_raw[n % 2][:, 0:hi - lo], scalar=W_SCALE,
                                   in1=w[:, lo:hi], op0=ALU.mult, op1=ALU.subtract)\
                .then_inc(S["chunk_lo_ready"], 1)

        def tile(t):
            hidden(t, 0)
            hidden_low(t, 0)
            result(t - 1)
            hidden(t, 1)
            hidden_low(t, 1)

        for half in range(2):
            hidden(0, half)
            hidden_low(0, half)
        for n in chunks_of(0):
            chunk_low(n)
        for t in range(1, FIRST):
            tile(t)
            for n in chunks_of(t):
                chunk_low(n)
        with dve.Fori(FIRST, MID) as t:
            tile(t)

        def combine(m):
            dve.wait_ge(S["first_shared_loaded" if (m + 1) * GROUP <= 2 * FIRST else "last_shared_loaded"], 16)
            dve.wait_ge(group_loaded[m], 16 * TOPK * GROUP)
            tiles = slice(m * GROUP, (m + 1) * GROUP)
            v.tensor_tensor(x2_all[:, tiles, :], x2_all[:, tiles, :], results[:, 2, tiles, :], ALU.add)\
                .then_inc(S["sum_step"], 1)
            for c in range(TOPK):
                dve.wait_ge(S["sum_step"], (1 + TOPK) * m + c + 1)
                for t in range(m * GROUP, (m + 1) * GROUP):
                    x2 = x2_all[:, t, :]
                    ins = v.scalar_tensor_tensor(out=x2, in0=results[:, c, t, :], scalar=w_tok[:, c, t:t + 1], in1=x2,
                                                 op0=ALU.mult, op1=ALU.add)
                ins.then_inc(S["sum_step"], 1)
            dve.wait_ge(S["sum_step"], (1 + TOPK) * (m + 1))
            dve.sem_inc(S["sum_ready"], 1)

        done = 0
        for t in range(MID, NT):
            tile(t)
            while done < (t - MID - 1) * 3 // 2 and (done + 1) * GROUP <= 2 * FIRST and t >= MID + 2:
                combine(done)
                done += 1
        result(NT - 1)
        for m in range(done, NTILE // GROUP):
            combine(m)


WEIGHT_DMAS = 3 + 16 + 8 + 5
N_FILL = -(-2 * NSLOT // 8)
SPLIT_TILES = FIRST - 2


def chunks_of(t):
    if not 0 <= t < SPLIT_TILES:
        return range(0)
    n = NCHUNK * NE
    return range(n * t // SPLIT_TILES, n * (t + 1) // SPLIT_TILES)



BOUND = 60.0
ROUTE_SELECTED = 3 + 5 * TOPK + 1 + 2
ROUTE_DONE = ROUTE_SELECTED + 4 + 2 + NE + 6 + 3 + 3 * TOPK + 5


_INS = ["x", "ctx_1024", "mask_BxS2_bf0", "L0_xattn_Wq", "L0_xattn_bq", "L0_xattn_Wk", "L0_xattn_bk", "L0_xattn_Wv",
        "L0_xattn_bv", "L0_xattn_Wo", "L0_xattn_bo", "L0_attn_Wq", "L0_attn_Wk", "L0_attn_Wg1", "L0_attn_Wg2",
        "L0_attn_Wv", "L0_attn_Wg", "L0_attn_bg", "L0_attn_Wo", "L0_ffn_shared_gate", "L0_ffn_shared_up",
        "L0_ffn_shared_down", "L0_ffn_routed_gate", "L0_ffn_routed_up", "L0_ffn_routed_down", "L0_ffn_Wr",
        "L0_ffn_routing_bias"]


def kernel(**inputs):
    import concourse.bacc as bacc
    from concourse.bass_utils import run_bass_kernel_spmd

    nc = bacc.Bacc("TRN2", target_bir_lowering=False, num_devices=1)
    arrays, args = {}, []
    for name in _INS:
        a = np.ascontiguousarray(inputs[name])
        arrays["in_" + name] = a
        args.append(nc.dram_tensor("in_" + name, a.shape, mybir.dt.from_np(a.dtype), kind="ExternalInput").ap())
    arrays["constants"] = constants()
    args.append(nc.dram_tensor("constants", [P, NCONST], F32, kind="ExternalInput").ap())
    args.append(nc.dram_tensor("out", [NB, SQ, D], F32, kind="ExternalOutput").ap())
    build(nc, *args)
    result = run_bass_kernel_spmd(nc, [arrays], core_ids=[0])
    return result.results[0]["out"]
```

```python
from contextlib import ExitStack

import numpy as np
import concourse.bass as bass
from concourse import mybir

ALU = mybir.AluOpType
ACT = mybir.ActivationFunctionType
AX = mybir.AxisListType
F32 = mybir.dt.float32
BF16 = mybir.dt.bfloat16
F16 = mybir.dt.float16
I32 = mybir.dt.int32
U32 = mybir.dt.uint32
U8 = mybir.dt.uint8

P = 128
D = 256
DK = D // P
NB, SQ, SK = 64, 64, 256
NPAIR = NB // 2
H, HC = 16, 16
GK, GV = 8, 16
NCH, CH = 4, 16
GATE_NORM = 16.0
EPS = 1e-5
HID = 704
HT = (HID + P - 1) // P
HR = HID - (HT - 1) * P
HH = HID // 2
NE, TOPK = 7, 2
NTILE = NB * SQ // P
R = 2 * P
NSLOT = (NB * SQ * TOPK + NE * (R - 1)) // R
NT = NTILE * P // R + NSLOT
EW_UP, EW_DOWN = DK * 2 * HID, HT * D
EW = EW_UP + EW_DOWN
EARLY = 2
LAST = 6
FIRST = NTILE * P // R - LAST
MID = FIRST + NSLOT
CHUNKS = [(0, 2 * HID), (2 * HID, 4 * HID), (EW_UP, EW_UP + HT * D // 2), (EW_UP + HT * D // 2, EW)]
NCHUNK = len(CHUNKS)
HALF = HT * R // 2
GROUP = 4
W_SCALE = 2.0 ** 6
V_SCALE = 2.0 ** 4
A_SCALE = 2.0 ** 6
NEG = -(2.0 ** 127)

CONST = {}
_at = 0
for _name, _n in (("ident", P), ("causal", SK), ("cosk", 32), ("sink", 32), ("cosq", HC), ("sinq", HC),
                  ("par", 2), ("head4", 4), ("gla", NCH * CH), ("upper", P), ("eps", 1), ("lnscale", 1),
                  ("one", 1), ("tile", NSLOT), ("desc", NE)):
    CONST[_name] = (_at, _at + _n)
    _at += _n
NCONST = _at


def constants():
    c = np.zeros((P, NCONST), np.float32)
    p = np.arange(P)

    def put(name, a):
        lo, hi = CONST[name]
        c[:, lo:hi] = np.broadcast_to(np.asarray(a, np.float32).reshape(-1, hi - lo), (P, hi - lo))

    inv = (1.0 / 10000.0 ** (np.arange(0, HC, 2, dtype=np.float32) / np.float32(HC))).astype(np.float32)

    def rope(pos, scale):
        t = pos[..., None].astype(np.float32) * inv
        cos = np.repeat(np.cos(t), 2, axis=-1)
        sin = np.repeat(np.sin(t), 2, axis=-1)
        sin[..., ::2] *= -1.0
        return cos * scale, sin * scale

    ck, sk = rope(p[:, None] + P * np.arange(SK // P)[None, :], 1.0)
    cq, sq = rope(p % SQ, HC ** -0.5)
    put("ident", np.eye(P))
    put("causal", np.arange(SK)[None, :] <= (p % SQ)[:, None] + SK - SQ)
    put("cosk", ck.reshape(P, -1))
    put("sink", sk.reshape(P, -1))
    put("cosq", cq)
    put("sinq", sq)
    put("par", (p[:, None] // HC) % 2 == np.arange(2)[None, :])
    put("head4", (p[:, None] // GK) % 4 == np.arange(4)[None, :])
    put("gla", (np.arange(SQ)[None, :] >= (p % SQ)[:, None]) * (A_SCALE / W_SCALE ** 2))
    put("upper", p[:, None] < p[None, :])
    put("eps", np.full((P, 1), EPS))
    put("lnscale", np.full((P, 1), np.log(GK ** -0.5)))
    put("one", np.ones((P, 1)))
    put("tile", np.arange(NSLOT)[None, :])
    put("desc", np.arange(NE, 0, -1)[None, :])
    return c


def bc(ap, axis, n):
    v = ap.unsqueeze(axis)
    shape = list(v.shape)
    shape[axis] = n
    return v.to_broadcast(shape)


def norm_count(p, k):
    return 2 if k == 0 and isinstance(p.n(1), int) and p.n(1) == 0 else p.n(3, k + 1)


class Step:

    def __init__(self, i, off):
        self.i, self.off = i, off

    def n(self, per, add=0):
        return self.i * (2 * per) + (self.off * per + add)

    def next(self, k=1):
        return Step(self.i, self.off + k)

    @property
    def par(self):
        return self.off % 2

    @property
    def half(self):
        return self.i + self.off // 2


def wait(eng, sem, value):
    if isinstance(value, int) and value <= 0:
        return
    eng.wait_ge(sem, value)


def build(nc, x, ctx_in, pad, xWq, xbq, xWk, xbk, xWv, xbv, xWo, xbo, gWq, gWk, gWg1, gWg2, gWv, gWg, gbg, gWo,
          sgate, sup, sdown, rgate, rup, rdown, Wr, rbias, consts_in, out):
    with ExitStack() as stack:
        program(nc, stack, x, ctx_in, pad, xWq, xbq, xWk, xbk, xWv, xbv, xWo, xbo, gWq, gWk, gWg1, gWg2, gWv,
                gWg, gbg, gWo, sgate, sup, sdown, rgate, rup, rdown, Wr, rbias, consts_in, out)


def program(nc, stack, x, ctx_in, pad, xWq, xbq, xWk, xbk, xWv, xbv, xWo, xbo, gWq, gWk, gWg1, gWg2, gWv,
            gWg, gbg, gWo, sgate, sup, sdown, rgate, rup, rdown, Wr, rbias, consts_in, out):
    def sb(name, shape, dt=F32):
        return stack.enter_context(nc.sbuf_tensor(name, shape, dt))

    def sem(name):
        return stack.enter_context(nc.semaphore(name))

    token_in, token_out = (nc.dram_tensor(n, [NTILE * P, D], F32, kind="Internal").ap()
                           for n in ("token_in", "token_out"))
    slot_in, slot_out = (nc.dram_tensor(n, [NSLOT * R, D], F32, kind="Internal").ap()
                         for n in ("slot_in", "slot_out"))

    experts = sb("experts", [P, 1 + NE, EW])
    x2_all = sb("x2_all", [P, NTILE, D])
    cst = sb("cst", [P, NCONST])
    logits = sb("logits", [P, NTILE, NE])
    work = sb("work", [P, 8900])

    arenas = [[experts[:, EARLY:, :].rearrange("p e n -> p (e n)"), 0, (1 + NE - EARLY) * EW],
              [work[:, :], 0, 8900]]

    def place(n, which=None):
        for k, a in enumerate(arenas):
            if (which is None or k == which) and a[1] + n <= a[2]:
                a[1] += n
                return a[0][:, a[1] - n:a[1]]
        raise ValueError("no room")

    def const(name):
        lo, hi = CONST[name]
        return cst[:, lo:hi]

    ident = const("ident")
    w_q = place(DK * D).rearrange("p (k n) -> p k n", k=DK)
    w_kv = place(DK * 2 * D).rearrange("p (k n) -> p k n", k=DK)
    w_o = place(2 * D).rearrange("p (a n) -> p a n", a=2)
    w_gqk = place(DK * D).rearrange("p (k n) -> p k n", k=DK)
    w_g1 = place(DK * 16).rearrange("p (k n) -> p k n", k=DK)

    def halves(k, n):
        return [place(k * n // 2).bitcast(F16).rearrange("p (k n) -> p k n", k=k) for _ in range(2)]

    w_gqk_s, w_g1_s, w_gvg_s = halves(DK, D), halves(DK, 16), halves(DK, 2 * D)
    w_g2 = place(P)
    w_gvg = place(DK * 2 * D).rearrange("p (k n) -> p k n", k=DK)
    w_go = place(DK * D).rearrange("p (k n) -> p k n", k=DK)
    w_r = place(DK * NE).rearrange("p (k n) -> p k n", k=DK)
    b_kv = place(2 * D)
    b_q = place(D)
    b_o = place(D)
    b_g = place(D)
    ident_bf = place(P // 2).bitcast(BF16)
    ident_h1 = place(P // 2).bitcast(F16)
    x_in = [place(D) for _ in range(2)]
    x_res = place(D)
    pad_in = [place(2 * SK // 4).bitcast(U8).rearrange("p (b j) -> p b j", b=2) for _ in range(2)]
    keep = place(2 * SK).rearrange("p (b j) -> p b j", b=2)
    masks = [place(2 * SK // 2).bitcast(BF16).rearrange("p (b j) -> p b j", b=2) for _ in range(2)]
    ctx_rows = place(4 * D).rearrange("p (t n) -> p t n", t=4)
    ctx_t = place(DK * 4 * P).rearrange("p (k n) -> p k n", k=DK)
    kv = place(4 * 2 * D).rearrange("p (t n) -> p t n", t=4)
    k_rot = place(4 * D).rearrange("p (t n) -> p t n", t=4)
    k_swap = place(4 * D).rearrange("p (t n) -> p t n", t=4)
    k_s = k_swap.rearrange("p t n -> p (t n)").bitcast(F16).rearrange("p (t h s c) -> p t h s c", t=4, h=8, s=2)
    k_t = place(4 * 2 * SK // 2).bitcast(F16).rearrange("p (m b j) -> p m b j", m=4, b=2)
    xn = place(D)
    xn_t = place(DK * P).rearrange("p (k n) -> p k n", k=DK)
    q_both = place(2 * D)
    q_nat, q_swap = q_both[:, 0:D], q_both[:, D:2 * D]
    q_rot = place(D)
    q_s = q_both.bitcast(F16).rearrange("p (s h r c) -> p s h r c", s=2, h=8, r=2)
    q_t = [place(4 * 2 * 2 * SQ // 2).bitcast(F16).rearrange("p (m b a i) -> p m b a i", m=4, b=2, a=2)
           for _ in range(2)]
    probs = [place(8 * SK).rearrange("p (s j) -> p s j", s=8) for _ in range(2)]
    probs_s = halves(4, 4 * P)
    v_s = [halves(4, D) for _ in range(2)]
    heads_out = [place(8 * HC).rearrange("p (h c) -> p h c", h=8) for _ in range(2)]
    heads_t = place(2 * 2 * SQ).rearrange("p (a b i) -> p a b i", a=2, b=2)
    neg_max = [place(8) for _ in range(2)]
    row_sum = [place(8) for _ in range(2)]
    row_inv = place(8)
    x1 = place(D)
    x1n = place(D)
    x1n_s = halves(DK, P)
    g_v_s = halves(1, D)
    gate = place(D)
    gate_e = place(D)
    gate_i = place(D)
    low_t = place(P)
    kg_abs = place(P)
    kg_min = place(P)
    kg_exp = place(P)
    kg_ln = place(P)
    log_gate = place(P)
    cum = place(2 * SQ).rearrange("p (b i) -> p b i", b=2)
    ref = place(2 * NCH).rearrange("p (b c) -> p b c", b=2)
    q_dec = place(2 * SQ)
    k_dec = place(NCH * 2 * SQ).rearrange("p (c b i) -> p c b i", c=NCH, b=2)
    qs_t = place(2 * SQ)
    q_heads = place(2 * NCH * 4 * CH).rearrange("p (b c h t) -> p b c h t", b=2, c=NCH, h=4)
    k_heads = place(NCH * 2 * SQ).rearrange("p (c b i) -> p c b i", c=NCH, b=2)
    a_t = w_gvg.rearrange("p k n -> p (k n)").rearrange("p (r h c t) -> p r h c t", r=4, h=4, c=NCH)
    a_s = [h.rearrange("p r (h c t) -> p r h c t", h=4, c=NCH) for h in halves(4, 4 * NCH * CH)]
    g_out = place(D)
    g_sq = place(D)
    g_norm = place(D)
    g_norm_t = place(DK * P).rearrange("p (k n) -> p k n", k=DK)
    g_stat = place(4 * H).rearrange("p (k h) -> p k h", k=4)
    x2n = [place(D) for _ in range(2)]
    x2n_s = [w_gqk[:, k, :] for k in range(2)]
    x2n_t = place(DK * P).rearrange("p (k n) -> p k n", k=DK)
    stats = [place(10) for _ in range(3)]

    warena = [0]

    def place2(n):
        warena[0] += n
        assert warena[0] <= 8900
        return work[:, warena[0] - n:warena[0]]

    ident_h = place2(P // 2).bitcast(F16)
    e_rows = place2(2 * D).rearrange("p (a d) -> p a d", a=2)
    e_rows_t = [place2(2 * DK * R // 2).bitcast(F16).rearrange("p (m n) -> p m n", n=R) for _ in range(2)]
    e_silu = place2(HALF)
    e_hid = place2(HALF)
    e_hid_s = [place2(HT * R // 2).bitcast(F16).rearrange("p (c n) -> p c n", c=HT) for _ in range(2)]
    e_y = place2(2 * D).rearrange("p (a d) -> p a d", a=2)
    stage_rows = [place2(D) for _ in range(2)] + [experts[:, NE, EW - (k + 1) * D:EW - k * D] for k in range(2)]
    w_raw = [place2(2 * HID) for _ in range(2)] + \
        [experts[:, NE - 1, k * 2 * HID:(k + 1) * 2 * HID] for k in range(3)] + \
        [experts[:, NE, k * 2 * HID:(k + 1) * 2 * HID] for k in range(2)]
    w_tok = place2(TOPK * NTILE).rearrange("p (c t) -> p c t", c=TOPK)
    slot_i = place2(TOPK * NTILE).bitcast(U32).rearrange("p (c t) -> p c t", c=TOPK)
    tile_e = place2(NT).bitcast(I32)
    experts_h = experts[:, :, :].bitcast(F16)
    results = experts[:, 1:, :].rearrange("p e n -> p (e n)")[:, 0:3 * NTILE * D]\
        .rearrange("p (c t d) -> p c t d", c=3, t=NTILE)
    rt = [0]

    def place3(n):
        rt[0] += n
        assert rt[0] <= EW - 2 * D
        return experts[:, NE, rt[0] - n:rt[0]]

    L = NTILE * NE
    te = lambda a: a.rearrange("p (t e) -> p t e", e=NE)
    et = lambda a: a.rearrange("p (e t) -> p e t", e=NE)
    r_z, r_e, r_p, r_c, r_eq = (te(place3(L)) for _ in range(5))
    r_oh = [te(place3(L)) for _ in range(TOPK)]
    r_sel = te(place3(L))
    r_in, r_tot = te(place3(L)), te(place3(L))
    r_cum, r_pos = te(place3(L)), te(place3(L))
    r_m = place3(6 * NTILE).rearrange("p (k t) -> p k t", k=6)
    r_n = place3(6 * NE).rearrange("p (k e) -> p k e", k=6)
    r_ni = place3(NE).bitcast(I32)
    r_t = place3(NSLOT * NE).rearrange("p (j e) -> p j e", e=NE)
    r_tf = place3(NSLOT)
    r_bias = place3(NE)
    r_ones = place3(P)

    ps = stack.enter_context(nc.psum_tensor("ps", [P, 8, 512], F32))
    ps_flat = ps[:, :, :].rearrange("p b n -> p (b n)")
    bank_ta, bank_tb, bank_ma, bank_mb = (ps[:, k, :] for k in range(4, 8))

    def probs_bank(b, r):
        return (bank_ma, bank_mb)[r % 2] if b == 0 else ps[:, r, :]

    S = {}
    for name in """
        cleared mask_step
        consts_loaded weights_loaded waits_met fill_ready slots_filled ctx_loaded ctx_turned
        ctx_t_ready kv_done kv_ready k_prod_ready k_swap_ready k_rot_ready k_turned k_t_ready x_stat_ready
        norm_log x_rstd_ready xn_ready xn_turned xn_t_ready q_done q_nat_ready q_prod_ready q_swap_ready
        q_rot_ready q_turned q_t_ready masks_ready x_res_ready norm_sums scores_done max_ready
        exp_done probs_turned probs_hi_ready probs_lo_ready v_split v_hi_ready a_hi_ready k_hi_ready k_split q_hi_ready q_split q_lo_t_ready g_v_hi_ready av_done inv_ready av_ready
        heads_turned heads_t_ready proj_done x1_ready  x1_stat_ready  x1_rstd_ready x1n_ready
        x1n_turned x1n_hi_ready x1n_lo_ready vg_done g_v_ready gate_ready qkl_done low_t_ready kg_done
        kg_abs_ready kg_min_ready gate_inv gate_silu kg_step  dec_ready dec_k_step
         dec_exp_q dec_exp_k qs_ready q_heads_ready k_heads_ready a_done a_ready go_done go_ready gs_var
        gs_log gs_rstd gn_step  gn_turned gn_t_ready gproj_done x2_ready  x2_stat_ready
         x2_rstd_ready x2n_ready x2n_turned x2n_t_ready logits_done logits_ready x2n_split
        shared_loaded shared_hi shared_lo chunk_hi_ready chunk_lo_ready gate_done hid_hi_ready
        hid_lo_ready route_step route_exp route_mm table_ready rows_turned rows_t_ready up_done
        silu_ready hid_ready down_done y_ready a_split gla_hi_ready gla_lo_ready gs_step decay_step
        gate_step sum_step last_store first_shared_loaded rows_loaded y_stored
        last_shared_loaded
    """.split():
        S[name] = sem(name)
    x_loaded = [sem(f"x_loaded{k}") for k in range(2)]
    pad_loaded = [sem(f"pad_loaded{k}") for k in range(2)]
    x2n_stored = [sem(f"x2n_stored{k}") for k in range(2)]
    staged = [sem(f"staged{k}") for k in range(4)]
    scattered = [sem(f"scattered{k}") for k in range(4)]
    chunk_loaded = [sem(f"chunk_loaded{k}") for k in range(5)]
    group_loaded = [sem(f"group_loaded{k}") for k in range(NTILE // GROUP)]

    pairs = x.rearrange("(q b) s d -> q (b s) d", b=2)
    ctx_pairs = ctx_in.rearrange("(q b) (t p) d -> q p (b t) d", b=2, p=P)
    pad_pairs = pad.rearrange("(q b) j -> q (b j)", b=2)
    out_tiles = out.rearrange("(q b) s d -> q (b s) d", b=2)
    token_in_t, token_out_t, slot_in_t = (a.rearrange("(t p) d -> t p d", p=P) for a in
                                          (token_in, token_out, slot_in))
    tokens, token_results, slots, slot_results = (a.rearrange("(t a p) d -> t p a d", a=2, p=P) for a in
                                                  (token_in, token_out, slot_in, slot_out))

    def over_pairs(eng, first, body, last, third=None):
        first(Step(0, 0))
        body(Step(0, 1))
        (third or body)(Step(0, 2))
        with eng.Fori(1, (NPAIR - 2) // 2) as i:
            body(Step(i, 1))
            body(Step(i, 2))
        last(Step(0, NPAIR - 1))

    block = stack.enter_context(nc.Block())

    def apart(eng):
        eng.sem_inc(S["waits_met"], 1)

    @block.sync
    def _(sp):
        sp.dma_start(cst[:, :], consts_in).then_inc(S["consts_loaded"], 16)

        def load_x(j):
            wait(sp, S["x_res_ready"], j.n(1, -1))
            wait(sp, S["xn_ready"], j.n(1, -1))
            apart(sp)
            sp.dma_start(x_in[j.par], pairs[j.n(1)]).then_inc(x_loaded[j.par], 16)
            wait(sp, S["mask_step"], j.n(2, -3))
            apart(sp)
            sp.dma_start(pad_in[j.par].rearrange("p b j -> p (b j)"),
                         pad_pairs[j.n(1)].partition_broadcast(P)).then_inc(pad_loaded[j.par], 16)

        def load_ctx(j):
            wait(sp, S["ctx_turned"], j.n(2))
            apart(sp)
            sp.dma_start(ctx_rows, ctx_pairs[j.n(1)]).then_inc(S["ctx_loaded"], 16)

        def store_x2n(g):
            wait(sp, S["x2n_split"], g.n(2, 2))
            apart(sp)
            sp.dma_start(token_in_t[g.n(1)], x2n_s[g.par]).then_inc(x2n_stored[g.par], 16)

        load_ctx(Step(0, 0))
        load_x(Step(0, 0))
        load_x(Step(0, 1))
        wl = S["weights_loaded"]

        def kmaj(w):
            return w.rearrange("(k p) n -> p k n", p=P)

        count = [0]

        def wload(dst, src):
            sp.dma_start(dst, src).then_inc(wl, 16)
            count[0] += 1

        wload(w_kv[:, :, 0:D], kmaj(xWk))
        wload(w_kv[:, :, D:2 * D], kmaj(xWv))
        wload(w_q, kmaj(xWq))
        for hp in range(8):
            for a in range(2):
                row = (2 * hp + a) * HC
                wload(w_o[hp * HC:(hp + 1) * HC, a, :], xWo[row:row + HC, :])
        wload(w_gqk[:, :, 0:P], kmaj(gWq))
        wload(w_gqk[:, :, P:2 * P], kmaj(gWk))
        wload(w_g1, kmaj(gWg1))
        wload(w_g2[0:16, :], gWg2)
        wload(w_gvg[:, :, 0:D], kmaj(gWv))
        wload(w_gvg[:, :, D:2 * D], kmaj(gWg))
        wload(w_go, kmaj(gWo))
        wload(w_r, kmaj(Wr))
        wload(b_kv[:, 0:D], xbk.partition_broadcast(P))
        wload(b_kv[:, D:2 * D], xbv.partition_broadcast(P))
        wload(b_q, xbq.partition_broadcast(P))
        wload(b_o, xbo.partition_broadcast(P))
        wload(b_g, gbg.partition_broadcast(P))
        assert count[0] == WEIGHT_DMAS
        load_ctx(Step(0, 1))

        def step(p, nxt2=True):
            if nxt2:
                load_x(p.next(2))
                load_ctx(p.next(2))
            store_x2n(p.next(-1))

        def first(p):
            load_x(p.next(2))
            load_ctx(p.next(2))

        first(Step(0, 0))
        step(Step(0, 1))
        step(Step(0, 2))
        with sp.Fori(1, (NPAIR - 4) // 2) as i:
            step(Step(i, 1))
            step(Step(i, 2))
        step(Step(0, NPAIR - 3))
        step(Step(0, NPAIR - 2), False)
        step(Step(0, NPAIR - 1), False)
        store_x2n(Step(0, NPAIR - 1))

        sp.wait_ge(x2n_stored[0], 16 * NPAIR // 2)
        sp.wait_ge(x2n_stored[1], 16 * NPAIR // 2)
        sp.wait_ge(S["logits_ready"], NPAIR)

        def load_rows(t, rows):
            wait(sp, S["rows_turned"], t)
            apart(sp)
            sp.dma_start(e_rows, rows).then_inc(S["rows_loaded"], 16)

        def stage(t):
            if t >= 4:
                sp.wait_ge(scattered[t % 4], 32 * (t // 4))
            sp.dma_start(stage_rows[t % 4], token_in_t[t]).then_inc(staged[t % 4], 16)

        def store_y(t, rows):
            wait(sp, S["y_ready"], t + 1)
            apart(sp)
            sp.dma_start(rows, e_y).then_inc(S["y_stored"], 16)

        sp.dma_start(r_bias, rbias.partition_broadcast(P)).then_inc(S["consts_loaded"], 16)
        load_rows(0, tokens[0])
        for t in range(NTILE):
            stage(t)
        for k in range(4):
            sp.wait_ge(scattered[k], 32 * (NTILE // 4))
        for t in range(FIRST, FIRST + 3):
            load_rows(t, slots[t - FIRST])
        store_y(FIRST - 1, token_results[FIRST - 1])
        with sp.Fori(FIRST + 3, MID) as t:
            load_rows(t, slots[t - FIRST])
            store_y(t - 3, slot_results[t - (FIRST + 3)])
        for t in range(MID, NT + 3):
            if t < NT:
                load_rows(t, tokens[t - NSLOT])
            store_y(t - 3, slot_results[t - 3 - FIRST] if t - 3 < MID else token_results[t - 3 - NSLOT])

        sp.wait_ge(S["y_stored"], 16 * NT)
        sp.dma_start(results[:, 2, 2 * FIRST:, :], token_out_t[2 * FIRST:].rearrange("t p d -> p t d"))\
            .then_inc(S["last_shared_loaded"], 16)
        for m in range(NTILE // GROUP):
            tiles = slice(m * GROUP, (m + 1) * GROUP)
            sp.wait_ge(S["sum_step"], (1 + TOPK) * (m + 1))
            sp.dma_start(out_tiles[tiles].rearrange("t p d -> p t d"), x2_all[:, tiles, :])\
                .then_inc(S["last_store"], 16)
        sp.wait_ge(S["last_store"], 16 * NTILE // GROUP)

    @block.gpsimd
    def _(pool):
        zeros = experts[:, 0, 0:8 * D].rearrange("p (t d) -> p t d", t=8)
        nc.gpsimd.memset(zeros, 0.0).then_inc(S["fill_ready"], 1)
        nc.gpsimd.memset(experts[:, 1, EW - D:], 0.0).then_inc(S["fill_ready"], 1)
        pool.wait_ge(S["consts_loaded"], 16)
        nc.gpsimd.tensor_copy(ident_bf, ident).then_inc(S["fill_ready"], 1)
        nc.gpsimd.tensor_copy(ident_h1, ident).then_inc(S["fill_ready"], 1)
        pool.wait_ge(S["fill_ready"], 4)

        def fill_slots():
            for t in range(0, 2 * NSLOT, 8):
                m = min(8, 2 * NSLOT - t)
                pool.dma_start(slot_in_t[t:t + m].rearrange("t p d -> p t d"), zeros[:, 0:m, :])\
                    .then_inc(S["slots_filled"], 16)

        def load_shared():
            w, s = experts[:, 1, :], S["shared_loaded"]
            up = w[:, 0:EW_UP].rearrange("p (k c n) -> p k c n", k=DK, c=2)
            down = w[:, EW_UP:].rearrange("p (c n) -> p c n", c=HT)
            main = (HT - 1) * P
            pool.dma_start(up[:, :, 0, :], sgate.rearrange("(k p) n -> p k n", p=P)).then_inc(s, 16)
            pool.dma_start(up[:, :, 1, :], sup.rearrange("(k p) n -> p k n", p=P)).then_inc(s, 16)
            pool.dma_start(down[:, 0:HT - 1, :], sdown[0:main, :].rearrange("(c p) n -> p c n", p=P)).then_inc(s, 16)
            pool.dma_start(down[0:HR, HT - 1, :], sdown[main:, :]).then_inc(s, 16)

        def split_x2(g):
            wait(pool, S["x2n_ready"], g.n(1, 1))
            wait(pool, x2n_stored[g.par], g.half * 16)
            apart(pool)
            both = x2n_s[g.par].bitcast(F16)
            nc.gpsimd.tensor_scalar(both[:, 0:D], x2n[g.par], 1.0, None, ALU.mult).then_inc(S["x2n_split"], 1)
            wait(pool, S["x2n_split"], g.n(2, 1))
            nc.gpsimd.tensor_tensor(both[:, D:2 * D], x2n[g.par], both[:, 0:D], ALU.subtract)\
                .then_inc(S["x2n_split"], 1)

        def masks_of(j):
            wait(pool, pad_loaded[j.par], j.half * 16 + 16)
            wait(pool, S["scores_done"], j.n(2, -2))
            wait(pool, S["masks_ready"], j.n(1))
            apart(pool)
            nc.gpsimd.tensor_scalar(keep, pad_in[j.par], -1.0, 1.0, ALU.mult, ALU.add).then_inc(S["mask_step"], 1)
            wait(pool, S["mask_step"], j.n(2, 1))
            nc.gpsimd.tensor_tensor(keep, keep, bc(const("causal"), 1, 2), ALU.mult).then_inc(S["mask_step"], 1)
            wait(pool, S["mask_step"], j.n(2, 2))
            apart(pool)
            nc.gpsimd.tensor_scalar(masks[j.par], keep, -NEG, NEG, ALU.mult, ALU.add).then_inc(S["masks_ready"], 1)

        def rope_k(j):
            kb = kv
            wait(pool, S["kv_ready"], j.n(4, 4))
            wait(pool, S["k_turned"], j.n(2))
            sin = const("sink").rearrange("p (t i e) -> p t i e", t=2, e=2)
            for b in range(2):
                for e in range(2):
                    for t in range(2):
                        src = kb[:, 2 * b + t, 0:D].rearrange("p (h i e) -> p h i e", h=H, e=2)
                        dst = k_swap[:, 2 * b + t, :].rearrange("p (h i e) -> p h i e", h=H, e=2)
                        ins = nc.gpsimd.tensor_tensor(dst[:, :, :, e], src[:, :, :, 1 - e],
                                                      bc(sin[:, t, :, e], 1, H), ALU.mult)
            ins.then_inc(S["k_swap_ready"], 1)

        def split_v(j):
            wait(pool, S["v_hi_ready"], j.n(1, 1))
            high, low = v_s[j.par]
            nc.gpsimd.tensor_tensor(low, kv[:, :, D:2 * D], high, ALU.subtract).then_inc(S["v_split"], 1)

        def split_k(j):
            wait(pool, S["k_hi_ready"], j.n(1, 1))
            nc.gpsimd.tensor_tensor(k_s[:, :, :, 1, :], k_rot.rearrange("p t (h c) -> p t h c", h=8),
                                    k_s[:, :, :, 0, :], ALU.subtract).then_inc(S["k_split"], 1)

        def split_a(g):
            wait(pool, S["a_hi_ready"], g.n(1, 1))
            nc.gpsimd.tensor_tensor(a_s[1], a_t, a_s[0], ALU.subtract).then_inc(S["a_split"], 1)

        def rope_q(j):
            wait(pool, S["q_nat_ready"], j.n(1, 1))
            wait(pool, S["q_turned"], j.n(1))
            sin = const("sinq").rearrange("p (i e) -> p i e", e=2)
            src = q_nat.rearrange("p (h i e) -> p h i e", h=H, e=2)
            dst = q_swap.rearrange("p (h i e) -> p h i e", h=H, e=2)
            for e in range(2):
                ins = nc.gpsimd.tensor_tensor(dst[:, :, :, e], src[:, :, :, 1 - e], bc(sin[:, :, e], 1, H), ALU.mult)
            ins.then_inc(S["q_swap_ready"], 1)

        def residual(p):
            wait(pool, x_loaded[p.par], p.half * 16 + 16)
            wait(pool, S["x1_ready"], p.n(1))
            nc.gpsimd.tensor_tensor(x_res, x_in[p.par], b_o, ALU.add).then_inc(S["x_res_ready"], 1)

        def step(p, nxt=True, gla=True):
            residual(p)
            if nxt:
                masks_of(p.next())
                rope_k(p.next())
            if gla:
                split_a(p.next(-1))
            if nxt:
                split_k(p.next())
                rope_q(p.next())
                split_v(p.next())
            if gla:
                split_x2(p.next(-1))

        pool.wait_ge(S["weights_loaded"], 16 * WEIGHT_DMAS)
        masks_of(Step(0, 0))
        rope_k(Step(0, 0))
        split_k(Step(0, 0))
        rope_q(Step(0, 0))
        split_v(Step(0, 0))

        def first(p):
            step(p, gla=False)
            load_shared()
            fill_slots()

        over_pairs(pool, first, step, lambda p: step(p, False))
        split_a(Step(0, NPAIR - 1))
        split_x2(Step(0, NPAIR - 1))

        pool.wait_ge(S["slots_filled"], 16 * N_FILL)
        pool.wait_ge(S["table_ready"], 1)
        for t in range(NTILE):
            pool.wait_ge(staged[t % 4], 16 * (t // 4 + 1))
            for c in range(TOPK):
                pool.indirect_dma_start(
                    out=slot_in, out_offset=bass.IndirectOffsetOnAxis(ap=slot_i[:, c, t:t + 1], axis=0),
                    in_=stage_rows[t % 4], in_offset=None).then_inc(scattered[t % 4], 16)
        pool.wait_ge(S["y_stored"], 16 * MID)
        pool.wait_ge(S["down_done"], MID)
        pool.dma_start(results[:, 2, 0:2 * FIRST, :], token_out_t[0:2 * FIRST].rearrange("t p d -> p t d"))\
            .then_inc(S["first_shared_loaded"], 16)
        for m in range(NTILE // GROUP):
            for t in range(m * GROUP, (m + 1) * GROUP):
                for c in range(TOPK):
                    pool.indirect_dma_start(
                        out=results[:, c, t, :], out_offset=None, in_=slot_out,
                        in_offset=bass.IndirectOffsetOnAxis(ap=slot_i[:, c, t:t + 1], axis=0))\
                        .then_inc(group_loaded[m], 16)

    @block.tensor
    def _(pe):
        def turn(bank, src, done):
            n = len(src)
            for k, a in enumerate(src):
                ins = pe.transpose(bank[:, k * P:(k + 1) * P], a, ident)
            ins.then_inc(done, 1)

        def product(bank, lhs, rhs, done):
            for k in range(len(lhs)):
                ins = pe.matmul(bank, lhs[k], rhs[k], start=(k == 0), stop=(k == len(lhs) - 1))
            if done is not None:
                ins.then_inc(done, 1)

        def split_product(bank, lhs, rhs, done):
            for k in range(len(lhs[0])):
                for a, b in ((0, 0), (0, 1), (1, 0)):
                    ins = pe.matmul(bank, lhs[a][k], rhs[b][k], start=(k == 0 and a + b == 0),
                                    stop=(k == len(lhs[0]) - 1 and a == 1))
            if done is not None:
                ins.then_inc(done, 1)

        def blocks(halves, lo=None, hi=None):
            return [[h[:, k, lo:hi] for k in range(h.shape[1])] for h in halves]

        def turn_ctx(j):
            wait(pe, S["ctx_loaded"], j.n(16, 16))
            for k, bank in enumerate((bank_ma, bank_mb)):
                turn(bank, [ctx_rows[:, t, k * P:(k + 1) * P] for t in range(4)], S["ctx_turned"])

        def project_kv(j, t):
            wait(pe, S["ctx_t_ready"], j.n(2, 2))
            if t >= 2:
                wait(pe, S["kv_ready"], j.n(4, t - 1))
            bank = (bank_ma, bank_mb)[t % 2]
            product(bank, [ctx_t[:, k, t * P:(t + 1) * P] for k in range(DK)],
                    [w_kv[:, k, :] for k in range(DK)], S["kv_done"])

        def turn_k(j):
            wait(pe, S["k_split"], j.n(1, 1))
            for g, bank in enumerate((bank_tb, bank_mb)):
                out = bank.bitcast(F16)
                for m in range(2):
                    for t in range(4):
                        at = (4 * m + t) * P
                        ins = pe.transpose(out[:, at:at + P], k_s[:, t, 4 * g + 2 * m:4 * g + 2 * m + 2, :, :]
                                           .rearrange("p h s c -> p (h s c)"), ident_h1)
                ins.then_inc(S["k_turned"], 1)

        def turn_xn(j):
            wait(pe, S["xn_ready"], j.n(1, 1))
            turn(bank_ta, [xn[:, k * P:(k + 1) * P] for k in range(DK)], S["xn_turned"])

        def project_q(j):
            wait(pe, S["xn_t_ready"], j.n(1, 1))
            product(bank_ta[:, 0:D], [xn_t[:, k, :] for k in range(DK)], [w_q[:, k, :] for k in range(DK)],
                    S["q_done"])

        def turn_q(j):
            wait(pe, S["q_split"], j.n(1, 1))
            out = bank_ta.bitcast(F16)
            for s in range(2):
                for m in range(4):
                    at = (4 * s + m) * P
                    ins = pe.transpose(out[:, at:at + P],
                                       q_s[:, s, 2 * m:2 * m + 2, :, :].rearrange("p h r c -> p (h r c)"), ident_h1)
            ins.then_inc(S["q_turned"], 1)

        def scores(p, b):
            wait(pe, S["masks_ready"], p.n(1, 1))
            wait(pe, S["k_t_ready"], p.n(2, 2))
            wait(pe, S["q_lo_t_ready"], p.n(1, 1))
            for r in range(4):
                pe.matmul(ps[:, r, :].rearrange("p (g j) -> p g j", g=2), ident_bf, bc(masks[p.par][:, b, :], 1, 2),
                          start=True, stop=False)
            for g in range(2):
                for r in range(4):
                    hp = 4 * g + r
                    m, row = hp // 2, 64 * (hp % 2)
                    for part, n in ((0, 64), (1, 32)):
                        ins = pe.matmul(ps[:, r, g * SK:(g + 1) * SK],
                                        q_t[part][row:row + n, m, b, :, :].rearrange("p a i -> p (a i)"),
                                        k_t[row:row + n, m, b, :], start=False, stop=(g == 1 and part == 1))
            ins.then_inc(S["scores_done"], 1)

        def turn_probs(p, b, kv_ready=0):
            for r in range(4):
                if r == 1:
                    wait(pe, S["kv_ready"], kv_ready)
                wait(pe, S["exp_done"], p.n(16, 8 * b + 2 * r + 2))
                if b == 0 and r >= 2:
                    wait(pe, S["probs_lo_ready"], p.n(8, 4 * b + r - 1))
                turn(probs_bank(b, r),
                     [probs[b][:, 2 * r + g, t * P:(t + 1) * P] for g in range(2) for t in range(2)],
                     S["probs_turned"])

        def weigh_values(p, b, bank):
            wait(pe, S["probs_lo_ready"], p.n(8, 4 * b + 4))
            wait(pe, S["v_split"], p.n(1, 1))
            for hp in range(8):
                g, r = hp // 4, hp % 4
                split_product(bank[:, hp * 32:hp * 32 + 32],
                              [[h[:, r, (2 * g + t) * P:(2 * g + t + 1) * P] for t in range(2)] for h in probs_s],
                              [[h[:, 2 * b + t, hp * 32:hp * 32 + 32] for t in range(2)] for h in v_s[p.par]],
                              S["av_done"] if hp == 7 else None)

        def turn_heads(p, b, bank):
            wait(pe, S["av_ready"], p.n(2, b + 1))
            turn(bank, [heads_out[b].rearrange("p h c -> p (h c)")], S["heads_turned"])

        def project_out(p):
            wait(pe, S["heads_t_ready"], p.n(2, 2))
            product(bank_ma[:, 0:D], [heads_t[:, a, :, :].rearrange("p b i -> p (b i)") for a in range(2)],
                    [w_o[:, a, :] for a in range(2)], S["proj_done"])

        def g_turn_x(g):
            wait(pe, S["x1n_ready"], g.n(1, 1))
            turn(bank_ta, [x1n[:, k * P:(k + 1) * P] for k in range(DK)], S["x1n_turned"])

        def g_project(g):
            wait(pe, S["x1n_lo_ready"], g.n(1, 1))
            wait(pe, S["gla_lo_ready"], 3)
            split_product(bank_tb, blocks(x1n_s), blocks(w_gvg_s), S["vg_done"])
            for c in range(2):
                split_product(bank_ta[:, c * P:(c + 1) * P], blocks(w_gqk_s, c * P, (c + 1) * P), blocks(x1n_s), None)
            split_product(bank_ta[0:16, 2 * P:3 * P], blocks(w_g1_s), blocks(x1n_s), S["qkl_done"])

        def g_gate(g):
            wait(pe, S["low_t_ready"], g.n(1, 1))
            wait(pe, S["g_v_ready"], g.n(1, 1))
            product(bank_tb[:, 0:P], [w_g2[0:16, :]], [low_t[0:16, :]], S["kg_done"])

        def g_scores(g):
            wait(pe, S["k_heads_ready"], g.n(1, 1))
            wait(pe, S["q_heads_ready"], g.n(1, 1))
            for r in range(4):
                q = slice(32 * r, 32 * r + 32)
                for b in range(2):
                    for c in range(NCH):
                        ins = pe.matmul(ps[SQ * b:SQ * b + SQ, r, c * 64:(c + 1) * 64], k_heads[q, c, b, :],
                                        q_heads[q, b, c, :, :].rearrange("p h t -> p (h t)"), start=True, stop=True)
            ins.then_inc(S["a_done"], 1)

        def g_values(g):
            wait(pe, S["a_split"], g.n(1, 1))
            wait(pe, S["g_v_ready"], g.n(1, 1))
            apart(pe)
            for b in range(2):
                rows = slice(SQ * b, SQ * b + SQ)
                for h in range(H):
                    split_product(bank_ma[rows, h * GV:(h + 1) * GV],
                                  [[a[rows, h // 4, h % 4, :, :].rearrange("p c t -> p (c t)")] for a in a_s],
                                  [[a[rows, 0, h * GV:(h + 1) * GV]] for a in g_v_s],
                                  S["go_done"] if (b, h) == (1, H - 1) else None)

        def g_turn_out(g):
            wait(pe, S["gn_step"], g.n(2, 2))
            turn(bank_ta, [g_norm[:, k * P:(k + 1) * P] for k in range(DK)], S["gn_turned"])

        def g_project_out(g):
            wait(pe, S["gn_t_ready"], g.n(1, 1))
            product(bank_mb[:, 0:D], [g_norm_t[:, k, :] for k in range(DK)], [w_go[:, k, :] for k in range(DK)],
                    S["gproj_done"])

        def g_turn_x2(g):
            wait(pe, S["x2n_ready"], g.n(1, 1))
            turn(bank_mb, [x2n[g.par][:, k * P:(k + 1) * P] for k in range(DK)], S["x2n_turned"])

        def g_logits(g):
            wait(pe, S["x2n_t_ready"], g.n(1, 1))
            product(bank_mb[:, 0:NE], [x2n_t[:, k, :] for k in range(DK)], [w_r[:, k, :] for k in range(DK)],
                    S["logits_done"])

        def step(p, nxt=True, gla=True, att=True):
            g, j = p.next(-1), p.next()
            if att:
                wait(pe, S["probs_lo_ready"], p.n(8))
                scores(p, 0)
            if gla:
                wait(pe, S["probs_lo_ready"], p.n(8))
                wait(pe, S["q_lo_t_ready"], p.n(1, 1 if att else 0))
                g_turn_x(g)
            if nxt:
                wait(pe, S["av_ready"], p.n(2))
                wait(pe, S["logits_ready"], g.n(1))
                wait(pe, S["x1_ready"], p.n(1))
                turn_ctx(j)
            if gla:
                wait(pe, S["heads_t_ready"], p.n(2))
                g_project(g)
            if nxt:
                project_kv(j, 0)
            if gla:
                g_gate(g)
            if nxt:
                for t in range(1, 4):
                    project_kv(j, t)
            if att:
                wait(pe, S["kv_ready"], (j if nxt else p).n(4, 3))
                wait(pe, S["av_ready"], p.n(2))
                wait(pe, S["x1_ready"], p.n(1))
                wait(pe, S["q_lo_t_ready"], p.n(1, 1))
                if gla:
                    wait(pe, S["logits_ready"], g.n(1))
                turn_probs(p, 0, (j if nxt else p).n(4, 4))
            if gla:
                if att:
                    wait(pe, S["exp_done"], p.n(16, 8))
                else:
                    wait(pe, S["probs_lo_ready"], p.n(8))
                g_scores(g)
            if nxt:
                wait(pe, S["k_heads_ready"], p.n(1))
                wait(pe, S["q_nat_ready"], p.n(1, 1))
                turn_xn(j)
            if att:
                weigh_values(p, 0, bank_mb)
                wait(pe, S["exp_done"], p.n(16, 8))
                wait(pe, S["a_ready"], p.n(4))
                scores(p, 1)
            if nxt:
                project_q(j)
            if gla:
                if not att:
                    wait(pe, S["logits_ready"], g.n(1))
                    wait(pe, S["av_ready"], p.n(2))
                g_values(g)
            if att:
                wait(pe, S["go_ready"], p.n(1))
                turn_heads(p, 0, bank_ma)
            if nxt:
                wait(pe, S["av_ready"], p.n(2, 1))
                wait(pe, S["kg_abs_ready"], p.n(1))
                turn_k(j)
            if att:
                turn_probs(p, 1)
            if gla:
                if nxt:
                    wait(pe, S["q_nat_ready"], j.n(1, 1))
                g_turn_out(g)
            if att:
                wait(pe, S["heads_t_ready"], p.n(2, 1))
                weigh_values(p, 1, bank_ma)
            if nxt:
                wait(pe, S["gn_t_ready"], p.n(1))
                turn_q(j)
            if gla:
                if nxt:
                    wait(pe, S["k_t_ready"], j.n(2, 2))
                elif att:
                    wait(pe, S["av_ready"], p.n(2, 1))
                else:
                    wait(pe, S["logits_ready"], g.n(1))
                g_project_out(g)
            if att:
                if nxt:
                    wait(pe, S["k_t_ready"], j.n(2, 1))
                else:
                    wait(pe, S["kg_abs_ready"], p.n(1))
                turn_heads(p, 1, bank_tb)
                wait(pe, S["av_ready"], p.n(2, 2))
                project_out(p)
            if gla:
                wait(pe, S["x2_ready"], g.n(1, 1))
                g_turn_x2(g)
                g_logits(g)

        pe.wait_ge(S["consts_loaded"], 16)
        pe.wait_ge(S["weights_loaded"], 16 * WEIGHT_DMAS)
        pe.wait_ge(S["fill_ready"], 4)
        zero = Step(0, 0)
        turn_ctx(zero)
        for t in range(4):
            project_kv(zero, t)
        turn_xn(zero)
        pe.wait_ge(S["kv_ready"], 4)
        turn_k(zero)
        project_q(zero)
        pe.wait_ge(S["q_nat_ready"], 1)
        turn_q(zero)
        over_pairs(pe, lambda p: step(p, gla=False), step, lambda p: step(p, nxt=False))
        step(Step(0, NPAIR), nxt=False, att=False)

        turned = ps[:, 0, :].bitcast(F16)

        def turn_rows(t):
            wait(pe, S["rows_loaded"], t * 16 + 16)
            wait(pe, S["rows_t_ready"], t)
            rows = e_rows.rearrange("p a d -> p (a d)").bitcast(F16)
            for m in range(2 * DK):
                for a in range(2):
                    ins = pe.transpose(turned[:, m * R + a * P:m * R + (a + 1) * P],
                                       rows[:, (a * 2 * DK + m) * P:(a * 2 * DK + m + 1) * P], ident_h)
            ins.then_inc(S["rows_turned"], 1)

        def up(t, k, e, half):
            wait(pe, S["rows_t_ready"], t + 1)
            for part, (free, done) in enumerate((("silu_ready", "gate_done"), ("hid_ready", "up_done"))):
                wait(pe, S[free], t * 2 + half)
                for c in range(half * HT // 2, (half + 1) * HT // 2):
                    for kk in range(DK):
                        for a, b in ((0, 0), (0, 1), (1, 0)):
                            at = a * EW + (2 * kk + part) * HID + c * P
                            ins = pe.matmul(ps[:, 1 + 3 * part + c // 2, (c % 2) * R:(c % 2 + 1) * R],
                                            experts_h[:, e, at:at + P], e_rows_t[k][:, b * DK + kk, :],
                                            start=(kk == 0 and a + b == 0), stop=(kk == DK - 1 and a == 1))
                ins.then_inc(S[done], 1)

        def down(t, e):
            wait(pe, S["hid_lo_ready"], t * 2 + 2)
            wait(pe, S["y_ready"], t)
            for r in range(2):
                for c in range(HT):
                    n = P if c < HT - 1 else HR
                    for a, b in ((0, 0), (0, 1), (1, 0)):
                        at = b * EW + EW_UP + c * D
                        ins = pe.matmul(ps[:, 7, r * D:(r + 1) * D], e_hid_s[a][0:n, c, r * P:(r + 1) * P],
                                        experts_h[0:n, e, at:at + D],
                                        start=(c == 0 and a + b == 0), stop=(c == HT - 1 and a == 1))
            ins.then_inc(S["down_done"], 1)

        pe.wait_ge(S["shared_lo"], 1)
        pe.wait_ge(S["cleared"], 3)
        pe.wait_ge(S["a_ready"], 4 * NPAIR)
        pe.wait_ge(S["x2n_t_ready"], NPAIR)
        pe.wait_ge(S["gn_t_ready"], NPAIR)
        pe.wait_ge(S["logits_ready"], NPAIR)
        turn_rows(0)
        up(0, 0, 0, 0)
        pe.wait_ge(S["route_step"], ROUTE_SELECTED)
        sel = r_sel.rearrange("p t e -> p (t e)")
        pe.matmul(bank_mb[:, L:2 * L], const("upper"), sel, start=True, stop=True).then_inc(S["route_mm"], 1)
        pe.matmul(bank_mb[:, 0:L], r_ones, sel, start=True, stop=True).then_inc(S["route_mm"], 1)

        turn_rows(1)
        up(0, 0, 0, 1)
        pe.wait_ge(S["route_step"], ROUTE_SELECTED + 6)

        def tile(t, k, e, e_before):
            up(t, k, e, 0)
            down(t - 1, e_before)
            turn_rows(t + 1)
            up(t, k, e, 1)

        tile(1, 1, 0, 0)
        with pe.Fori(1, FIRST // 2) as i:
            tile(i * 2, 0, 0, 0)
            tile(i * 2 + 1, 1, 0, 0)
        pe.wait_ge(S["chunk_lo_ready"], NCHUNK * NE)
        with pe.Fori(FIRST // 2, NT // 2 - 1) as i:
            e = [pe.value_load(tile_e[0:1, bass.ds(i * 2 + m, 1)], min_val=0, max_val=NE) for m in range(-1, 2)]
            tile(i * 2, 0, e[1], e[0])
            tile(i * 2 + 1, 1, e[2], e[1])
        tile(NT - 2, 0, 0, 0)
        up(NT - 1, 1, 0, 0)
        down(NT - 2, 0)
        up(NT - 1, 1, 0, 1)
        down(NT - 1, 0)

    @block.scalar
    def _(act):
        def copy(dst, src, done):
            nc.scalar.activation(dst, src, ACT.Copy).then_inc(done, 1)

        def rstd(k, which, n, m):
            wait(act, S[which + "_stat_ready"], n)
            nc.scalar.activation(stats[k][:, 8:9], stats[k][:, 7:8], ACT.Ln, bias=const("eps"))\
                .then_inc(S["norm_log"], 1)
            wait(act, S["norm_log"], m)
            nc.scalar.activation(stats[k][:, 9:10], stats[k][:, 8:9], ACT.Exp, scale=-0.5)\
                .then_inc(S[which + "_rstd_ready"], 1)

        def ctx_copies(j):
            for k, bank in enumerate((bank_ma, bank_mb)):
                wait(act, S["ctx_turned"], j.n(2, k + 1))
                copy(ctx_t[:, k, :], bank, S["ctx_t_ready"])

        def k_high(j):
            wait(act, S["k_rot_ready"], j.n(1, 1))
            nc.scalar.activation(k_s[:, :, :, 0, :], k_rot.rearrange("p t (h c) -> p t h c", h=8), ACT.Copy)\
                .then_inc(S["k_hi_ready"], 1)

        def v_high(j):
            wait(act, S["kv_ready"], j.n(4, 4))
            wait(act, S["av_done"], j.n(2, -2))
            copy(v_s[j.par][0], kv[:, :, D:2 * D], S["v_hi_ready"])

        def q_high(j):
            wait(act, S["q_rot_ready"], j.n(1, 1))
            nc.scalar.activation(q_s[:, 0], bc(q_rot.rearrange("p (h c) -> p h c", h=8), 2, 2), ACT.Copy)\
                .then_inc(S["q_hi_ready"], 1)

        def q_low_turned(j):
            wait(act, S["q_t_ready"], j.n(1, 1))
            wait(act, S["scores_done"], j.n(2))
            src = bank_ta.bitcast(F16)[:, 4 * P:8 * P].rearrange("p (m b i) -> p m b i", m=4, b=2)
            for a in range(2):
                ins = nc.scalar.activation(q_t[1][:, :, :, a, :], src, ACT.Identity, scale=const("par")[:, a:a + 1])
            ins.then_inc(S["q_lo_t_ready"], 1)

        def k_copies(j):
            wait(act, S["scores_done"], j.n(2))
            for g, bank in enumerate((bank_tb, bank_mb)):
                wait(act, S["k_turned"], j.n(2, g + 1))
                copy(k_t[:, 2 * g:2 * g + 2, :, :].rearrange("p m b j -> p (m b j)"), bank.bitcast(F16),
                     S["k_t_ready"])

        def exps(p, b, r):
            wait(act, S["max_ready"], p.n(8, 4 * b + r + 1))
            wait(act, S["probs_turned"], p.n(8, 4 * b - 4))
            wait(act, S["inv_ready"], p.n(2, b - 1))
            for g in range(2):
                hp = 4 * g + r
                nc.scalar.activation(probs[b][:, 2 * r + g, :], ps[:, r, g * SK:(g + 1) * SK], ACT.Exp,
                                     bias=neg_max[b][:, hp:hp + 1], accum_out=row_sum[b][:, hp:hp + 1])\
                    .then_inc(S["exp_done"], 1)

        def probs_high(p, b, lo=0, hi=4):
            wait(act, S["av_done"], p.n(2, b))
            for r in range(lo, hi):
                wait(act, S["probs_turned"], p.n(8, 4 * b + r + 1))
                copy(probs_s[0][:, r, :], probs_bank(b, r), S["probs_hi_ready"])

        def heads_copy(p, b, bank):
            wait(act, S["heads_turned"], p.n(2, b + 1))
            wait(act, S["proj_done"], p.n(1))
            copy(heads_t[:, :, b, :], bank[:, 0:P].rearrange("p (a i) -> p a i", a=2), S["heads_t_ready"])

        def two_blocks(dst, bank, turned, n, done):
            wait(act, S[turned], n)
            copy(dst, bank[:, 0:D].rearrange("p (k n) -> p k n", k=DK), S[done])

        def step(p, nxt=True, gla=True, att=True):
            g, j = p.next(-1), p.next()
            if not nxt:
                act.sem_inc(S["norm_log"], 1)
            if gla:
                two_blocks(x1n_s[0], bank_ta, "x1n_turned", p.n(1), "x1n_hi_ready")
            if nxt:
                rstd(0, "x", j.n(1, 1), norm_count(p, 0))
                ctx_copies(j)
            if att:
                exps(p, 0, 0)
            if gla:
                wait(act, S["qkl_done"], p.n(1))
                nc.scalar.activation(low_t[0:16, :], bank_ta[0:16, 2 * P:3 * P], ACT.Copy, scale=1 / W_SCALE)\
                    .then_inc(S["low_t_ready"], 1)
            if att:
                for r in range(1, 4):
                    exps(p, 0, r)
            if gla:
                wait(act, S["kg_abs_ready"], p.n(1))
                nc.scalar.activation(kg_exp, kg_abs, ACT.Exp, scale=-1.0).then_inc(S["kg_step"], 1)
                wait(act, S["kg_step"], g.n(2, 1))
                nc.scalar.activation(kg_ln, kg_exp, ACT.Ln, bias=const("one")).then_inc(S["kg_step"], 1)
                wait(act, S["dec_ready"], p.n(1))
                nc.scalar.activation(q_dec, q_dec, ACT.Exp, scale=1.0 / GATE_NORM).then_inc(S["dec_exp_q"], 1)
                wait(act, S["dec_k_step"], g.n(2, 2))
                nc.scalar.activation(k_dec.rearrange("p c b i -> p (c b i)"), k_dec.rearrange("p c b i -> p (c b i)"),
                                     ACT.Exp, bias=const("lnscale"), scale=1.0 / GATE_NORM).then_inc(S["dec_exp_k"], 1)
            if att:
                probs_high(p, 0)
            if gla:
                wait(act, S["gate_ready"], p.n(1))
                nc.scalar.activation(gate_e, gate, ACT.Exp, scale=-1.0).then_inc(S["gate_step"], 1)
                wait(act, S["gate_step"], g.n(2, 1))
                nc.scalar.activation(gate_e, gate_e, ACT.Ln, bias=const("one")).then_inc(S["gate_step"], 1)
                wait(act, S["gate_step"], g.n(2, 2))
                wait(act, S["gn_step"], g.n(2, -1))
                nc.scalar.activation(gate_i, gate_e, ACT.Exp, scale=-1.0).then_inc(S["gate_inv"], 1)
                wait(act, S["a_ready"], g.n(4, 4))
                nc.scalar.activation(a_s[0], a_t, ACT.Copy).then_inc(S["a_hi_ready"], 1)
            if nxt:
                two_blocks(xn_t, bank_ta, "xn_turned", j.n(1, 1), "xn_t_ready")
                k_high(j)
            if att:
                exps(p, 1, 0)
            if gla:
                wait(act, S["go_done"], p.n(1))
                nc.scalar.activation(g_out, bank_ma[:, 0:D], ACT.Copy, scale=1 / (A_SCALE * V_SCALE))\
                    .then_inc(S["go_ready"], 1)
            if att:
                exps(p, 1, 1)
                heads_copy(p, 0, bank_ma)
                exps(p, 1, 2)
                exps(p, 1, 3)
            if gla:
                wait(act, S["gs_var"], p.n(1))
                nc.scalar.activation(g_stat[:, 2, :], g_stat[:, 1, :], ACT.Ln, bias=const("eps"), scale=1.0 / GV)\
                    .then_inc(S["gs_log"], 1)
                wait(act, S["gs_log"], p.n(1))
                nc.scalar.activation(g_stat[:, 3, :], g_stat[:, 2, :], ACT.Exp, scale=-0.5).then_inc(S["gs_rstd"], 1)
            if att:
                probs_high(p, 1, 0, 2)
            if nxt:
                q_high(j)
            if att:
                probs_high(p, 1, 2, 4)
            if gla:
                two_blocks(g_norm_t, bank_ta, "gn_turned", p.n(1), "gn_t_ready")
            if nxt:
                k_copies(j)
            if att:
                heads_copy(p, 1, bank_tb)
            if nxt:
                q_low_turned(j)
            if gla:
                rstd(2, "x2", p.n(1), norm_count(p, 1))
                two_blocks(x2n_t, bank_mb, "x2n_turned", p.n(1), "x2n_t_ready")
            if nxt:
                v_high(j)
            if gla:
                wait(act, S["logits_done"], p.n(1))
                copy(logits[:, g.n(1), :] if isinstance(g.n(1), int) else
                     logits[:, bass.ds(g.n(1), 1), :].rearrange("p a e -> p (a e)"), bank_mb[:, 0:NE],
                     S["logits_ready"])
            if att:
                rstd(1, "x1", p.n(1, 1), norm_count(p, 2))

        act.preload_act_table_set("natural_log_exp_and_others")
        act.wait_ge(S["consts_loaded"], 16)
        zero = Step(0, 0)
        rstd(0, "x", 1, 1)
        ctx_copies(zero)
        two_blocks(xn_t, bank_ta, "xn_turned", 1, "xn_t_ready")
        k_high(zero)
        k_copies(zero)
        v_high(zero)
        q_high(zero)
        q_low_turned(zero)

        def third(p):
            step(p)
            act.wait_ge(S["shared_loaded"], 64)
            act.wait_ge(S["slots_filled"], 16 * N_FILL)
            nc.scalar.activation(experts_h[:, 0, 0:EW], experts[:, 1, :], ACT.Copy, scale=W_SCALE)\
                .then_inc(S["shared_hi"], 1)

        over_pairs(act, lambda p: step(p, gla=False), step, lambda p: step(p, nxt=False), third)
        step(Step(0, NPAIR), nxt=False, att=False)

        act.wait_ge(S["route_step"], 1)
        nc.scalar.activation(r_e, r_z, ACT.Exp, scale=-1.0).then_inc(S["route_exp"], 1)

        def rows_copy(t, k):
            wait(act, S["up_done"], t * 2 - 2)
            wait(act, S["rows_turned"], t + 1)
            copy(e_rows_t[k].rearrange("p m n -> p (m n)"), ps[:, 0, :].bitcast(F16), S["rows_t_ready"])

        def silu(t, half):
            wait(act, S["gate_done"], t * 2 + half + 1)
            wait(act, S["hid_ready"], t * 2 + half)
            nc.scalar.activation(e_silu, ps_flat[:, 512 + half * HALF:512 + (half + 1) * HALF], ACT.Silu,
                                 scale=1 / W_SCALE).then_inc(S["silu_ready"], 1)

        def hidden_high(t, half):
            wait(act, S["hid_ready"], t * 2 + half + 1)
            wait(act, S["down_done"], t)
            c = slice(half * HT // 2, (half + 1) * HT // 2)
            copy(e_hid_s[0][:, c, :].rearrange("p c n -> p (c n)"), e_hid, S["hid_hi_ready"])

        def load_chunk(n):
            wait(act, S["chunk_lo_ready"], CHUNK_AFTER[n] + 1)
            e, c = n // NCHUNK, n % NCHUNK
            raw, done = w_raw[CHUNK_PLACE[n]], chunk_loaded[CHUNK_SEM[n]]
            if c < DK:
                act.dma_start(raw[:, 0:HID], rgate[e, c * P:(c + 1) * P, :]).then_inc(done, 16)
                act.dma_start(raw[:, HID:2 * HID], rup[e, c * P:(c + 1) * P, :]).then_inc(done, 16)
            else:
                k = HT // 2
                lo, hi = (c - DK) * k * P, min((c - DK + 1) * k * P, HID)
                full = (hi - lo) // P
                act.dma_start(raw[:, 0:full * D].rearrange("p (c n) -> p c n", n=D),
                              rdown[e, lo:lo + full * P, :].rearrange("(c p) n -> p c n", p=P)).then_inc(done, 16)
                if full < k:
                    act.dma_start(raw[0:HR, full * D:k * D], rdown[e, lo + full * P:hi, :]).then_inc(done, 16)

        def chunk_high(n):
            e, c = n // NCHUNK, n % NCHUNK
            loads = sum(1 if m % NCHUNK == DK else 2 for m in range(n + 1) if CHUNK_SEM[m] == CHUNK_SEM[n])
            act.wait_ge(chunk_loaded[CHUNK_SEM[n]], 16 * loads)
            if n % NCHUNK == 0 and e > 0:
                act.wait_ge(S["chunk_lo_ready"], n)
            if n == NCHUNK * (NE - 1):
                for k in range(4):
                    act.wait_ge(scattered[k], 32 * (NTILE // 4))
            lo, hi = CHUNKS[c]
            nc.scalar.activation(experts_h[:, 1 + e, lo:hi], w_raw[CHUNK_PLACE[n]][:, 0:hi - lo], ACT.Copy,
                                 scale=W_SCALE).then_inc(S["chunk_hi_ready"], 1)

        def chunks(t, part):
            for n in part_of(chunks_of(t), part):
                for m in range(5, NCHUNK * NE):
                    if max(m - 4, CHUNK_AFTER[m] + 1) == n:
                        load_chunk(m)
                chunk_high(n)

        def load_rows(t):
            act.dma_start(e_rows, tokens[t]).then_inc(S["rows_loaded"], 16)

        def tile(t, k, first=False):
            silu(t, 0)
            if first:
                chunks(t, 0)
            hidden_high(t, 0)
            rows_copy(t + 1, 1 - k)
            if first:
                if t + 2 < FIRST:
                    load_rows(t + 2)
                chunks(t, 1)
            silu(t, 1)
            hidden_high(t, 1)
            if first and t >= 1:
                act.wait_ge(S["y_ready"], t)
                act.dma_start(token_results[t - 1], e_y).then_inc(S["y_stored"], 16)

        rows_copy(0, 0)
        load_rows(1)
        act.wait_ge(S["cleared"], 2)
        for n in range(5):
            load_chunk(n)
        tile(0, 0, True)
        act.wait_ge(S["table_ready"], 1)
        for t in range(1, FIRST):
            tile(t, t % 2, True)
        with act.Fori(FIRST // 2, NT // 2 - 1) as i:
            tile(i * 2, 0)
            tile(i * 2 + 1, 1)
        tile(NT - 2, 0)
        for half in range(2):
            silu(NT - 1, half)
            hidden_high(NT - 1, half)

    @block.vector
    def _(dve):
        v = nc.vector

        def copy(dst, src, done):
            v.tensor_copy(dst, src).then_inc(done, 1)

        def norm_stats(k, src, which, n, m):
            v.bn_stats(stats[k][:, 0:6], src).then_inc(S["norm_sums"], 1)
            wait(dve, S["norm_sums"], m)
            apart(dve)
            v.bn_aggr(stats[k][:, 6:8], stats[k][:, 0:6]).then_inc(S[which + "_stat_ready"], 1)

        def norm_apply(k, dst, src, which, done, n):
            wait(dve, S[which + "_rstd_ready"], n)
            v.tensor_scalar(dst, src, stats[k][:, 6:7], stats[k][:, 9:10], ALU.subtract, ALU.mult)\
                .then_inc(S[done], 1)

        def x_stats(j, m):
            wait(dve, x_loaded[j.par], j.half * 16 + 16)
            norm_stats(0, x_in[j.par], "x", j.n(1, 1), m)

        def x_norm(j):
            wait(dve, S["xn_turned"], j.n(1))
            norm_apply(0, xn, x_in[j.par], "x", "xn_ready", j.n(1, 1))

        def max_rows(p, b):
            wait(dve, S["scores_done"], p.n(2, b + 1))
            wait(dve, S["exp_done"], p.n(16, 8 * b - 8))
            nm = neg_max[b].rearrange("p (g r) -> p g r", g=2)
            for r in range(4):
                v.tensor_reduce(nm[:, :, r], ps[:, r, :].rearrange("p (g j) -> p g j", g=2), AX.X, ALU.max,
                                negate=True).then_inc(S["max_ready"], 1)

        def kv_bias(j, t):
            wait(dve, S["kv_done"], j.n(4, t + 1))
            wait(dve, S["k_swap_ready"], j.n(1))
            wait(dve, S["k_prod_ready"], j.n(1))
            wait(dve, S["v_split"], j.n(1))
            bank = (bank_ma, bank_mb)[t % 2]
            v.tensor_tensor(kv[:, t, :], bank, b_kv, ALU.add).then_inc(S["kv_ready"], 1)

        def k_cos(j):
            wait(dve, S["kv_ready"], j.n(4, 4))
            wait(dve, S["k_turned"], j.n(2))
            cos = const("cosk").rearrange("p (t c) -> p t c", t=2)
            for b in range(2):
                ins = v.tensor_tensor(k_rot[:, 2 * b:2 * b + 2, :].rearrange("p t (h c) -> p t h c", h=H),
                                      kv[:, 2 * b:2 * b + 2, 0:D].rearrange("p t (h c) -> p t h c", h=H),
                                      bc(cos, 2, H), ALU.mult)
            ins.then_inc(S["k_prod_ready"], 1)

        def k_add(j):
            wait(dve, S["k_swap_ready"], j.n(1, 1))
            wait(dve, S["k_prod_ready"], j.n(1, 1))
            v.tensor_tensor(k_rot, k_rot, k_swap, ALU.add).then_inc(S["k_rot_ready"], 1)

        def q_bias(j):
            wait(dve, S["q_done"], j.n(1, 1))
            wait(dve, S["q_turned"], j.n(1))
            v.tensor_tensor(q_nat, bank_ta[:, 0:D], b_q, ALU.add).then_inc(S["q_nat_ready"], 1)
            wait(dve, S["q_nat_ready"], j.n(1, 1))
            wait(dve, S["q_turned"], j.n(1))
            v.tensor_tensor(q_rot.rearrange("p (h c) -> p h c", h=H), q_nat.rearrange("p (h c) -> p h c", h=H),
                            bc(const("cosq"), 1, H), ALU.mult).then_inc(S["q_prod_ready"], 1)

        def q_add(j):
            wait(dve, S["q_swap_ready"], j.n(1, 1))
            wait(dve, S["q_prod_ready"], j.n(1, 1))
            v.tensor_tensor(q_rot, q_rot, q_swap, ALU.add).then_inc(S["q_rot_ready"], 1)

        def q_low(j):
            wait(dve, S["q_hi_ready"], j.n(1, 1))
            v.tensor_tensor(q_s[:, 1], bc(q_rot.rearrange("p (h c) -> p h c", h=8), 2, 2), q_s[:, 0],
                            ALU.subtract).then_inc(S["q_split"], 1)

        def q_heads_split(j):
            wait(dve, S["q_turned"], j.n(1, 1))
            wait(dve, S["scores_done"], j.n(2))
            src = bank_ta.bitcast(F16)[:, 0:4 * P].rearrange("p (m b i) -> p m b i", m=4, b=2)
            for a in range(2):
                ins = v.tensor_scalar(q_t[0][:, :, :, a, :], src, const("par")[:, a:a + 1], None, ALU.mult)
            ins.then_inc(S["q_t_ready"], 1)

        def probs_low(p, b, lo=0, hi=4):
            for r in range(lo, hi):
                wait(dve, S["probs_hi_ready"], p.n(8, 4 * b + r + 1))
                v.tensor_tensor(probs_s[1][:, r, :], probs_bank(b, r), probs_s[0][:, r, :], ALU.subtract)\
                    .then_inc(S["probs_lo_ready"], 1)

        def normalise(p, b, bank):
            wait(dve, S["exp_done"], p.n(16, 8 * b + 8))
            v.reciprocal(row_inv, row_sum[b]).then_inc(S["inv_ready"], 1)
            wait(dve, S["inv_ready"], p.n(2, b + 1))
            wait(dve, S["av_done"], p.n(2, b + 1))
            wait(dve, S["heads_turned"], p.n(2, b - 1))
            for a in range(2):
                rows = slice(SQ * a, SQ * a + SQ)
                src = bank[rows, 0:D].rearrange("p (h a c) -> p h a c", h=8, a=2)[:, :, a, :]
                ins = v.tensor_tensor(heads_out[b][rows], src, bc(row_inv[rows, :], 2, HC), ALU.mult)
            ins.then_inc(S["av_ready"], 1)

        def add_x1(p):
            wait(dve, S["proj_done"], p.n(1, 1))
            wait(dve, S["x_res_ready"], p.n(1, 1))
            v.tensor_tensor(x1, bank_ma[:, 0:D], x_res, ALU.add).then_inc(S["x1_ready"], 1)
            wait(dve, S["x1_ready"], p.n(1, 1))
            norm_stats(1, x1, "x1", p.n(1, 1), norm_count(p, 2))
            norm_apply(1, x1n, x1, "x1", "x1n_ready", p.n(1, 1))

        def step(p, nxt=True, gla=True, att=True):
            g, j = p.next(-1), p.next()
            if not nxt:
                dve.sem_inc(S["norm_sums"], 1)
            n = p.n(1)
            if gla:
                wait(dve, S["x1n_hi_ready"], n)
                turned = bank_ta[:, 0:D].rearrange("p (k n) -> p k n", k=DK)
                v.tensor_tensor(x1n_s[1], turned, x1n_s[0], ALU.subtract)\
                    .then_inc(S["x1n_lo_ready"], 1)
            if nxt:
                x_stats(j, norm_count(p, 0))
            if att:
                max_rows(p, 0)
            if gla:
                wait(dve, S["vg_done"], n)
                v.tensor_scalar(g_v_s[0][:, 0, :], bank_tb[:, 0:D], V_SCALE / W_SCALE, None, ALU.mult)\
                    .then_inc(S["g_v_hi_ready"], 1)
                v.scalar_tensor_tensor(out=gate, in0=bank_tb[:, D:2 * D], scalar=1 / W_SCALE, in1=b_g, op0=ALU.mult,
                                       op1=ALU.add).then_inc(S["gate_ready"], 1)
                wait(dve, S["g_v_hi_ready"], n)
                v.scalar_tensor_tensor(out=g_v_s[1][:, 0, :], in0=bank_tb[:, 0:D], scalar=V_SCALE / W_SCALE,
                                       in1=g_v_s[0][:, 0, :], op0=ALU.mult, op1=ALU.subtract)\
                    .then_inc(S["g_v_ready"], 1)
            if nxt:
                x_norm(j)
                kv_bias(j, 0)
            if gla:
                wait(dve, S["kg_done"], n)
                v.tensor_scalar(kg_min, bank_tb[:, 0:P], 0.0, None, ALU.min).then_inc(S["kg_min_ready"], 1)
                wait(dve, S["kg_min_ready"], n)
                v.scalar_tensor_tensor(out=kg_abs, in0=kg_min, scalar=-2.0, in1=bank_tb[:, 0:P], op0=ALU.mult,
                                       op1=ALU.add).then_inc(S["kg_abs_ready"], 1)
            if nxt:
                kv_bias(j, 1)
            if gla:
                wait(dve, S["kg_step"], g.n(2, 2))
                wait(dve, S["kg_min_ready"], n)
                v.tensor_tensor(log_gate, kg_min, kg_ln, ALU.subtract).then_inc(S["decay_step"], 1)
                wait(dve, S["decay_step"], g.n(3, 1))
                for b in range(2):
                    ins = v.tensor_tensor_scan(cum[:, b, :], log_gate[:, b * SQ:(b + 1) * SQ],
                                               log_gate[:, b * SQ:(b + 1) * SQ], 0.0, ALU.add, ALU.bypass)
                ins.then_inc(S["decay_step"], 1)
                if nxt:
                    kv_bias(j, 2)
                wait(dve, S["decay_step"], g.n(3, 2))
                copy(ref[:, :, 1:NCH], cum.rearrange("p b (c t) -> p b c t", t=CH)[:, :, 0:NCH - 1, CH - 1],
                     S["decay_step"])
                wait(dve, S["decay_step"], g.n(3, 3))
                v.tensor_tensor(q_dec.rearrange("p (b c t) -> p b c t", b=2, c=NCH),
                                cum.rearrange("p b (c t) -> p b c t", t=CH), bc(ref, 3, CH), ALU.subtract)\
                    .then_inc(S["dec_ready"], 1)
                v.tensor_tensor(k_dec, bc(ref.rearrange("p b c -> p c b"), 3, SQ), bc(cum, 1, NCH), ALU.subtract)\
                    .then_inc(S["dec_k_step"], 1)
                wait(dve, S["dec_k_step"], g.n(2, 1))
                kd = k_dec.rearrange("p c b i -> p (c b i)")
                v.tensor_scalar(kd, kd, BOUND * GATE_NORM, None, ALU.min).then_inc(S["dec_k_step"], 1)
            if nxt:
                if not gla:
                    kv_bias(j, 2)
                kv_bias(j, 3)
            if gla:
                wait(dve, S["dec_exp_q"], n)
                v.tensor_tensor(qs_t, bank_ta[:, 0:P], q_dec, ALU.mult).then_inc(S["qs_ready"], 1)
                wait(dve, S["dec_exp_k"], n)
                v.tensor_tensor(k_heads, bc(bank_ta[:, P:2 * P].rearrange("p (b i) -> p b i", b=2), 1, NCH), k_dec,
                                ALU.mult).then_inc(S["k_heads_ready"], 1)
                wait(dve, S["qs_ready"], n)
                v.tensor_tensor(q_heads.rearrange("p b c h t -> p (b c) h t"),
                                bc(qs_t.rearrange("p (m t) -> p m t", t=CH), 2, 4),
                                bc(bc(const("head4"), 1, 2 * NCH), 3, CH), ALU.mult).then_inc(S["q_heads_ready"], 1)
            if att:
                probs_low(p, 0)
            if nxt:
                k_cos(j)
            if gla:
                wait(dve, S["a_done"], n)
                for r in range(4):
                    v.tensor_tensor(a_t[:, r].rearrange("p h c t -> p c h t"), ps[:, r, 0:256].rearrange("p (c h t) -> p c h t", c=NCH, h=4),
                                    bc(const("gla").rearrange("p (c t) -> p c t", c=NCH), 2, 4), ALU.mult)\
                        .then_inc(S["a_ready"], 1)
            if nxt:
                k_add(j)
            if att:
                normalise(p, 0, bank_mb)
            if gla:
                wait(dve, S["gate_inv"], n)
                v.tensor_tensor(gate_i, gate, gate_i, ALU.mult).then_inc(S["gate_silu"], 1)
            if att:
                max_rows(p, 1)
            if nxt:
                q_bias(j)
            if gla:
                wait(dve, S["go_ready"], n)
                heads = g_out.rearrange("p (h c) -> p h c", h=H)
                sq = g_sq.rearrange("p (h c) -> p h c", h=H)
                gn = g_norm.rearrange("p (h c) -> p h c", h=H)
                v.tensor_reduce(g_stat[:, 0, :], heads, AX.X, ALU.add).then_inc(S["gs_step"], 1)
                wait(dve, S["gs_step"], g.n(4, 1))
                v.tensor_scalar(g_stat[:, 0, :], g_stat[:, 0, :], 1.0 / GV, None, ALU.mult).then_inc(S["gs_step"], 1)
                wait(dve, S["gs_step"], g.n(4, 2))
                v.tensor_tensor(heads, heads, bc(g_stat[:, 0, :], 2, GV), ALU.subtract).then_inc(S["gs_step"], 1)
                wait(dve, S["gs_step"], g.n(4, 3))
                v.tensor_tensor(sq, heads, heads, ALU.mult).then_inc(S["gs_step"], 1)
                wait(dve, S["gs_step"], g.n(4, 4))
                v.tensor_reduce(g_stat[:, 1, :], sq, AX.X, ALU.add).then_inc(S["gs_var"], 1)
                wait(dve, S["gate_silu"], n)
                wait(dve, S["gs_var"], n)
                v.tensor_tensor(g_sq, g_out, gate_i, ALU.mult).then_inc(S["gn_step"], 1)
                wait(dve, S["gn_step"], g.n(2, 1))
            if nxt:
                q_add(j)
            if gla:
                wait(dve, S["gs_rstd"], n)
                v.tensor_tensor(gn, sq, bc(g_stat[:, 3, :], 2, GV), ALU.mult).then_inc(S["gn_step"], 1)
            if att:
                probs_low(p, 1)
            if nxt:
                q_low(j)
            if att:
                normalise(p, 1, bank_ma)
            if nxt:
                q_heads_split(j)
            if gla:
                wait(dve, S["gproj_done"], n)
                gt = g.n(1)
                x2 = x2_all[:, gt, :] if isinstance(gt, int) else \
                    x2_all[:, bass.ds(gt, 1), :].rearrange("p a d -> p (a d)")
                v.tensor_tensor(x2, bank_mb[:, 0:D], x1, ALU.add).then_inc(S["x2_ready"], 1)
                wait(dve, S["x2_ready"], n)
                apart(dve)
                norm_stats(2, x2, "x2", n, norm_count(p, 1))
                wait(dve, S["x2n_split"], g.n(2, -2))
                norm_apply(2, x2n[g.par], x2, "x2", "x2n_ready", n)
            if att:
                add_x1(p)

        dve.wait_ge(S["consts_loaded"], 16)
        dve.wait_ge(S["weights_loaded"], 16 * WEIGHT_DMAS)
        v.memset(ref[:, :, 0:1], 0.0).then_inc(S["cleared"], 1)
        dve.wait_ge(S["cleared"], 1)
        zero = Step(0, 0)
        x_stats(zero, 1)
        x_norm(zero)
        for t in range(4):
            kv_bias(zero, t)
        k_cos(zero)
        k_add(zero)
        q_bias(zero)
        q_add(zero)
        q_low(zero)
        q_heads_split(zero)
        for k, (w, (high, low)) in enumerate(((w_gqk, w_gqk_s), (w_g1, w_g1_s), (w_gvg, w_gvg_s))):
            v.tensor_scalar(high, w, W_SCALE, None, ALU.mult).then_inc(S["gla_hi_ready"], 1)
            dve.wait_ge(S["gla_hi_ready"], k + 1)
            v.scalar_tensor_tensor(out=low, in0=w, scalar=W_SCALE, in1=high, op0=ALU.mult, op1=ALU.subtract)\
                .then_inc(S["gla_lo_ready"], 1)

        def third(p):
            step(p)
            dve.wait_ge(S["shared_hi"], 1)
            v.scalar_tensor_tensor(out=experts_h[:, 0, EW:], in0=experts[:, 1, :], scalar=W_SCALE,
                                   in1=experts_h[:, 0, 0:EW], op0=ALU.mult, op1=ALU.subtract)\
                .then_inc(S["shared_lo"], 1)

        over_pairs(dve, lambda p: step(p, gla=False), step, lambda p: step(p, nxt=False), third)
        step(Step(0, NPAIR), nxt=False, att=False)

        def hidden(t, half):
            wait(dve, S["up_done"], t * 2 + half + 1)
            wait(dve, S["silu_ready"], t * 2 + half + 1)
            wait(dve, S["hid_lo_ready"], t * 2 + half)
            v.scalar_tensor_tensor(out=e_hid, in0=ps_flat[:, 2048 + half * HALF:2048 + (half + 1) * HALF],
                                   scalar=1 / W_SCALE, in1=e_silu, op0=ALU.mult, op1=ALU.mult)\
                .then_inc(S["hid_ready"], 1)

        def hidden_low(t, half):
            wait(dve, S["hid_hi_ready"], t * 2 + half + 1)
            c = slice(half * HT // 2, (half + 1) * HT // 2)
            high, low = (h[:, c, :].rearrange("p c n -> p (c n)") for h in e_hid_s)
            v.tensor_tensor(low, e_hid, high, ALU.subtract).then_inc(S["hid_lo_ready"], 1)

        count = [0]

        def link(ins):
            ins.then_inc(S["route_step"], 1)
            count[0] += 1
            dve.wait_ge(S["route_step"], count[0])

        dve.wait_ge(S["logits_ready"], NPAIR)
        dve.wait_ge(x2n_stored[0], 16 * NPAIR // 2)
        dve.wait_ge(x2n_stored[1], 16 * NPAIR // 2)
        for raw in w_raw[0:5]:
            ins = v.memset(raw[:, (HT - 1) * D - HT * D // 2:HT * D // 2], 0.0)
        ins.then_inc(S["cleared"], 1)
        v.tensor_copy(ident_h, ident).then_inc(S["cleared"], 1)
        dve.wait_ge(S["consts_loaded"], 32)
        link(v.tensor_tensor(r_z, logits[:, :, :], bc(r_bias, 1, NTILE), ALU.mult))
        dve.wait_ge(S["route_exp"], 1)
        link(v.tensor_scalar(r_c, r_e, 1.0, None, ALU.add))
        link(v.reciprocal(r_p, r_c))
        desc = bc(const("desc"), 1, NTILE)
        for c in range(TOPK):
            link(v.tensor_reduce(r_m[:, c, :], r_p, AX.X, ALU.max))
            link(v.tensor_tensor(r_eq, r_p, bc(r_m[:, c, :], 2, NE), ALU.is_equal))
            link(v.tensor_tensor(r_c, r_eq, desc, ALU.mult))
            link(v.tensor_reduce(r_m[:, 2, :], r_c, AX.X, ALU.max))
            link(v.tensor_tensor(r_oh[c], r_c, bc(r_m[:, 2, :], 2, NE), ALU.is_equal))
            if c == 0:
                link(v.scalar_tensor_tensor(out=r_p, in0=r_oh[0], scalar=-4.0, in1=r_p, op0=ALU.mult, op1=ALU.add))
        link(v.memset(r_ones, 1.0))
        link(v.tensor_tensor(r_sel, r_oh[0], r_oh[1], ALU.add))
        assert count[0] == ROUTE_SELECTED
        hidden(0, 0)
        hidden_low(0, 0)
        link(v.tensor_tensor(r_m[:, 3, :], r_m[:, 0, :], r_m[:, 1, :], ALU.add))
        link(v.reciprocal(r_m[:, 4, :], r_m[:, 3, :]))
        for c in range(TOPK):
            link(v.tensor_tensor(w_tok[:, c, :], r_m[:, c, :], r_m[:, 4, :], ALU.mult))
        dve.wait_ge(S["route_mm"], 2)
        link(v.tensor_copy(r_in.rearrange("p t e -> p (t e)"), bank_mb[:, L:2 * L]))
        link(v.tensor_copy(r_tot.rearrange("p t e -> p (t e)"), bank_mb[:, 0:L]))
        for e in range(NE):
            link(v.tensor_tensor_scan(r_cum[:, :, e], r_tot[:, :, e], r_tot[:, :, e], 0.0, ALU.add, ALU.bypass))
        hidden(0, 1)
        hidden_low(0, 1)
        link(v.tensor_scalar(r_ni, r_cum[:, NTILE - 1, :], float(R - 1), None, ALU.add))
        link(v.tensor_scalar(r_ni, r_ni, R.bit_length() - 1, None, ALU.arith_shift_right))
        link(v.tensor_copy(r_n[:, 0, :], r_ni))
        link(v.tensor_tensor_scan(r_n[:, 1, :], r_n[:, 0, :], r_n[:, 0, :], 0.0, ALU.add, ALU.bypass))
        link(v.tensor_tensor(r_n[:, 2, :], r_n[:, 1, :], r_n[:, 0, :], ALU.subtract))
        link(v.tensor_scalar(r_n[:, 3, :], r_n[:, 2, :], float(R), None, ALU.mult))
        link(v.tensor_tensor(r_pos, r_cum, r_tot, ALU.subtract))
        link(v.tensor_tensor(r_pos, r_pos, r_in, ALU.add))
        link(v.tensor_tensor(r_pos, r_pos, bc(r_n[:, 3, :], 1, NTILE), ALU.add))
        for c in range(TOPK):
            link(v.tensor_tensor(r_c, r_oh[c], r_pos, ALU.mult))
            link(v.tensor_reduce(r_m[:, 5, :], r_c, AX.X, ALU.add))
            link(v.tensor_copy(slot_i[:, c, :], r_m[:, 5, :]))
        link(v.tensor_tensor(r_t, bc(const("tile"), 2, NE), bc(r_n[:, 1, :], 1, NSLOT), ALU.is_ge))
        link(v.tensor_reduce(r_tf, r_t, AX.X, ALU.add))
        link(v.tensor_scalar(r_tf, r_tf, 1.0, float(NE), ALU.add, ALU.min))
        link(v.memset(tile_e, 0))
        link(v.tensor_copy(tile_e[:, FIRST:MID], r_tf))
        assert count[0] == ROUTE_DONE
        v.memset(r_ones[:, 0:1], 1.0).then_inc(S["table_ready"], 1)

        def result(t):
            wait(dve, S["down_done"], t + 1)
            wait(dve, S["y_stored"], t * 16)
            v.tensor_scalar(e_y.rearrange("p a d -> p (a d)"), ps[:, 7, :], 1 / W_SCALE, None, ALU.mult)\
                .then_inc(S["y_ready"], 1)

        def chunk_low(n):
            dve.wait_ge(S["chunk_hi_ready"], n + 1)
            e, c = n // NCHUNK, n % NCHUNK
            lo, hi = CHUNKS[c]
            w = experts_h[:, 1 + e, :]
            v.scalar_tensor_tensor(out=w[:, EW + lo:EW + hi], in0=w_raw[CHUNK_PLACE[n]][:, 0:hi - lo], scalar=W_SCALE,
                                   in1=w[:, lo:hi], op0=ALU.mult, op1=ALU.subtract)\
                .then_inc(S["chunk_lo_ready"], 1)

        def chunks(t, part):
            for n in part_of(chunks_of(t), part):
                chunk_low(n)

        def tile(t, split=False):
            hidden(t, 0)
            if split:
                chunks(t, 0)
            result(t - 1)
            hidden_low(t, 0)
            if split:
                chunks(t, 1)
            hidden(t, 1)
            hidden_low(t, 1)

        for t in range(1, FIRST):
            tile(t, True)
        with dve.Fori(FIRST, MID) as t:
            tile(t)

        def combine(m):
            dve.wait_ge(S["first_shared_loaded" if (m + 1) * GROUP <= 2 * FIRST else "last_shared_loaded"], 16)
            dve.wait_ge(group_loaded[m], 16 * TOPK * GROUP)
            tiles = slice(m * GROUP, (m + 1) * GROUP)
            v.tensor_tensor(x2_all[:, tiles, :], x2_all[:, tiles, :], results[:, 2, tiles, :], ALU.add)\
                .then_inc(S["sum_step"], 1)
            for c in range(TOPK):
                dve.wait_ge(S["sum_step"], (1 + TOPK) * m + c + 1)
                for t in range(m * GROUP, (m + 1) * GROUP):
                    x2 = x2_all[:, t, :]
                    ins = v.scalar_tensor_tensor(out=x2, in0=results[:, c, t, :], scalar=w_tok[:, c, t:t + 1], in1=x2,
                                                 op0=ALU.mult, op1=ALU.add)
                ins.then_inc(S["sum_step"], 1)

        done = 0
        for t in range(MID, NT):
            tile(t)
            while done < (t - MID - 1) * 3 // 2 and (done + 1) * GROUP <= 2 * FIRST and t >= MID + 2:
                combine(done)
                done += 1
        result(NT - 1)
        for m in range(done, NTILE // GROUP):
            combine(m)


WEIGHT_DMAS = 3 + 16 + 8 + 5
N_FILL = -(-2 * NSLOT // 8)
SPLIT_TILES = FIRST - 1


def part_of(chunks, part):
    return chunks[2:] if part else chunks[:2]


def chunks_of(t):
    if t < 1:
        return range(0)
    n = NCHUNK * NE
    return range(n * (t - 1) // SPLIT_TILES, n * t // SPLIT_TILES)



BOUND = 60.0
ROUTE_SELECTED = 3 + 5 * TOPK + 1 + 2
ROUTE_DONE = ROUTE_SELECTED + 4 + 2 + NE + 6 + 3 + 3 * TOPK + 5


_SPARE = NCHUNK * (NE - 2)
CHUNK_PLACE = [n % 5 if n < _SPARE else (0, 1, 5, 6, 0, 1, 0, 1)[n - _SPARE] for n in range(NCHUNK * NE)]
CHUNK_SEM = [k if k < 5 else k - 3 for k in CHUNK_PLACE]
CHUNK_AFTER = [max([m for m in range(n) if CHUNK_SEM[m] == CHUNK_SEM[n]], default=-1) for n in range(NCHUNK * NE)]


_INS = ["x", "ctx_1024", "mask_BxS2_bf0", "L0_xattn_Wq", "L0_xattn_bq", "L0_xattn_Wk", "L0_xattn_bk", "L0_xattn_Wv",
        "L0_xattn_bv", "L0_xattn_Wo", "L0_xattn_bo", "L0_attn_Wq", "L0_attn_Wk", "L0_attn_Wg1", "L0_attn_Wg2",
        "L0_attn_Wv", "L0_attn_Wg", "L0_attn_bg", "L0_attn_Wo", "L0_ffn_shared_gate", "L0_ffn_shared_up",
        "L0_ffn_shared_down", "L0_ffn_routed_gate", "L0_ffn_routed_up", "L0_ffn_routed_down", "L0_ffn_Wr",
        "L0_ffn_routing_bias"]


def kernel(**inputs):
    import concourse.bacc as bacc
    from concourse.bass_utils import run_bass_kernel_spmd

    nc = bacc.Bacc("TRN2", target_bir_lowering=False, num_devices=1)
    arrays, args = {}, []
    for name in _INS:
        a = np.ascontiguousarray(inputs[name])
        arrays["in_" + name] = a
        args.append(nc.dram_tensor("in_" + name, a.shape, mybir.dt.from_np(a.dtype), kind="ExternalInput").ap())
    arrays["constants"] = constants()
    args.append(nc.dram_tensor("constants", [P, NCONST], F32, kind="ExternalInput").ap())
    args.append(nc.dram_tensor("out", [NB, SQ, D], F32, kind="ExternalOutput").ap())
    build(nc, *args)
    result = run_bass_kernel_spmd(nc, [arrays], core_ids=[0])
    return result.results[0]["out"]
```
